# Optimizing a Trainium2 kernel written in Bass

```python
import numpy as np
import jax
import jax.numpy as jnp

def _softmax(x, axis=-1):
    return jax.nn.softmax(x, axis=axis)

def _gelu(x):
    return jax.nn.gelu(x, approximate=True)

def _silu(x):
    return jax.nn.silu(x)

def _sigmoid(x):
    return jax.nn.sigmoid(x)

def _layernorm(x, axis=-1, eps=1e-05):
    m = jnp.mean(x, axis=axis, keepdims=True)
    v = jnp.var(x, axis=axis, keepdims=True)
    return (x - m) / jnp.sqrt(v + eps)

def _scatter_add(tgt, idx, src, axis=0):
    return tgt.at[idx].add(src)

def _segment_sum(src, seg, n):
    return jax.ops.segment_sum(src, seg, n)
kernel_name = 'mk_gnn_resnorm_d2_gnn_r32_4d9de2'

def setup_inputs(seed: int=0):
    np.random.seed(seed)
    _w = jnp.asarray

    def _rec_inputs():
        import jax
        import jax.numpy as jnp
        _gk = jax.random.key(seed)
        x = -0.0006008 + 1.001 * jax.random.normal(jax.random.fold_in(_gk, 1), (3125, 256), jnp.float32)
        src = jax.random.randint(jax.random.fold_in(_gk, 2), (50000,), 0, 3125, jnp.int32)
        dst = jnp.minimum((3125 * jax.random.uniform(jax.random.fold_in(_gk, 3), (50000,)) ** 2.0).astype(jnp.int32), 99999)
        _o = jnp.argsort(dst, stable=True)
        src = src[_o]
        dst = dst[_o]
        edge_attr_4 = 0.000126197 + 0.999763 * jax.random.normal(jax.random.fold_in(_gk, 11), (50000, 4), jnp.float32)
        edge_attr_64 = 0.000312547 + 1.00004 * jax.random.normal(jax.random.fold_in(_gk, 12), (50000, 64), jnp.float32)
        return (x, src, dst, edge_attr_4, edge_attr_64)
    x, src, dst, edge_attr_4, edge_attr_64 = _rec_inputs()

    def _L0_gnn_setup():
        import jax, jax.numpy as jnp
        import numpy as np
        N, E, H, DE = (10000, 250000, 256, 64)
        EPS = 1e-05

        def _lin_init(k, fan_in, shape):
            s = 1.0 / np.sqrt(fan_in)
            return jax.random.uniform(k, shape, jnp.float32, -s, s)
        key = jax.random.key(seed)
        ks = jax.random.split(key, 12)
        x = jax.random.normal(ks[0], (N, H), jnp.float32)
        edge_index = jax.random.randint(ks[1], (2, E), 0, N)
        edge_attr = jax.random.normal(ks[2], (E, DE), jnp.float32)
        d_in = H + DE
        W1 = _lin_init(ks[3], d_in, (d_in, H))
        b1 = _lin_init(ks[4], d_in, (H,))
        W2 = _lin_init(ks[5], H, (H, H))
        b2 = _lin_init(ks[6], H, (H,))
        Wg = _lin_init(ks[7], d_in, (d_in, H))
        bg = _lin_init(ks[8], d_in, (H,))
        gamma = jnp.ones((H,), jnp.float32)
        beta = jnp.zeros((H,), jnp.float32)
        return {'x': x, 'edge_index': edge_index, 'edge_attr': edge_attr, 'W1': W1, 'b1': b1, 'W2': W2, 'b2': b2, 'Wg': Wg, 'bg': bg, 'gamma': gamma, 'beta': beta}
    _L0_gnn_all = _L0_gnn_setup()
    _L0_gnn_in = {k: v for k, v in _L0_gnn_all.items() if k in ('W1', 'b1', 'W2', 'b2', 'Wg', 'bg', 'gamma', 'beta')}
    del _L0_gnn_all

    def _L1_gnn_setup():
        import jax, jax.numpy as jnp
        import numpy as np
        NEG_SLOPE = 0.2
        LN_EPS = 1e-05

        def _layernorm(x, gamma, beta):
            mu = x.mean(-1, keepdims=True)
            var = x.var(-1, keepdims=True)
            return (x - mu) * jax.lax.rsqrt(var + LN_EPS) * gamma + beta

        def _gatv2_conv(x, src, dst, eattr, Wl, Wr, We, att, bias, concat):
            N = x.shape[0]
            H, C = att.shape
            xl = (x @ Wl).reshape(N, H, C)
            xr = (x @ Wr).reshape(N, H, C)
            e = (eattr @ We).reshape(-1, H, C)
            m = xl[src] + xr[dst] + e
            score = jnp.sum(jax.nn.leaky_relu(m, NEG_SLOPE) * att, -1)
            smax = jax.ops.segment_max(score, dst, num_segments=N)
            ex = jnp.exp(score - smax[dst])
            denom = jax.ops.segment_sum(ex, dst, num_segments=N)
            alpha = ex / (denom[dst] + 1e-16)
            out = jax.ops.segment_sum(alpha[:, :, None] * xl[src], dst, num_segments=N)
            out = out.reshape(N, H * C) if concat else out.mean(axis=1)
            return out + bias
        key = jax.random.key(seed)
        ks = jax.random.split(key, 20)
        N, E = (10000, 10000)
        D, HID, HEADS, ED = (256, 128, 4, 4)
        HC = HID * HEADS

        def w(k, fi, fo):
            return jax.random.normal(k, (fi, fo), jnp.float32) / np.sqrt(fi)
        x = jax.random.normal(ks[0], (N, D), jnp.float32)
        edge_index = jax.random.randint(ks[1], (2, E), 0, N, jnp.int64)
        edge_attr = jax.random.normal(ks[2], (E, ED), jnp.float32)
        return {'x': x, 'edge_index': edge_index, 'edge_attr': edge_attr, 'Wl1': w(ks[3], D, HC), 'Wr1': w(ks[4], D, HC), 'We1': w(ks[5], ED, HC), 'att1': jax.random.normal(ks[6], (HEADS, HID), jnp.float32) / np.sqrt(HID), 'b1': jnp.zeros((HC,), jnp.float32), 'g1': jnp.ones((HC,), jnp.float32), 'be1': jnp.zeros((HC,), jnp.float32), 'Wl2': w(ks[7], HC, D), 'Wr2': w(ks[8], HC, D), 'We2': w(ks[9], ED, D), 'att2': jax.random.normal(ks[10], (1, D), jnp.float32) / np.sqrt(D), 'b2': jnp.zeros((D,), jnp.float32), 'g2': jnp.ones((D,), jnp.float32), 'be2': jnp.zeros((D,), jnp.float32)}
    _L1_gnn_all = _L1_gnn_setup()
    _L1_gnn_in = {k: v for k, v in _L1_gnn_all.items() if k in ('Wl1', 'Wr1', 'We1', 'att1', 'b1', 'g1', 'be1', 'Wl2', 'Wr2', 'We2', 'att2', 'b2', 'g2', 'be2')}
    del _L1_gnn_all
    return {'x': x, 'src': src, 'dst': dst, 'edge_attr_4': edge_attr_4, 'edge_attr_64': edge_attr_64, 'L0_gnn_W1': _L0_gnn_in['W1'], 'L0_gnn_b1': _L0_gnn_in['b1'], 'L0_gnn_W2': _L0_gnn_in['W2'], 'L0_gnn_b2': _L0_gnn_in['b2'], 'L0_gnn_Wg': _L0_gnn_in['Wg'], 'L0_gnn_bg': _L0_gnn_in['bg'], 'L0_gnn_gamma': _L0_gnn_in['gamma'], 'L0_gnn_beta': _L0_gnn_in['beta'], 'L1_gnn_Wl1': _L1_gnn_in['Wl1'], 'L1_gnn_Wr1': _L1_gnn_in['Wr1'], 'L1_gnn_We1': _L1_gnn_in['We1'], 'L1_gnn_att1': _L1_gnn_in['att1'], 'L1_gnn_b1': _L1_gnn_in['b1'], 'L1_gnn_g1': _L1_gnn_in['g1'], 'L1_gnn_be1': _L1_gnn_in['be1'], 'L1_gnn_Wl2': _L1_gnn_in['Wl2'], 'L1_gnn_Wr2': _L1_gnn_in['Wr2'], 'L1_gnn_We2': _L1_gnn_in['We2'], 'L1_gnn_att2': _L1_gnn_in['att2'], 'L1_gnn_b2': _L1_gnn_in['b2'], 'L1_gnn_g2': _L1_gnn_in['g2'], 'L1_gnn_be2': _L1_gnn_in['be2']}

def reference(x, src, dst, edge_attr_4, edge_attr_64, L0_gnn_W1, L0_gnn_b1, L0_gnn_W2, L0_gnn_b2, L0_gnn_Wg, L0_gnn_bg, L0_gnn_gamma, L0_gnn_beta, L1_gnn_Wl1, L1_gnn_Wr1, L1_gnn_We1, L1_gnn_att1, L1_gnn_b1, L1_gnn_g1, L1_gnn_be1, L1_gnn_Wl2, L1_gnn_Wr2, L1_gnn_We2, L1_gnn_att2, L1_gnn_b2, L1_gnn_g2, L1_gnn_be2):
    import jax
    import jax.numpy as jnp

    def _L0_gnn_ref(x, edge_index, edge_attr, W1, b1, W2, b2, Wg, bg, gamma, beta):
        import jax, jax.numpy as jnp
        import numpy as np
        N, E, H, DE = (10000, 250000, 256, 64)
        EPS = 1e-05

        def _lin_init(k, fan_in, shape):
            s = 1.0 / np.sqrt(fan_in)
            return jax.random.uniform(k, shape, jnp.float32, -s, s)
        src, dst = (edge_index[0], edge_index[1])
        ei = jnp.concatenate([x[src], edge_attr], axis=-1)
        core = jnp.maximum(ei @ W1 + b1, 0.0) @ W2 + b2
        gate = jax.nn.sigmoid(ei @ Wg + bg)
        msg = gate * core
        agg = jax.ops.segment_sum(msg, dst, num_segments=x.shape[0])
        out = agg + x
        mu = jnp.mean(out, axis=-1, keepdims=True)
        var = jnp.var(out, axis=-1, keepdims=True)
        out = (out - mu) * jax.lax.rsqrt(var + EPS) * gamma + beta
        return out

    def _L1_gnn_ref(x, edge_index, edge_attr, Wl1, Wr1, We1, att1, b1, g1, be1, Wl2, Wr2, We2, att2, b2, g2, be2):
        import jax, jax.numpy as jnp
        import numpy as np
        NEG_SLOPE = 0.2
        LN_EPS = 1e-05

        def _layernorm(x, gamma, beta):
            mu = x.mean(-1, keepdims=True)
            var = x.var(-1, keepdims=True)
            return (x - mu) * jax.lax.rsqrt(var + LN_EPS) * gamma + beta

        def _gatv2_conv(x, src, dst, eattr, Wl, Wr, We, att, bias, concat):
            N = x.shape[0]
            H, C = att.shape
            xl = (x @ Wl).reshape(N, H, C)
            xr = (x @ Wr).reshape(N, H, C)
            e = (eattr @ We).reshape(-1, H, C)
            m = xl[src] + xr[dst] + e
            score = jnp.sum(jax.nn.leaky_relu(m, NEG_SLOPE) * att, -1)
            smax = jax.ops.segment_max(score, dst, num_segments=N)
            ex = jnp.exp(score - smax[dst])
            denom = jax.ops.segment_sum(ex, dst, num_segments=N)
            alpha = ex / (denom[dst] + 1e-16)
            out = jax.ops.segment_sum(alpha[:, :, None] * xl[src], dst, num_segments=N)
            out = out.reshape(N, H * C) if concat else out.mean(axis=1)
            return out + bias
        N = x.shape[0]
        loop = jnp.arange(N, dtype=edge_index.dtype)
        src = jnp.concatenate([edge_index[0], loop])
        dst = jnp.concatenate([edge_index[1], loop])
        ea = jnp.concatenate([edge_attr, jnp.broadcast_to(edge_attr.mean(0), (N, edge_attr.shape[1]))])
        h = _gatv2_conv(x, src, dst, ea, Wl1, Wr1, We1, att1, b1, concat=True)
        h = _layernorm(h, g1, be1)
        h = jax.nn.elu(h)
        h = _gatv2_conv(h, src, dst, ea, Wl2, Wr2, We2, att2, b2, concat=False)
        h = _layernorm(h, g2, be2)
        return h + x
    edge_index = jnp.stack([src, dst])
    x = _layernorm(x + _L0_gnn_ref(x, edge_index, edge_attr_64, L0_gnn_W1, L0_gnn_b1, L0_gnn_W2, L0_gnn_b2, L0_gnn_Wg, L0_gnn_bg, L0_gnn_gamma, L0_gnn_beta), axis=-1)
    x = _layernorm(x + _L1_gnn_ref(x, edge_index, edge_attr_4, L1_gnn_Wl1, L1_gnn_Wr1, L1_gnn_We1, L1_gnn_att1, L1_gnn_b1, L1_gnn_g1, L1_gnn_be1, L1_gnn_Wl2, L1_gnn_Wr2, L1_gnn_We2, L1_gnn_att2, L1_gnn_b2, L1_gnn_g2, L1_gnn_be2), axis=-1)
    return x

_drawn_inputs = setup_inputs


def setup_inputs(seed=0):
    import zlib

    import numpy as np

    out = dict(_drawn_inputs(seed))
    spreads = {'L0_gnn_gamma': (1.0, 0.2),
     'L0_gnn_beta': (0.0, 0.1),
     'L1_gnn_b1': (0.0, 0.1),
     'L1_gnn_g1': (1.0, 0.2),
     'L1_gnn_be1': (0.0, 0.1),
     'L1_gnn_b2': (0.0, 0.1),
     'L1_gnn_g2': (1.0, 0.2),
     'L1_gnn_be2': (0.0, 0.1)}
    factors = {'L0_gnn_bg': 7.481}
    for name, (base, spread) in spreads.items():
        noise = np.random.default_rng([zlib.crc32(name.encode()), seed]).standard_normal(out[name].shape)
        drawn = base * np.exp(spread * noise) if base else spread * noise
        out[name] = jnp.asarray(drawn.astype(out[name].dtype))
    for name, factor in factors.items():
        out[name] = (out[name] * factor).astype(out[name].dtype)
    return out
```

```python
from contextlib import ExitStack

import numpy as np

import concourse.bass as bass
from concourse import mybir
from concourse.alu_op_type import AluOpType as ALU

ACT = mybir.ActivationFunctionType
AX = mybir.AxisListType
F32 = mybir.dt.float32
BF16 = mybir.dt.bfloat16
I32 = mybir.dt.int32

P = 128
N, E, D = 3125, 50000, 256
DE, ED = 64, 4
HEADS, HID = 4, 128
NT = 26
NP = NT * P
U = 8
BASE = -(-E // P) + -(-N // P) - 1
STEPS = -(-BASE // U) * U
SW = -(-STEPS // P)
ST = SW * P
RMAX = -(-E // P) * P
DC = RMAX // P + 2
EP = DC * P
IRING = 4
BIG = 1e30
PARTS = 3
EROWS = PARTS * PARTS * ED
SLOPE = 0.2
EPS = 1e-5


class Step:

    def __init__(self, it, k, unroll, count):
        self.it, self.k, self.unroll, self.count = it, k, unroll, count

    def back(self, n):
        return Step(self.it, self.k - n, self.unroll, self.count)

    @property
    def live(self):
        return not isinstance(self.it, int) or 0 <= self.it * self.unroll + self.k < self.count

    @property
    def s(self):
        return self.it * self.unroll + self.k

    @property
    def done(self):
        return self.it * self.unroll + (self.k + 1)

    def slot(self, ring):
        return self.k % ring

    def turns(self, ring):
        return self.it * (self.unroll // ring) + (self.k // ring + 1)

    def turns_of(self, group, ring):
        return self.it * (self.unroll // (group * ring)) + (self.k // (group * ring) + 1)


def run_steps(eng, body, unroll, count, lag, head=None):
    turns = count // unroll
    if head:
        head(0)
    for k in range(unroll):
        body(Step(0, k, unroll, count))
    with eng.Fori(1, turns) as it:
        if head:
            head(it)
        for k in range(unroll):
            body(Step(it, k, unroll, count))
    if head and lag:
        head(turns)
    for k in range(lag):
        body(Step(turns, k, unroll, count))


def gnn(nc, a, out):
    with ExitStack() as whole:
        def sb(name, shape, dt=F32, scope=whole):
            return scope.enter_context(nc.sbuf_tensor(name, shape, dt))

        banks = whole.enter_context(nc.psum_tensor("banks", [P, 8, 512], F32))
        taken = []

        def ps(name, shape, scope):
            count = shape[1] if len(shape) == 3 else 1
            n = len(taken)
            assert n + count <= 8, name
            taken.extend([name] * count)
            scope.callback(taken.__delitem__, slice(n, n + count))
            return banks[:, n:n + count] if len(shape) == 3 else banks[:, n]

        def sem(name, scope):
            if scope not in held:
                held[scope] = []
                scope.callback(clear, scope)
            held[scope].append(nc.alloc_semaphore(name))
            return held[scope][-1]

        held = {}

        def clear(scope):
            nc.clear_and_free_semaphores(held.pop(scope))
            nc.all_engine_barrier()

        k = {"in": a}
        k["acc"] = sb("acc", [P, NT, 512])
        k["xn"] = sb("xn", [P, NT, D])
        k["mrun"] = sb("mrun", [P, NT, HEADS])
        k["den"] = sb("den", [P, NT, HEADS])
        k["ident"] = sb("ident", [P, P])
        k["bigi"] = sb("bigi", [P, P], BF16)
        k["node_row"] = sb("node_row", [P, P])
        k["part"] = sb("part", [P, 1])
        k["dl"] = sb("dl", [P, ST])
        k["off"] = sb("off", [P, ST])
        k["idx"] = sb("idx", [P, ST, 2], I32)
        k["row_i"] = sb("row_i", [1, ST], I32)
        k["tile_i"] = sb("tile_i", [1, U + ST], I32)
        k["w1e"] = sb("w1e", [DE, D])
        k["wge"] = sb("wge", [DE, D])
        k["w2"] = sb("w2", [P, 2, D])
        k["b2s"] = sb("b2s", [PARTS, D], BF16)
        k["ones3"] = sb("ones3", [PARTS, P], BF16)
        k["emean"] = sb("emean", [ED, P])
        k["mv"] = sb("mv", [P, NT, 2])
        k["st"] = sb("st", [P, NT, 6])
        k["rstd"] = sb("rstd", [P, NT])
        k["rden"] = sb("rden", [P, NT * HEADS])
        k["sel"] = sb("sel", [P, 2 * PARTS])
        k["d_row"] = nc.dram_tensor("d_row", (ST, 1), I32, kind="Internal").ap()
        k["d_tile"] = nc.dram_tensor("d_tile", (ST, 1), I32, kind="Internal").ap()
        k["d_dl"] = nc.dram_tensor("d_dl", (ST, P), F32, kind="Internal").ap()
        k["d_ea"] = nc.dram_tensor("d_ea", (ST, EROWS, P), BF16, kind="Internal").ap()
        k["d_xw"] = nc.dram_tensor("d_xw", (NP, 2 * D), F32, kind="Internal").ap()
        for c, w in ((1, HEADS * HID + HEADS), (2, D + 1)):
            for side in "lr":
                k[f"d_x{side}{c}"] = nc.dram_tensor(f"d_x{side}{c}", (NP, w), F32, kind="Internal").ap()

        setup(nc, a, k, sb, ps, sem)
        with ExitStack() as scope:
            gated_steps(nc, a, k, sb, ps, sem, scope)
        with ExitStack() as scope:
            w = attention_weights(nc, a, k, sb, ps, sem, scope, 1, D, HEADS, HID)
            gated_nodes(nc, a, k, sb, ps, sem)
            project(nc, k, w, sb, ps, sem, 1, D, HEADS, HID)
            attention_steps(nc, k, w, sb, ps, sem, 1, HEADS, HID)
        with ExitStack() as scope:
            w = attention_weights(nc, a, k, sb, ps, sem, scope, 2, HEADS * HID, 1, D)
            attended_nodes(nc, a, k, sb, ps, sem)
            project(nc, k, w, sb, ps, sem, 2, HEADS * HID, 1, D)
            attention_steps(nc, k, w, sb, ps, sem, 2, 1, D)
        with ExitStack() as scope:
            last_nodes(nc, a, k, sb, ps, sem, out)


class Chain:

    def __init__(self, eng, semaphore):
        self.eng, self.semaphore, self.n = eng, semaphore, 0

    def __call__(self, instruction):
        self.n += 1
        instruction.then_inc(self.semaphore, 1)
        self.eng.wait_ge(self.semaphore, self.n)


def split(link, nc, src, parts, rest):
    link(nc.vector.tensor_copy(parts[0], src))
    link(nc.vector.tensor_tensor(rest, src, parts[0], ALU.subtract))
    link(nc.vector.tensor_copy(parts[1], rest))
    link(nc.vector.tensor_tensor(rest, rest, parts[1], ALU.subtract))
    link(nc.vector.tensor_copy(parts[2], rest))


def pick(link, nc, dst, parts, masks, n):
    for i in range(PARTS):
        link(nc.vector.tensor_scalar(parts[i], parts[i], masks[0:n, i:i + 1], None, ALU.mult))
    link(nc.vector.tensor_tensor(parts[0], parts[0], parts[1], ALU.add))
    link(nc.vector.tensor_tensor(dst, parts[0], parts[2], ALU.add))


def setup(nc, a, k, sb, ps, sem):
    with ExitStack() as scope:
        def tmp(name, shape, dt=F32):
            return sb("s_" + name, shape, dt, scope)

        wa = tmp("wa", [P, 2, 2 * D])
        ba = tmp("ba", [P, 2 * D])
        beta = tmp("beta", [P, D])
        xt = tmp("xt", [P, 2, 2, P])
        xws = tmp("xws", [P, 2, 2 * D])
        dst_i = tmp("dst_i", [P, DC], I32)
        dst_f = tmp("dst_f", [P, DC])
        below = tmp("below", [P, DC])
        cnt = tmp("cnt", [P, NT])
        ea = tmp("ea", [P, DC, ED])
        easum = tmp("easum", [P, ED])
        ones = tmp("ones", [P, P])
        iot_i = tmp("iot_i", [P, P], I32)
        par_i = tmp("par_i", [P, 1], I32)
        stp_i = tmp("stp_i", [P, SW], I32)
        stp = tmp("stp", [P, SW])
        first = tmp("first", [P, NT + 1])
        need = tmp("need", [P, NT])
        need_i = tmp("need_i", [P, NT], I32)
        wins_i = tmp("wins_i", [P, NT], I32)
        sa = tmp("sa", [P, 16 + NT])
        sbb = tmp("sbb", [P, 16 + NT])
        uu = tmp("uu", [P, 1 + NT])
        dd = tmp("dd", [P, NT])
        ge = tmp("ge", [P, NT])
        gd = tmp("gd", [P, NT])
        tcol = tmp("tcol", [P, SW])
        rcol = tmp("rcol", [P, SW])
        toff = tmp("toff", [P, SW])
        rcol_i = tmp("rcol_i", [P, SW], I32)
        tcol_i = tmp("tcol_i", [P, SW], I32)
        dwin = tmp("dwin", [P, SW, P], I32)
        swin = tmp("swin", [P, SW, P], I32)
        ewin = tmp("ewin", [P, SW, P * ED])
        dwf = tmp("dwf", [P, SW, P])
        swf = tmp("swf", [P, SW, P])
        dcl = tmp("dcl", [P, SW, P])
        dlw = tmp("dlw", [P, SW, P])
        eparts = tmp("eparts", [P, SW, PARTS, ED * P], BF16)
        erest = tmp("erest", [P, ED * P])
        on = tmp("on", [P, ST])
        b2r = tmp("b2r", [PARTS, D])
        b2p = tmp("b2p", [PARTS, PARTS, D], BF16)
        b2q = tmp("b2q", [PARTS, D])

        xw_ps = ps("xw_ps", [P, 2, 512], scope)
        cnt_ps = ps("cnt_ps", [P, 512], scope)
        tr_ps = ps("tr_ps", [P, 3, 512], scope)

        loaded_dst = sem("loaded_dst", scope)
        loaded = sem("loaded", scope)
        loaded_w = sem("loaded_w", scope)
        xt_in = [sem(f"xt_in{i}", scope) for i in range(2)]
        xw_made = sem("xw_made", scope)
        xw_taken = sem("xw_taken", scope)
        xw_out = [sem(f"xw_out{i}", scope) for i in range(2)]
        consts = sem("consts", scope)
        pool_own = sem("pool_own", scope)
        counted = sem("counted", scope)
        summed = sem("summed", scope)
        rows_known = sem("rows_known", scope)
        table_out = sem("table_out", scope)
        row_out = sem("row_out", scope)
        row_in = sem("row_in", scope)
        win_in = sem("win_in", scope)
        win_f = sem("win_f", scope)
        turned = sem("turned", scope)
        esplit = sem("esplit", scope)
        zeroed = sem("zeroed", scope)
        dve_own = sem("dve_own", scope)
        xb = sem("xb", scope)

        with nc.Block() as block:
            @block.sync
            def _(sp):
                sp.dma_start(dst_i[:], a["dst"].rearrange("(p c) one -> p (c one)", p=P)).then_inc(loaded_dst, 16)
                for c in range(2):
                    sp.dma_start(wa[:, c, 0:D], a["W1"][c * P:(c + 1) * P, :]).then_inc(loaded_w, 16)
                    sp.dma_start(wa[:, c, D:], a["Wg"][c * P:(c + 1) * P, :]).then_inc(loaded_w, 16)
                sp.dma_start(ba[:, 0:D], a["b1"].to_broadcast((P, D))).then_inc(loaded_w, 16)
                sp.dma_start(ba[:, D:], a["bg"].to_broadcast((P, D))).then_inc(loaded_w, 16)

                def load_xt(i):
                    if i.back(2).live:
                        sp.wait_ge(xw_made, i.back(2).done)
                    sp.dma_start(xt[:, i.slot(2)], a["xt"].rearrange("(c p) n -> p c n", p=P)[
                        :, :, bass.ds(i.s * P, P)]).then_inc(xt_in[i.slot(2)], 16)

                def body(i):
                    if i.live:
                        load_xt(i)
                    j = i.back(2)
                    if j.live:
                        sp.wait_ge(xw_taken, j.done)
                        sp.dma_start(k["d_xw"][bass.ds(j.s * P, P), :], xws[:, j.slot(2)]).then_inc(xw_out[j.slot(2)], 16)
                run_steps(sp, body, 2, NT, 2)
                for i in range(2):
                    sp.wait_ge(xw_out[i], 16 * (NT // 2))

            @block.scalar
            def _(act):
                act.dma_start(ea[:], a["ea4"].rearrange("(p c) k -> p c k", p=P)).then_inc(loaded, 16)
                act.dma_start(beta[:], a["beta"].to_broadcast((P, D))).then_inc(loaded, 16)
                act.dma_start(k["xn"][:], a["x"].rearrange("(t p) f -> p t f", p=P)).then_inc(loaded, 16)
                act.dma_start(k["acc"][:, :, 0:D], a["x"].rearrange("(t p) f -> p t f", p=P)).then_inc(loaded, 16)
                act.dma_start(k["w1e"][:], a["W1"][D:D + DE, :]).then_inc(loaded, 16)
                act.dma_start(k["wge"][:], a["Wg"][D:D + DE, :]).then_inc(loaded, 16)
                act.dma_start(k["w2"][:], a["W2"].rearrange("(c p) f -> p c f", p=P)).then_inc(loaded, 16)
                act.dma_start(b2r[:], a["b2"].to_broadcast((PARTS, D))).then_inc(loaded, 16)
                act.wait_ge(rows_known, 2)
                with nc.allow_non_contiguous_dma(reason="a number a step"):
                    act.dma_start(k["d_row"].rearrange("(j p) one -> p (j one)", p=P), rcol_i[:]).then_inc(row_out, 16)
                    act.dma_start(k["d_tile"].rearrange("(j p) one -> p (j one)", p=P), tcol_i[:]).then_inc(row_out, 16)
                act.wait_ge(row_out, 32)
                act.dma_start(k["row_i"][:], k["d_row"].rearrange("s one -> one s")).then_inc(row_in, 16)
                act.wait_ge(zeroed, 1)
                act.dma_start(k["tile_i"][0:1, U:], k["d_tile"].rearrange("s one -> one s")).then_inc(row_in, 16)
                act.wait_ge(win_f, 1)
                act.dma_start(k["d_dl"].rearrange("(j p) e -> p j e", p=P), dlw[:]).then_inc(table_out, 16)
                for j in range(SW):
                    act.wait_ge(esplit, j + 1)
                    for i in range(PARTS):
                        act.dma_start(
                            k["d_ea"][j * P:(j + 1) * P, i * PARTS * ED:(i + 1) * PARTS * ED, :].rearrange("s r e -> s (r e)"),
                            eparts[:, j].rearrange("p a b -> p (a b)")).then_inc(table_out, 16)
                act.wait_ge(row_in, 32)
                act.wait_ge(table_out, 16 + 16 * SW * PARTS)
                act.wait_ge(loaded, 16 * 8)

            @block.gpsimd
            def _(pool):
                nc.gpsimd.iota(iot_i[:], [[1, P]], base=0, channel_multiplier=0)
                nc.gpsimd.iota(par_i[:], [[0, 1]], base=0, channel_multiplier=1)
                nc.gpsimd.iota(stp_i[:], [[P, SW]], base=0, channel_multiplier=1)
                nc.gpsimd.memset(ones[:], 1.0)
                nc.gpsimd.memset(k["den"][:], 1.0)
                nc.gpsimd.memset(k["ident"][:], 0.0)
                nc.gpsimd.memset(k["bigi"][:], 0.0).then_inc(pool_own, 1)
                pool.wait_ge(pool_own, 1)
                nc.gpsimd.affine_select(out=k["ident"][:], in_=k["ident"][:], compare_op=ALU.not_equal, fill=1.0,
                                        base=0, pattern=[[-1, P]], channel_multiplier=1)
                nc.gpsimd.affine_select(out=k["bigi"][:], in_=k["bigi"][:], compare_op=ALU.not_equal, fill=BIG,
                                        base=0, pattern=[[-1, P]], channel_multiplier=1).then_inc(consts, 1)
                pool.wait_ge(rows_known, 1)
                for j in range(SW):
                    at = bass.IndirectOffsetOnAxis(ap=rcol_i[:, j:j + 1], axis=0)
                    nc.gpsimd.indirect_dma_start(out=dwin[:, j], out_offset=None, in_=a["dst"], in_offset=at).then_inc(win_in, 16)
                    nc.gpsimd.indirect_dma_start(out=swin[:, j], out_offset=None, in_=a["src"], in_offset=at).then_inc(win_in, 16)
                    nc.gpsimd.indirect_dma_start(out=ewin[:, j], out_offset=None, in_=a["ea4"], in_offset=at).then_inc(win_in, 16)
                pool.wait_ge(loaded, 16 * 8)
                for t in range(NT):
                    last = nc.gpsimd.tensor_tensor(k["xn"][:, t], k["xn"][:, t], beta[:], ALU.add)
                last.then_inc(xb, 1)

            @block.tensor
            def _(pe):
                pe.wait_ge(loaded_w, 16 * 6)

                def body(i):
                    pe.wait_ge(xt_in[i.slot(2)], i.turns(2) * 16)
                    if i.back(2).live:
                        pe.wait_ge(xw_taken, i.back(2).done)
                    for c in range(2):
                        last = nc.tensor.matmul(xw_ps[:, i.slot(2)], xt[:, i.slot(2), c], wa[:, c], start=(c == 0), stop=(c == 1))
                    last.then_inc(xw_made, 1)
                run_steps(pe, body, 2, NT, 0)
                pe.wait_ge(consts, 1)
                pe.wait_ge(counted, 1)
                nc.tensor.matmul(cnt_ps[:, 0:NT], ones[:], cnt[:], start=True, stop=True)
                nc.tensor.matmul(cnt_ps[0:ED, P:2 * P], easum[:], ones[:], start=True, stop=True).then_inc(summed, 1)
                pe.wait_ge(win_f, 2)
                for n, src in enumerate((dlw, swf, dcl)):
                    for j in range(SW):
                        last = nc.tensor.transpose(tr_ps[:, n, j * P:(j + 1) * P], src[:, j], k["ident"][:])
                last.then_inc(turned, 1)

            @block.vector
            def _(dve):
                link = Chain(dve, dve_own)
                nc.vector.memset(k["tile_i"][:], 0).then_inc(zeroed, 1)
                nc.vector.memset(k["ones3"][:], 1.0)
                nc.vector.memset(sa[:], 0.0)
                nc.vector.memset(uu[:], 0.0)
                link(nc.vector.memset(sbb[:], 0.0))
                dve.wait_ge(loaded_dst, 16)
                link(nc.vector.tensor_copy(dst_f[:], dst_i[:]))
                for t in range(NT):
                    last = nc.vector.tensor_scalar(below[:], dst_f[:], float(t * P), None, ALU.is_lt, ALU.add,
                                                   accum_out=cnt[:, t:t + 1])
                    link(last)
                dve.wait_ge(loaded, 16 * 8)
                nc.vector.tensor_reduce(easum[:], ea[:].rearrange("p c k -> p k c"), AX.X, ALU.add).then_inc(counted, 1)

                dve.wait_ge(consts, 1)
                link(nc.vector.tensor_copy(k["node_row"][:], iot_i[:]))
                link(nc.vector.tensor_copy(k["part"][:], par_i[:]))
                link(nc.vector.tensor_copy(stp[:], stp_i[:]))
                for g, size in ((0, 1), (PARTS, PARTS * ED)):
                    for i in range(PARTS):
                        m = k["sel"][:, g + i:g + i + 1]
                        link(nc.vector.tensor_scalar(m, k["part"][:], float(i * size), None, ALU.is_ge))
                        link(nc.vector.tensor_scalar(below[:, 0:1], k["part"][:], float((i + 1) * size), None, ALU.is_lt))
                        link(nc.vector.tensor_tensor(m, m, below[:, 0:1], ALU.mult))
                split(link, nc, b2r[:], [b2p[:, i] for i in range(PARTS)], b2q[:])
                pick(link, nc, k["b2s"][:], [b2p[:, i] for i in range(PARTS)], k["sel"], PARTS)

                def take(i):
                    dve.wait_ge(xw_made, i.done)
                    if i.back(2).live:
                        dve.wait_ge(xw_out[i.slot(2)], i.back(2).turns(2) * 16)
                    nc.vector.tensor_tensor(xws[:, i.slot(2)], xw_ps[:, i.slot(2)], ba[:], ALU.add).then_inc(xw_taken, 1)
                dve.wait_ge(loaded_w, 16 * 6)
                run_steps(dve, take, 2, NT, 0)

                dve.wait_ge(summed, 1)
                link(nc.vector.tensor_copy(first[:, 0:NT], cnt_ps[:, 0:NT]))
                link(nc.vector.memset(first[:, NT:], float(E)))
                link(nc.vector.tensor_scalar(k["emean"][:], cnt_ps[0:ED, P:2 * P], 1.0 / E, None, ALU.mult))
                link(nc.vector.tensor_tensor(need[:], first[:, 1:], first[:, 0:NT], ALU.subtract))
                link(nc.vector.tensor_scalar(need_i[:], need[:], float(P - 1), None, ALU.add))
                link(nc.vector.tensor_scalar(wins_i[:], need_i[:], P.bit_length() - 1, None, ALU.arith_shift_right))
                link(nc.vector.tensor_copy(sa[:, 17:], wins_i[:, 0:NT - 1]))
                cur, other = sa, sbb
                for d in (1, 2, 4, 8, 16):
                    link(nc.vector.tensor_tensor(other[:, 16:], cur[:, 16:], cur[:, 16 - d:16 + NT - d], ALU.add))
                    cur, other = other, cur
                starts = cur[:, 16:]
                link(nc.vector.tensor_scalar(uu[:, 1:], starts, -float(P), None, ALU.mult))
                link(nc.vector.tensor_tensor(uu[:, 1:], uu[:, 1:], first[:, 0:NT], ALU.add))
                link(nc.vector.tensor_tensor(dd[:], uu[:, 1:], uu[:, 0:NT], ALU.subtract))
                for j in range(SW):
                    link(nc.vector.tensor_scalar(ge[:], starts, stp[:, j:j + 1], None, ALU.is_le, ALU.add,
                                                 accum_out=tcol[:, j:j + 1]))
                    link(nc.vector.tensor_tensor_reduce(gd[:], ge[:], dd[:], 1.0, 0.0, ALU.mult, ALU.add,
                                                        rcol[:, j:j + 1]))
                link(nc.vector.scalar_tensor_tensor(rcol[:], stp[:], float(P), rcol[:], ALU.mult, ALU.add))
                nc.vector.tensor_scalar(rcol_i[:], rcol[:], float(RMAX), None, ALU.min).then_inc(rows_known, 1)
                link(nc.vector.tensor_scalar(toff[:], tcol[:], float(P), -float(P), ALU.mult, ALU.add))
                nc.vector.tensor_scalar(tcol_i[:], tcol[:], -1.0, None, ALU.add).then_inc(rows_known, 1)

                dve.wait_ge(win_in, 16 * 3 * SW)
                link(nc.vector.tensor_copy(dwf[:], dwin[:]))
                link(nc.vector.tensor_copy(swf[:], swin[:]))
                link(nc.vector.tensor_scalar(dcl[:], dwf[:], float(N - 1), None, ALU.min))
                for j in range(SW):
                    last = nc.vector.tensor_scalar(dlw[:, j], dwf[:, j], toff[:, j:j + 1], None, ALU.subtract)
                last.then_inc(win_f, 2)
                dve.wait_ge(turned, 1)
                link(nc.vector.tensor_copy(k["dl"][:], tr_ps[:, 0]))
                link(nc.vector.tensor_copy(k["idx"][:, :, 0], tr_ps[:, 1]))
                link(nc.vector.tensor_copy(k["idx"][:, :, 1], tr_ps[:, 2]))
                link(nc.vector.tensor_scalar(on[:], k["dl"][:], 0.0, None, ALU.is_ge))
                link(nc.vector.tensor_scalar(k["off"][:], k["dl"][:], float(P), None, ALU.is_lt))
                link(nc.vector.tensor_tensor(k["off"][:], k["off"][:], on[:], ALU.mult))
                link(nc.vector.tensor_scalar(k["off"][:], k["off"][:], -1.0, BIG, ALU.add, ALU.mult))
                for j in range(SW):
                    parts = [eparts[:, j, i].rearrange("p (k e) -> p k e", e=P) for i in range(PARTS)]
                    src = ewin[:, j].rearrange("p (e k) -> p k e", k=ED)
                    split(link, nc, src, parts, erest[:].rearrange("p (k e) -> p k e", e=P))
                    nc.vector.tensor_copy(gd[:, 0:1], ge[:, 0:1]).then_inc(esplit, 1)
                dve.wait_ge(xb, 1)


def gated_steps(nc, a, k, sb, ps, sem, scope):
    RING = 4
    with ExitStack() as scope:
        ix = sb("g_ix", [P, 2, IRING, 2], I32, scope)
        xw = sb("g_xw", [P, RING, 2 * D], F32, scope)
        eat = sb("g_eat", [DE, RING, P], F32, scope)
        rt = sb("g_rt", [P, 2, 2 * P], F32, scope)
        gate = sb("g_gate", [P, 2, D], F32, scope)
        msg = sb("g_msg", [P, 2, D], F32, scope)
        hot = sb("g_hot", [P, 2, P], F32, scope)
        hid_ps = ps("hid_ps", [P, 2, 512], scope)
        gate_ps = ps("gate_ps", [P, 2, 512], scope)
        core_ps = ps("core_ps", [P, 2, 512], scope)
        sum_ps = ps("sum_ps", [P, 2, 512], scope)

        ix_ready = sem("g_ix_ready", scope)
        xw_in = [sem(f"g_xw_in{i}", scope) for i in range(RING)]
        ea_in = [sem(f"g_ea_in{i}", scope) for i in range(RING)]
        hid_made = sem("g_hid_made", scope)
        relu_made = sem("g_relu_made", scope)
        gate_in = sem("g_gate_in", scope)
        gate_made = sem("g_gate_made", scope)
        core_made = sem("g_core_made", scope)
        hot_made = sem("g_hot_made", scope)
        msg_made = sem("g_msg_made", scope)
        sum_made = sem("g_sum_made", scope)
        added = sem("g_added", scope)

        with nc.Block() as block:
            @block.sync
            def _(sp):
                regs = [sp.alloc_register(f"g_row{i}") for i in range(U)]
                rows = [None] * U

                def head(it):
                    sp.load(regs, k["row_i"][0:1, bass.ds(it * U, U)])
                    for i in range(U):
                        rows[i] = sp.snap(regs[i], min_val=0, max_val=RMAX)

                def body(i):
                    if i.back(RING).live:
                        sp.wait_ge(hid_made, i.back(RING).done)
                        nc.sync.nop(nofuse=True)
                    sp.dma_start(eat[:, i.slot(RING)], a["ea64t"][:, bass.ds(rows[i.k], P)]).then_inc(ea_in[i.slot(RING)], 16)
                run_steps(sp, body, U, STEPS, 0, head)

            @block.gpsimd
            def _(pool):
                def body(i):
                    if i.k % IRING == 0:
                        if i.back(2 * IRING).live:
                            j = i.back(IRING + 1)
                            pool.wait_ge(xw_in[j.slot(RING)], j.turns(RING) * 16)
                        nc.gpsimd.tensor_copy(ix[:, i.k // IRING % 2], k["idx"][:, bass.ds(i.s, IRING), :]).then_inc(ix_ready, 1)
                        pool.wait_ge(ix_ready, i.turns(IRING))
                        nc.gpsimd.nop(nofuse=True)
                    if i.back(RING).live:
                        pool.wait_ge(gate_in, i.back(RING).done)
                        pool.wait_ge(hid_made, i.back(RING).done)
                        nc.gpsimd.nop(nofuse=True)
                    at = bass.IndirectOffsetOnAxis(ap=ix[:, i.k // IRING % 2, i.k % IRING, 0:1], axis=0)
                    nc.gpsimd.indirect_dma_start(out=xw[:, i.slot(RING)], out_offset=None, in_=k["d_xw"],
                                                 in_offset=at).then_inc(xw_in[i.slot(RING)], 16)
                run_steps(pool, body, U, STEPS, 0)

            @block.tensor
            def _(pe):
                def body(i):
                    j = i.back(1)
                    if j.live:
                        pe.wait_ge(relu_made, j.done)
                        if j.back(2).live:
                            pe.wait_ge(msg_made, j.back(2).done)
                        o = core_ps[:, j.slot(2), 0:D]
                        for c in range(2):
                            nc.tensor.matmul(o, rt[:, j.slot(2), c * P:(c + 1) * P], k["w2"][:, c], start=(c == 0), stop=False)
                        nc.tensor.matmul(o, k["ones3"][:], k["b2s"][:], start=False, stop=True).then_inc(core_made, 1)
                    if i.live:
                        pe.wait_ge(ea_in[i.slot(RING)], i.turns(RING) * 16)
                        pe.wait_ge(xw_in[i.slot(RING)], i.turns(RING) * 16)
                        if i.back(2).live:
                            pe.wait_ge(relu_made, i.back(2).done)
                            pe.wait_ge(gate_in, i.back(2).done)
                        e = eat[:, i.slot(RING)]
                        for c in range(2):
                            cols = slice(c * P, (c + 1) * P)
                            nc.tensor.matmul(hid_ps[:, i.slot(2), cols], xw[:, i.slot(RING), cols], k["ident"][:],
                                             is_transpose=True, start=True, stop=False, skip_group_check=True)
                            nc.tensor.matmul(hid_ps[:, i.slot(2), cols], k["w1e"][:, cols], e,
                                             start=False, stop=True, skip_group_check=True)
                        nc.tensor.matmul(gate_ps[:, i.slot(2), 0:D], e, k["wge"][:], start=True, stop=True).then_inc(hid_made, 1)
                    j = i.back(2)
                    if j.live:
                        pe.wait_ge(msg_made, j.done)
                        pe.wait_ge(hot_made, j.done)
                        if j.back(2).live:
                            pe.wait_ge(added, j.back(2).done)
                        nc.tensor.matmul(sum_ps[:, j.slot(2), 0:D], hot[:, j.slot(2)], msg[:, j.slot(2)],
                                         start=True, stop=True).then_inc(sum_made, 1)
                run_steps(pe, body, U, STEPS, 2)

            @block.scalar
            def _(act):
                def body(i):
                    act.wait_ge(hid_made, i.done)
                    if i.back(2).live:
                        act.wait_ge(core_made, i.back(2).done)
                    nc.scalar.activation(rt[:, i.slot(2)], hid_ps[:, i.slot(2), 0:2 * P], ACT.Relu).then_inc(relu_made, 1)
                    act.wait_ge(gate_in, i.done)
                    nc.scalar.activation(gate[:, i.slot(2)], gate[:, i.slot(2)], ACT.Sigmoid).then_inc(gate_made, 1)
                run_steps(act, body, U, STEPS, 0)

            @block.vector
            def _(dve):
                LAG = 2
                regs = [dve.alloc_register(f"g_tile{i}") for i in range(U)]
                tiles = [None] * U

                def head(it):
                    dve.load(regs, k["tile_i"][0:1, bass.ds(it * U + (U - LAG), U)])
                    for i in range(U):
                        tiles[i] = dve.snap(regs[i], min_val=0, max_val=NT - 1)

                def body(i):
                    j = i.back(1)
                    if j.live:
                        if j.back(2).live:
                            dve.wait_ge(sum_made, j.back(2).done)
                        nc.vector.tensor_scalar(hot[:, j.slot(2)], k["node_row"][:], k["dl"][:, bass.ds(j.s, 1)], None,
                                                ALU.is_equal).then_inc(hot_made, 1)
                        dve.wait_ge(core_made, j.done)
                        dve.wait_ge(gate_made, j.done)
                        nc.vector.tensor_tensor(msg[:, j.slot(2)], core_ps[:, j.slot(2), 0:D], gate[:, j.slot(2)],
                                                ALU.mult).then_inc(msg_made, 1)
                    if i.live:
                        dve.wait_ge(hid_made, i.done)
                        dve.wait_ge(xw_in[i.slot(RING)], i.turns(RING) * 16)
                        if i.back(2).live:
                            dve.wait_ge(msg_made, i.back(2).done)
                        nc.vector.tensor_tensor(gate[:, i.slot(2)], gate_ps[:, i.slot(2), 0:D], xw[:, i.slot(RING), D:],
                                                ALU.add).then_inc(gate_in, 1)
                    j = i.back(LAG)
                    if j.live:
                        dve.wait_ge(sum_made, j.done)
                        if j.back(1).live:
                            dve.wait_ge(added, j.back(1).done)
                        row = k["acc"][:, bass.ds(tiles[i.k], 1), 0:D].rearrange("p t f -> p (t f)")
                        nc.vector.tensor_tensor(row, row, sum_ps[:, j.slot(2), 0:D], ALU.add).then_inc(added, 1)
                run_steps(dve, body, U, STEPS, LAG, head)


def attention_weights(nc, a, k, sb, ps, sem, scope, layer, din, heads, ch):
    W = heads * ch
    K = din // P
    w = {
        "wl": sb(f"wl{layer}", [P, K, W], F32, scope), "wr": sb(f"wr{layer}", [P, K, W], F32, scope),
        "lin": sb(f"lin{layer}", [P, K, 2 * heads], F32, scope),
        "we": sb(f"we{layer}", [EROWS, W + heads], BF16, scope),
        "ebias": sb(f"ebias{layer}", [P, W + heads], F32, scope),
        "att_row": sb(f"att_row{layer}", [P, W], F32, scope),
        "att_col": sb(f"att_col{layer}", [P, W // P], F32, scope),
    }
    with ExitStack() as own:
        wef = sb(f"wef{layer}", [EROWS, W + heads], F32, own)
        weq = sb(f"weq{layer}", [EROWS, W + heads], F32, own)
        wep = sb(f"wep{layer}", [EROWS, PARTS, W + heads], BF16, own)
        prod = sb(f"prod{layer}", [P, W], F32, own)
        arow = sb(f"arow{layer}", [P, W], F32, own)
        ebias_ps = ps(f"ebias_ps{layer}", [P, 2, 512], own)
        loaded = sem(f"w_loaded{layer}", own)
        dve_own = sem(f"w_dve_own{layer}", own)
        we_made = sem(f"w_we_made{layer}", own)
        eb_made = sem(f"w_eb_made{layer}", own)
        n_loads = 4 + PARTS * PARTS
        with nc.Block() as block:
            @block.sync
            def _(sp):
                sp.dma_start(w["wl"][:], a[f"Wl{layer}"].rearrange("(c p) f -> p c f", p=P)).then_inc(loaded, 16)
                sp.dma_start(w["wr"][:], a[f"Wr{layer}"].rearrange("(c p) f -> p c f", p=P)).then_inc(loaded, 16)
                sp.dma_start(arow[:], a[f"att{layer}"].to_broadcast((P, W))).then_inc(loaded, 16)
                with nc.allow_non_contiguous_dma(reason="a column of attention weights"):
                    sp.dma_start(w["att_col"][:], a[f"att{layer}"].rearrange("one (c p) -> p (one c)", p=P)).then_inc(loaded, 16)
                for g in range(PARTS * PARTS):
                    sp.dma_start(wef[g * ED:(g + 1) * ED, 0:W], a[f"We{layer}"]).then_inc(loaded, 16)

            @block.vector
            def _(dve):
                link = Chain(dve, dve_own)
                dve.wait_ge(loaded, 16 * n_loads)
                link(nc.vector.tensor_scalar(w["att_row"][:], arow[:], 1.0 - SLOPE, None, ALU.mult))
                link(nc.vector.tensor_scalar(w["att_col"][:], w["att_col"][:], 1.0 - SLOPE, None, ALU.mult))
                for h in range(heads):
                    cols = slice(h * ch, (h + 1) * ch)
                    for side, src in enumerate((w["wl"], w["wr"])):
                        for c in range(K):
                            link(nc.vector.tensor_tensor_reduce(prod[:, cols], src[:, c, cols], arow[:, cols], SLOPE, 0.0,
                                                                ALU.mult, ALU.add,
                                                                w["lin"][:, c, side * heads + h:side * heads + h + 1]))
                    link(nc.vector.tensor_tensor_reduce(prod[0:EROWS, cols], wef[:, cols], arow[0:EROWS, cols], SLOPE, 0.0,
                                                        ALU.mult, ALU.add, wef[:, W + h:W + h + 1]))
                nc.vector.tensor_copy(prod[:, 0:1], arow[:, 0:1]).then_inc(we_made, 1)
                split(link, nc, wef[:], [wep[:, i] for i in range(PARTS)], weq[:])
                pick(link, nc, w["we"][:], [wep[:, i] for i in range(PARTS)], k["sel"][:, PARTS:], EROWS)
                dve.wait_ge(eb_made, 1)
                link(nc.vector.tensor_copy(w["ebias"][:, 0:W], ebias_ps[:, 0, 0:W]))
                link(nc.vector.tensor_copy(w["ebias"][:, W:], ebias_ps[:, 1, 0:heads]))

            @block.tensor
            def _(pe):
                pe.wait_ge(we_made, 1)
                nc.tensor.matmul(ebias_ps[:, 0, 0:W], k["emean"][:], wef[0:ED, 0:W], start=True, stop=True)
                nc.tensor.matmul(ebias_ps[:, 1, 0:heads], k["emean"][:], wef[0:ED, W:], start=True, stop=True).then_inc(eb_made, 1)
    return w


def spread(k, nc, dve, act_sem, dve_sem, link, count):
    for t in range(NT):
        last = nc.vector.bn_aggr(k["mv"][:, t], k["st"][:, t])
    link(last)
    nc.vector.tensor_scalar(k["rstd"][:], k["mv"][:, :, 1], EPS, None, ALU.add).then_inc(dve_sem, 1)
    dve.wait_ge(act_sem, count)
    link(nc.vector.reciprocal(k["rstd"][:], k["rstd"][:]))


def root(k, nc, act, act_sem, dve_sem, count):
    act.wait_ge(dve_sem, count)
    nc.scalar.activation(k["rstd"][:], k["rstd"][:], ACT.Sqrt).then_inc(act_sem, 1)


def tile_of(buf, t, width):
    return buf[:, bass.ds(t, 1), 0:width].rearrange("p t f -> p (t f)")


def gated_nodes(nc, a, k, sb, ps, sem):
    with ExitStack() as own:
        gamma = sb("gamma", [P, D], F32, own)
        y = sb("gn_y", [P, 2, D], F32, own)
        loaded = sem("gn_loaded", own)
        stats = sem("gn_stats", own)
        dve_own = sem("gn_own", own)
        to_root = sem("gn_to_root", own)
        rooted = sem("gn_rooted", own)
        normed = sem("gn_normed", own)
        scaled = sem("gn_scaled", own)
        shifted = sem("gn_shifted", own)
        with nc.Block() as block:
            @block.sync
            def _(sp):
                sp.dma_start(gamma[:], a["gamma"].to_broadcast((P, D))).then_inc(loaded, 16)

            @block.scalar
            def _(act):
                for n in range(2):
                    root(k, nc, act, rooted, to_root, n + 1)

            @block.vector
            def _(dve):
                link = Chain(dve, dve_own)

                def stat(i):
                    nc.vector.bn_stats(tile_of(k["st"], i.s, 6), tile_of(k["acc"], i.s, D)).then_inc(stats, 1)
                run_steps(dve, stat, 2, NT, 0)
                dve.wait_ge(stats, NT)
                spread(k, nc, dve, rooted, to_root, link, 1)
                dve.wait_ge(loaded, 16)

                def body(i):
                    if i.live:
                        if i.back(2).live:
                            dve.wait_ge(shifted, i.back(2).done)
                        nc.vector.tensor_scalar(y[:, i.slot(2)], tile_of(k["acc"], i.s, D), k["mv"][:, bass.ds(i.s, 1), 0],
                                                k["rstd"][:, bass.ds(i.s, 1)], ALU.subtract, ALU.mult).then_inc(normed, 1)
                    j = i.back(1)
                    if j.live:
                        dve.wait_ge(normed, j.done)
                        nc.vector.tensor_tensor(y[:, j.slot(2)], y[:, j.slot(2)], gamma[:], ALU.mult).then_inc(scaled, 1)
                        dve.wait_ge(scaled, j.done)
                        nc.vector.tensor_tensor(tile_of(k["acc"], j.s, D), y[:, j.slot(2)], tile_of(k["xn"], j.s, D),
                                                ALU.add).then_inc(shifted, 1)
                    j = i.back(2)
                    if j.live:
                        dve.wait_ge(shifted, j.done)
                        nc.vector.bn_stats(tile_of(k["st"], j.s, 6), tile_of(k["acc"], j.s, D)).then_inc(stats, 1)
                run_steps(dve, body, 2, NT, 2)
                dve.wait_ge(stats, 2 * NT)
                spread(k, nc, dve, rooted, to_root, link, 2)


def attended_nodes(nc, a, k, sb, ps, sem):
    W = HEADS * HID
    with ExitStack() as own:
        bias = sb("an_bias", [P, W], F32, own)
        loaded = sem("an_loaded", own)
        stats = sem("an_stats", own)
        dve_own = sem("an_own", own)
        to_root = sem("an_to_root", own)
        rooted = sem("an_rooted", own)
        divided = sem("an_divided", own)
        with nc.Block() as block:
            @block.sync
            def _(sp):
                sp.dma_start(bias[:], a["cb1"].to_broadcast((P, W))).then_inc(loaded, 16)

            @block.scalar
            def _(act):
                root(k, nc, act, rooted, to_root, 1)

            @block.vector
            def _(dve):
                link = Chain(dve, dve_own)
                den = k["den"][:].rearrange("p t h -> p (t h)")
                link(nc.vector.tensor_scalar(den, den, 1e-16, None, ALU.add))
                link(nc.vector.reciprocal(k["rden"][:], den))
                dve.wait_ge(loaded, 16)

                def body(i):
                    if i.live:
                        for h in range(HEADS):
                            row = k["acc"][:, bass.ds(i.s, 1), h * HID:(h + 1) * HID].rearrange("p t f -> p (t f)")
                            last = nc.vector.scalar_tensor_tensor(row, row, k["rden"][:, bass.ds(i.s * HEADS + h, 1)],
                                                                  bias[:, h * HID:(h + 1) * HID], ALU.mult, ALU.add)
                        last.then_inc(divided, 1)
                    j = i.back(1)
                    if j.live:
                        dve.wait_ge(divided, j.done)
                        nc.vector.bn_stats(tile_of(k["st"], j.s, 6), tile_of(k["acc"], j.s, W)).then_inc(stats, 1)
                run_steps(dve, body, 2, NT, 1)
                dve.wait_ge(stats, NT)
                spread(k, nc, dve, rooted, to_root, link, 1)
                link(nc.vector.memset(k["den"][:], 1.0))


def project(nc, k, w, sb, ps, sem, layer, din, heads, ch):
    W = heads * ch
    K = din // P
    n = f"p{layer}_"
    dl, dr = k[f"d_xl{layer}"], k[f"d_xr{layer}"]
    with ExitStack() as own:
        xs = sb(n + "xs", [P, 2, din], F32, own)
        xt = sb(n + "xt", [P, 2, din], F32, own)
        xl = sb(n + "xl", [P, 2, W + heads], F32, own)
        xr = sb(n + "xr", [P, 2, W + heads], F32, own)
        xre = sb(n + "xre", [P, 2, W + heads], F32, own)
        own_m = sb(n + "own_m", [P, 2, W + heads], F32, own)
        prod = sb(n + "prod", [P, W], F32, own)
        q = sb(n + "q", [P, 2, heads], F32, own)
        if layer == 2:
            gain = sb(n + "gain", [P, din], F32, own)
            offset = sb(n + "offset", [P, din], F32, own)
            ya = sb(n + "ya", [P, 2, din], F32, own)
            yb = sb(n + "yb", [P, 2, din], F32, own)
        xt_ps = ps(n + "xt_ps", [P, 2, 512], own)
        xl_ps = ps(n + "xl_ps", [P, 2, 512], own)
        xr_ps = ps(n + "xr_ps", [P, 2, 512], own)
        lin_ps = ps(n + "lin_ps", [P, 2, 512], own)
        loaded = sem(n + "loaded", own)
        normed = sem(n + "normed", own)
        gained = sem(n + "gained", own)
        offsetted = sem(n + "offsetted", own)
        lowed = sem(n + "lowed", own)
        exped = sem(n + "exped", own)
        x_made = sem(n + "x_made", own)
        x_kept = sem(n + "x_kept", own)
        turned = sem(n + "turned", own)
        xt_made = sem(n + "xt_made", own)
        rows_made = sem(n + "rows_made", own)
        l_taken = sem(n + "l_taken", own)
        r_taken = sem(n + "r_taken", own)
        lin_taken = sem(n + "lin_taken", own)
        summed = sem(n + "summed", own)
        xre_made = sem(n + "xre_made", own)
        acc_set = sem(n + "acc_set", own)
        highed = sem(n + "highed", own)
        scored = sem(n + "scored", own)
        m_set = sem(n + "m_set", own)
        l_out = [sem(n + f"l_out{i}", own) for i in range(2)]
        r_out = [sem(n + f"r_out{i}", own) for i in range(2)]

        with nc.Block() as block:
            @block.sync
            def _(sp):
                if layer == 2:
                    sp.dma_start(gain[:], k["in"]["g1"].to_broadcast((P, din))).then_inc(loaded, 16)
                    sp.dma_start(offset[:], k["in"]["be1"].to_broadcast((P, din))).then_inc(loaded, 16)

                def body(i):
                    sp.wait_ge(l_taken, i.done)
                    sp.wait_ge(lin_taken, i.done)
                    sp.dma_start(dl[bass.ds(i.s * P, P), 0:W + heads], xl[:, i.slot(2)]).then_inc(l_out[i.slot(2)], 16)
                    sp.wait_ge(r_taken, i.done)
                    sp.dma_start(dr[bass.ds(i.s * P, P), 0:W + heads], xr[:, i.slot(2)]).then_inc(r_out[i.slot(2)], 16)
                run_steps(sp, body, 2, NT, 0)
                for i in range(2):
                    sp.wait_ge(l_out[i], 16 * (NT // 2))
                    sp.wait_ge(r_out[i], 16 * (NT // 2))

            @block.tensor
            def _(pe):
                def body(i):
                    if i.live:
                        pe.wait_ge(x_made, i.done)
                        if i.back(2).live:
                            pe.wait_ge(xt_made, i.back(2).done)
                        for c in range(K):
                            last = nc.tensor.transpose(xt_ps[:, i.slot(2), c * P:(c + 1) * P], xs[:, i.slot(2), c * P:(c + 1) * P],
                                                       k["ident"][:])
                        last.then_inc(turned, 1)
                    j = i.back(1)
                    if j.live:
                        pe.wait_ge(xt_made, j.done)
                        if j.back(2).live:
                            pe.wait_ge(l_taken, j.back(2).done)
                            pe.wait_ge(r_taken, j.back(2).done)
                            pe.wait_ge(lin_taken, j.back(2).done)
                        for bank, m, width in ((xl_ps, w["wl"], W), (xr_ps, w["wr"], W), (lin_ps, w["lin"], 2 * heads)):
                            for c in range(K):
                                last = nc.tensor.matmul(bank[:, j.slot(2), 0:width], xt[:, j.slot(2), c * P:(c + 1) * P], m[:, c],
                                                        start=(c == 0), stop=(c == K - 1))
                        last.then_inc(rows_made, 1)
                run_steps(pe, body, 2, NT, 1)

            @block.scalar
            def _(act):
                def body(i):
                    if i.live:
                        if layer == 2:
                            act.wait_ge(lowed, i.done)
                            nc.scalar.activation(yb[:, i.slot(2)], yb[:, i.slot(2)], ACT.Exp).then_inc(exped, 1)
                        act.wait_ge(turned, i.done)
                        if i.back(2).live:
                            act.wait_ge(rows_made, i.back(2).done)
                        nc.scalar.copy(xt[:, i.slot(2)], xt_ps[:, i.slot(2), 0:din]).then_inc(xt_made, 1)
                    j = i.back(1)
                    if j.live:
                        act.wait_ge(rows_made, j.done)
                        if j.back(2).live:
                            act.wait_ge(l_out[j.slot(2)], j.back(2).turns(2) * 16)
                            act.wait_ge(r_out[j.slot(2)], j.back(2).turns(2) * 16)
                            act.wait_ge(acc_set, j.back(2).done)
                            act.wait_ge(summed, j.back(2).done)
                        nc.scalar.copy(xl[:, j.slot(2), 0:W], xl_ps[:, j.slot(2), 0:W]).then_inc(l_taken, 1)
                        nc.scalar.copy(xr[:, j.slot(2), 0:W], xr_ps[:, j.slot(2), 0:W]).then_inc(r_taken, 1)
                run_steps(act, body, 2, NT, 1)

            @block.gpsimd
            def _(pool):
                def body(i):
                    if layer == 1 and i.live:
                        pool.wait_ge(x_made, i.done)
                        nc.gpsimd.tensor_copy(tile_of(k["xn"], i.s, D), xs[:, i.slot(2)]).then_inc(x_kept, 1)
                    j = i.back(1)
                    if j.live:
                        pool.wait_ge(l_taken, j.done)
                        pool.wait_ge(lin_taken, j.done)
                        pool.wait_ge(xre_made, j.done)
                        nc.gpsimd.tensor_copy(tile_of(k["acc"], j.s, W), xl[:, j.slot(2), 0:W]).then_inc(acc_set, 1)
                        nc.gpsimd.tensor_tensor(own_m[:, j.slot(2)], xl[:, j.slot(2)], xre[:, j.slot(2)],
                                                ALU.add).then_inc(summed, 1)
                run_steps(pool, body, 2, NT, 1)

            @block.vector
            def _(dve):
                if layer == 2:
                    dve.wait_ge(loaded, 32)

                def source(i):
                    if i.back(2).live:
                        dve.wait_ge(turned, i.back(2).done)
                    if layer == 1:
                        if i.back(2).live:
                            dve.wait_ge(x_kept, i.back(2).done)
                        nc.vector.tensor_scalar(xs[:, i.slot(2)], tile_of(k["acc"], i.s, din), k["mv"][:, bass.ds(i.s, 1), 0],
                                                k["rstd"][:, bass.ds(i.s, 1)], ALU.subtract, ALU.mult).then_inc(x_made, 1)
                        return
                    nc.vector.tensor_scalar(ya[:, i.slot(2)], tile_of(k["acc"], i.s, din), k["mv"][:, bass.ds(i.s, 1), 0],
                                            k["rstd"][:, bass.ds(i.s, 1)], ALU.subtract, ALU.mult).then_inc(normed, 1)
                    dve.wait_ge(normed, i.done)
                    nc.vector.tensor_tensor(ya[:, i.slot(2)], ya[:, i.slot(2)], gain[:], ALU.mult).then_inc(gained, 1)
                    dve.wait_ge(gained, i.done)
                    nc.vector.tensor_tensor(ya[:, i.slot(2)], ya[:, i.slot(2)], offset[:], ALU.add).then_inc(offsetted, 1)
                    dve.wait_ge(offsetted, i.done)
                    nc.vector.tensor_scalar(yb[:, i.slot(2)], ya[:, i.slot(2)], 0.0, None, ALU.min).then_inc(lowed, 1)
                    dve.wait_ge(lowed, i.done)
                    nc.vector.tensor_scalar(ya[:, i.slot(2)], ya[:, i.slot(2)], 0.0, -1.0, ALU.max, ALU.add).then_inc(highed, 1)
                    dve.wait_ge(highed, i.done)
                    dve.wait_ge(exped, i.done)
                    nc.vector.tensor_tensor(xs[:, i.slot(2)], ya[:, i.slot(2)], yb[:, i.slot(2)], ALU.add).then_inc(x_made, 1)

                def body(i):
                    if i.live:
                        source(i)
                    j = i.back(1)
                    if j.live:
                        dve.wait_ge(rows_made, j.done)
                        dve.wait_ge(l_taken, j.done)
                        if j.back(2).live:
                            dve.wait_ge(summed, j.back(2).done)
                        nc.vector.tensor_copy(xl[:, j.slot(2), W:], lin_ps[:, j.slot(2), 0:heads])
                        nc.vector.tensor_copy(xr[:, j.slot(2), W:], lin_ps[:, j.slot(2), heads:2 * heads])
                        nc.vector.tensor_tensor(xre[:, j.slot(2), W:], lin_ps[:, j.slot(2), heads:2 * heads], w["ebias"][:, W:],
                                                ALU.add).then_inc(lin_taken, 1)
                        dve.wait_ge(r_taken, j.done)
                        nc.vector.tensor_tensor(xre[:, j.slot(2), 0:W], xr[:, j.slot(2), 0:W], w["ebias"][:, 0:W],
                                                ALU.add).then_inc(xre_made, 1)
                    j = i.back(2)
                    if j.live:
                        dve.wait_ge(summed, j.done)
                        for h in range(heads):
                            cols = slice(h * ch, (h + 1) * ch)
                            last = nc.vector.scalar_tensor_tensor(prod[:, cols], own_m[:, j.slot(2), cols], 0.0,
                                                                  w["att_row"][:, cols], ALU.max, ALU.mult,
                                                                  accum_out=q[:, j.slot(2), h:h + 1])
                        last.then_inc(scored, 1)
                        dve.wait_ge(scored, j.done)
                        nc.vector.tensor_tensor(k["mrun"][:, bass.ds(j.s, 1), 0:heads].rearrange("p t h -> p (t h)"),
                                                q[:, j.slot(2)], own_m[:, j.slot(2), W:], ALU.add).then_inc(m_set, 1)
                run_steps(dve, body, 2, NT, 2)


def attention_steps(nc, k, w, sb, ps, sem, layer, heads, ch):
    W = heads * ch
    K = W // P
    R = W + heads
    RING = 8
    n = f"t{layer}_"
    with ExitStack() as own:
        ix = sb(n + "ix", [P, 2, IRING, 2], I32, own)
        xl = sb(n + "xl", [P, RING, R], F32, own)
        xr = sb(n + "xr", [P, RING, R], F32, own)
        ea = sb(n + "ea", [EROWS, 2, IRING, P], BF16, own)
        dlb = sb(n + "dlb", [P, 2, IRING, P], F32, own)
        relu = sb(n + "relu", [P, 2, W], F32, own)
        px = sb(n + "px", [P, 2, W], F32, own)
        cold = sb(n + "cold", [P, 2, P], BF16, own)
        hot = sb(n + "hot", [P, 2, P], F32, own)
        hot_t = sb(n + "hot_t", [P, 2, P], F32, own)
        linear = sb(n + "linear", [P, 2, heads], F32, own)
        score = sb(n + "score", [P, 2, heads], F32, own)
        top = sb(n + "top", [P, 2, heads], F32, own)
        new_m = sb(n + "new_m", [P, 2, heads], F32, own)
        drop = sb(n + "drop", [P, 4, heads], F32, own)
        gap = sb(n + "gap", [P, 2, heads], F32, own)
        prob = sb(n + "prob", [P, 4, heads], F32, own)
        dnew = sb(n + "dnew", [P, 2, heads], F32, own)
        m_ps = ps(n + "m_ps", [P, 2, 512], own)
        score_ps = ps(n + "score_ps", [P, 512], own)
        wide_ps = ps(n + "wide_ps", [P, 512], own)
        gap_ps = ps(n + "gap_ps", [P, 512], own)
        sum_ps = ps(n + "sum_ps", [P, 2, 512], own)
        den_ps = ps(n + "den_ps", [P, 512], own)

        ix_ready = sem(n + "ix_ready", own)
        xl_in = [sem(n + f"xl_in{i}", own) for i in range(RING)]
        xr_in = [sem(n + f"xr_in{i}", own) for i in range(RING)]
        ea_in = [sem(n + f"ea_in{i}", own) for i in range(2)]
        dlb_in = [sem(n + f"dlb_in{i}", own) for i in range(2)]
        m_made = sem(n + "m_made", own)
        relu_made = sem(n + "relu_made", own)
        dots_made = sem(n + "dots_made", own)
        linear_made = sem(n + "linear_made", own)
        score_made = sem(n + "score_made", own)
        cold_made = sem(n + "cold_made", own)
        hot_made = sem(n + "hot_made", own)
        hot_t_made = sem(n + "hot_t_made", own)
        wide_made = sem(n + "wide_made", own)
        top_made = sem(n + "top_made", own)
        m_new = sem(n + "m_new", own)
        drop_made = sem(n + "drop_made", own)
        m_kept = sem(n + "m_kept", own)
        faded = sem(n + "faded", own)
        spread_made = sem(n + "spread_made", own)
        gap_made = sem(n + "gap_made", own)
        prob_made = sem(n + "prob_made", own)
        px_made = sem(n + "px_made", own)
        sum_made = sem(n + "sum_made", own)
        added = sem(n + "added", own)
        den_faded = sem(n + "den_faded", own)
        den_added = sem(n + "den_added", own)

        with nc.Block() as block:
            @block.sync
            def _(sp):
                def body(i):
                    if i.k % IRING:
                        return
                    half = i.k // IRING % 2
                    j = i.back(IRING + 1)
                    if j.live:
                        sp.wait_ge(m_made, j.done)
                        sp.wait_ge(hot_t_made, j.done)
                        nc.sync.nop(nofuse=True)
                    sp.dma_start(ea[:, half], k["d_ea"][bass.ds(i.s, IRING)].rearrange("s r e -> r s e")).then_inc(ea_in[half], 16)
                    sp.dma_start(dlb[:, half].rearrange("p s e -> p (s e)"),
                                 k["d_dl"].rearrange("(one s) e -> one (s e)", one=1)[:, bass.ds(i.s * P, IRING * P)]
                                 .to_broadcast((P, IRING * P))).then_inc(dlb_in[half], 16)
                run_steps(sp, body, U, STEPS, 0)

            @block.gpsimd
            def _(pool):
                def body(i):
                    half = i.k // IRING % 2
                    if i.k % IRING == 0:
                        if i.back(2 * IRING).live:
                            j = i.back(IRING + 1)
                            pool.wait_ge(xl_in[j.slot(RING)], j.turns(RING) * 16)
                            pool.wait_ge(xr_in[j.slot(RING)], j.turns(RING) * 16)
                        nc.gpsimd.tensor_copy(ix[:, half], k["idx"][:, bass.ds(i.s, IRING), :]).then_inc(ix_ready, 1)
                        pool.wait_ge(ix_ready, i.turns(IRING))
                        nc.gpsimd.nop(nofuse=True)
                    if i.back(RING).live:
                        pool.wait_ge(px_made, i.back(RING).done)
                        pool.wait_ge(linear_made, i.back(RING).done)
                        nc.gpsimd.nop(nofuse=True)
                    for c, (rows, table, landed) in enumerate(((xl, k[f"d_xl{layer}"], xl_in), (xr, k[f"d_xr{layer}"], xr_in))):
                        at = bass.IndirectOffsetOnAxis(ap=ix[:, half, i.k % IRING, c:c + 1], axis=0)
                        nc.gpsimd.indirect_dma_start(out=rows[:, i.slot(RING)], out_offset=None, in_=table,
                                                     in_offset=at).then_inc(landed[i.slot(RING)], 16)
                run_steps(pool, body, U, STEPS, 0)

            @block.tensor
            def _(pe):
                def mix(i, c0, c1):
                    for c in range(c0, c1):
                        cols = slice(c * P, (c + 1) * P)
                        o = m_ps[:, i.slot(2), cols]
                        for r, rows in enumerate((xl, xr)):
                            nc.tensor.matmul(o, rows[:, i.slot(RING), cols], k["ident"][:], is_transpose=True,
                                             start=(r == 0), stop=False, skip_group_check=True)
                        last = nc.tensor.matmul(o, w["we"][:, cols], ea[:, i.k // IRING % 2, i.k % IRING], start=False, stop=True,
                                                skip_group_check=True)
                    return last

                def body(i):
                    j = i.back(3)
                    if j.live:
                        pe.wait_ge(px_made, j.done)
                        pe.wait_ge(hot_made, j.done)
                        if j.back(1).live:
                            pe.wait_ge(den_added, j.back(1).done)
                        if j.back(2).live:
                            pe.wait_ge(added, j.back(2).done)
                        nc.tensor.matmul(den_ps[:, 0:heads], hot[:, j.slot(2)], prob[:, j.slot(4)], start=True, stop=True)
                        nc.tensor.matmul(sum_ps[:, j.slot(2), 0:W], hot[:, j.slot(2)], px[:, j.slot(2)],
                                         start=True, stop=True).then_inc(sum_made, 1)
                    j = i.back(2)
                    if j.live:
                        pe.wait_ge(m_new, j.done)
                        pe.wait_ge(hot_t_made, j.done)
                        if j.back(1).live:
                            pe.wait_ge(gap_made, j.back(1).done)
                        nc.tensor.matmul(gap_ps[:, 0:heads], hot_t[:, j.slot(2)], new_m[:, j.slot(2)],
                                         start=True, stop=True).then_inc(spread_made, 1)
                    j = i.back(1)
                    if j.live:
                        half, col = j.k // IRING % 2, j.k % IRING
                        pe.wait_ge(relu_made, j.done)
                        if j.back(1).live:
                            pe.wait_ge(score_made, j.back(1).done)
                        nc.tensor.matmul(score_ps[:, 0:heads], ea[:, half, col], w["we"][:, W:], start=True, stop=False,
                                         skip_group_check=True)
                        for c in range(K):
                            h = c * P // ch
                            last = nc.tensor.matmul(score_ps[:, h:h + 1], relu[:, j.slot(2), c * P:(c + 1) * P],
                                                    w["att_col"][:, c:c + 1], start=False, stop=(c == K - 1),
                                                    skip_group_check=True)
                        last.then_inc(dots_made, 1)
                    if i.live:
                        pe.wait_ge(xl_in[i.slot(RING)], i.turns(RING) * 16)
                        pe.wait_ge(xr_in[i.slot(RING)], i.turns(RING) * 16)
                        if i.back(2).live:
                            pe.wait_ge(relu_made, i.back(2).done)
                        pe.wait_ge(ea_in[i.k // IRING % 2], i.turns_of(IRING, 2) * 16)
                        mix(i, 0, K // 2)
                    if j.live:
                        pe.wait_ge(score_made, j.done)
                        pe.wait_ge(cold_made, j.done)
                        if j.back(1).live:
                            pe.wait_ge(top_made, j.back(1).done)
                        for h in range(heads):
                            o = wide_ps[:, h * P:(h + 1) * P]
                            nc.tensor.matmul(o, score[:, j.slot(2), h:h + 1].to_broadcast((P, P)), k["ident"][:], is_transpose=True,
                                             start=True, stop=False, skip_group_check=True)
                            last = nc.tensor.matmul(o, cold[:, j.slot(2)], k["bigi"][:], start=False, stop=True,
                                                    skip_group_check=True)
                        last.then_inc(wide_made, 1)
                    if i.live:
                        mix(i, K // 2, K).then_inc(m_made, 1)
                run_steps(pe, body, U, STEPS, 3)

            @block.scalar
            def _(act):
                def body(i):
                    j = i.back(2)
                    if j.live:
                        act.wait_ge(gap_made, j.done)
                        if j.back(4).live:
                            act.wait_ge(sum_made, j.back(4).done)
                        nc.scalar.activation(prob[:, j.slot(4)], gap[:, j.slot(2)], ACT.Exp,
                                             bias=k["off"][:, bass.ds(j.s, 1)]).then_inc(prob_made, 1)
                        act.wait_ge(prob_made, j.done)
                        if j.back(2).live:
                            act.wait_ge(sum_made, j.back(2).done)
                        for h in range(heads):
                            cols = slice(h * ch, (h + 1) * ch)
                            last = nc.scalar.activation(px[:, j.slot(2), cols], xl[:, j.slot(RING), cols], ACT.Copy,
                                                        scale=prob[:, j.slot(4), h:h + 1])
                        last.then_inc(px_made, 1)
                    if i.live:
                        act.wait_ge(m_made, i.done)
                        if i.back(2).live:
                            act.wait_ge(dots_made, i.back(2).done)
                        nc.scalar.activation(relu[:, i.slot(2)], m_ps[:, i.slot(2), 0:W], ACT.Relu).then_inc(relu_made, 1)
                    j = i.back(1)
                    if j.live:
                        act.wait_ge(drop_made, j.done)
                        nc.scalar.activation(drop[:, j.slot(4)], drop[:, j.slot(4)], ACT.Exp).then_inc(faded, 1)
                run_steps(act, body, U, STEPS, 2)

            @block.vector
            def _(dve):
                r1 = [dve.alloc_register(f"{n}top{i}") for i in range(U)]
                r3 = [dve.alloc_register(f"{n}sum{i}") for i in range(U)]
                t1, t3 = [None] * U, [None] * U

                def head(it):
                    dve.load(r1, k["tile_i"][0:1, bass.ds(it * U + (U - 1), U)])
                    dve.load(r3, k["tile_i"][0:1, bass.ds(it * U + (U - 3), U)])
                    for i in range(U):
                        t1[i] = dve.snap(r1[i], min_val=0, max_val=NT - 1)
                        t3[i] = dve.snap(r3[i], min_val=0, max_val=NT - 1)

                def body(i):
                    j = i.back(2)
                    if j.live:
                        dve.wait_ge(spread_made, j.done)
                        if j.back(2).live:
                            dve.wait_ge(prob_made, j.back(2).done)
                        nc.vector.tensor_tensor(gap[:, j.slot(2)], score[:, j.slot(2)], gap_ps[:, 0:heads],
                                                ALU.subtract).then_inc(gap_made, 1)
                    j = i.back(1)
                    if j.live:
                        dve.wait_ge(dots_made, j.done)
                        dve.wait_ge(linear_made, j.done)
                        if j.back(2).live:
                            dve.wait_ge(gap_made, j.back(2).done)
                        nc.vector.tensor_tensor(score[:, j.slot(2)], score_ps[:, 0:heads], linear[:, j.slot(2)],
                                                ALU.add).then_inc(score_made, 1)
                    if i.live:
                        dve.wait_ge(xl_in[i.slot(RING)], i.turns(RING) * 16)
                        dve.wait_ge(xr_in[i.slot(RING)], i.turns(RING) * 16)
                        if i.back(2).live:
                            dve.wait_ge(wide_made, i.back(2).done)
                        nc.vector.tensor_tensor(linear[:, i.slot(2)], xl[:, i.slot(RING), W:], xr[:, i.slot(RING), W:],
                                                ALU.add).then_inc(linear_made, 1)
                        nc.vector.tensor_scalar(cold[:, i.slot(2)], k["node_row"][:], k["dl"][:, bass.ds(i.s, 1)], -1.0,
                                                ALU.is_equal, ALU.add).then_inc(cold_made, 1)
                    j = i.back(1)
                    if j.live:
                        half, col = j.k // IRING % 2, j.k % IRING
                        dve.wait_ge(dlb_in[half], j.turns_of(IRING, 2) * 16)
                        if j.back(2).live:
                            dve.wait_ge(spread_made, j.back(2).done)
                        nc.vector.tensor_scalar(hot_t[:, j.slot(2)], dlb[:, half, col], k["part"][:, 0:1], None,
                                                ALU.is_equal).then_inc(hot_t_made, 1)
                    j = i.back(2)
                    if j.live:
                        if j.back(2).live:
                            dve.wait_ge(sum_made, j.back(2).done)
                        nc.vector.tensor_scalar(hot[:, j.slot(2)], k["node_row"][:], k["dl"][:, bass.ds(j.s, 1)], None,
                                                ALU.is_equal).then_inc(hot_made, 1)
                    j = i.back(3)
                    if j.live:
                        dve.wait_ge(sum_made, j.done)
                        dve.wait_ge(faded, j.done)
                        if j.back(1).live:
                            dve.wait_ge(added, j.back(1).done)
                            dve.wait_ge(den_added, j.back(1).done)
                        den = k["den"][:, bass.ds(t3[i.k], 1), 0:heads].rearrange("p t h -> p (t h)")
                        nc.vector.tensor_tensor(dnew[:, j.slot(2)], den, drop[:, j.slot(4)], ALU.mult).then_inc(den_faded, 1)
                        for h in range(heads):
                            cols = slice(h * ch, (h + 1) * ch)
                            row = k["acc"][:, bass.ds(t3[i.k], 1), cols].rearrange("p t f -> p (t f)")
                            last = nc.vector.scalar_tensor_tensor(row, row, drop[:, j.slot(4), h:h + 1],
                                                                  sum_ps[:, j.slot(2), cols], ALU.mult, ALU.add)
                        last.then_inc(added, 1)
                        dve.wait_ge(den_faded, j.done)
                        nc.vector.tensor_tensor(den, dnew[:, j.slot(2)], den_ps[:, 0:heads], ALU.add).then_inc(den_added, 1)
                    j = i.back(1)
                    if j.live:
                        dve.wait_ge(wide_made, j.done)
                        nc.vector.tensor_reduce(top[:, j.slot(2)], wide_ps[:, 0:heads * P].rearrange("p (h e) -> p h e", e=P),
                                                AX.X, ALU.max).then_inc(top_made, 1)
                        dve.wait_ge(top_made, j.done)
                        if j.back(1).live:
                            dve.wait_ge(m_kept, j.back(1).done)
                        if j.back(2).live:
                            dve.wait_ge(spread_made, j.back(2).done)
                        m = k["mrun"][:, bass.ds(t1[i.k], 1), 0:heads].rearrange("p t h -> p (t h)")
                        nc.vector.tensor_tensor(new_m[:, j.slot(2)], m, top[:, j.slot(2)], ALU.max).then_inc(m_new, 1)
                        dve.wait_ge(m_new, j.done)
                        nc.vector.tensor_tensor(drop[:, j.slot(4)], m, new_m[:, j.slot(2)], ALU.subtract).then_inc(drop_made, 1)
                        dve.wait_ge(drop_made, j.done)
                        nc.vector.tensor_tensor(m, m, top[:, j.slot(2)], ALU.max).then_inc(m_kept, 1)
                run_steps(dve, body, U, STEPS, 3, head)


def last_nodes(nc, a, k, sb, ps, sem, out):
    with ExitStack() as own:
        bias = sb("ln_bias", [P, D], F32, own)
        gain = sb("ln_gain", [P, D], F32, own)
        offset = sb("ln_offset", [P, D], F32, own)
        y = sb("ln_y", [P, 2, D], F32, own)
        yo = sb("ln_yo", [P, 2, D], F32, own)
        loaded = sem("ln_loaded", own)
        divided = sem("ln_divided", own)
        normed = sem("ln_normed", own)
        scaled = sem("ln_scaled", own)
        offsetted = sem("ln_offsetted", own)
        doubled = sem("ln_doubled", own)
        stats = sem("ln_stats", own)
        dve_own = sem("ln_own", own)
        to_root = sem("ln_to_root", own)
        rooted = sem("ln_rooted", own)
        made = sem("ln_made", own)
        stored = [sem(f"ln_stored{i}", own) for i in range(2)]
        FULL = N // P
        with nc.Block() as block:
            @block.sync
            def _(sp):
                sp.dma_start(bias[:], a["cb2"].to_broadcast((P, D))).then_inc(loaded, 16)
                sp.dma_start(gain[:], a["g2"].to_broadcast((P, D))).then_inc(loaded, 16)
                sp.dma_start(offset[:], a["be2"].to_broadcast((P, D))).then_inc(loaded, 16)

                def body(i):
                    sp.wait_ge(made, i.done)
                    sp.dma_start(out[bass.ds(i.s * P, P), :], yo[:, i.slot(2)]).then_inc(stored[i.slot(2)], 16)
                run_steps(sp, body, 2, FULL, 0)
                sp.wait_ge(made, FULL + 1)
                sp.dma_start(out[FULL * P:N, :], yo[0:N - FULL * P, 0]).then_inc(stored[0], 16)
                sp.wait_ge(stored[0], 16 * (FULL // 2 + 1))
                sp.wait_ge(stored[1], 16 * (FULL // 2))

            @block.scalar
            def _(act):
                for c in range(2):
                    root(k, nc, act, rooted, to_root, c + 1)

            @block.vector
            def _(dve):
                link = Chain(dve, dve_own)
                den = k["den"][:, :, 0]
                rden = k["rden"][:, 0:NT]
                link(nc.vector.tensor_scalar(den, den, 1e-16, None, ALU.add))
                link(nc.vector.reciprocal(rden, den))
                dve.wait_ge(loaded, 48)

                def body(i):
                    if i.live:
                        row = tile_of(k["acc"], i.s, D)
                        nc.vector.scalar_tensor_tensor(row, row, k["rden"][:, bass.ds(i.s, 1)], bias[:],
                                                       ALU.mult, ALU.add).then_inc(divided, 1)
                    j = i.back(1)
                    if j.live:
                        dve.wait_ge(divided, j.done)
                        nc.vector.bn_stats(tile_of(k["st"], j.s, 6), tile_of(k["acc"], j.s, D)).then_inc(stats, 1)
                run_steps(dve, body, 2, NT, 1)
                dve.wait_ge(stats, NT)
                spread(k, nc, dve, rooted, to_root, link, 1)

                def body(i):
                    if i.live:
                        if i.back(2).live:
                            dve.wait_ge(doubled, i.back(2).done)
                        nc.vector.tensor_scalar(y[:, i.slot(2)], tile_of(k["acc"], i.s, D), k["mv"][:, bass.ds(i.s, 1), 0],
                                                k["rstd"][:, bass.ds(i.s, 1)], ALU.subtract, ALU.mult).then_inc(normed, 1)
                    j = i.back(1)
                    if j.live:
                        dve.wait_ge(normed, j.done)
                        nc.vector.tensor_tensor(y[:, j.slot(2)], y[:, j.slot(2)], gain[:], ALU.mult).then_inc(scaled, 1)
                        dve.wait_ge(scaled, j.done)
                        nc.vector.tensor_tensor(y[:, j.slot(2)], y[:, j.slot(2)], offset[:], ALU.add).then_inc(offsetted, 1)
                        dve.wait_ge(offsetted, j.done)
                        nc.vector.scalar_tensor_tensor(tile_of(k["acc"], j.s, D), tile_of(k["xn"], j.s, D), 2.0,
                                                       y[:, j.slot(2)], ALU.mult, ALU.add).then_inc(doubled, 1)
                    j = i.back(2)
                    if j.live:
                        dve.wait_ge(doubled, j.done)
                        nc.vector.bn_stats(tile_of(k["st"], j.s, 6), tile_of(k["acc"], j.s, D)).then_inc(stats, 1)
                run_steps(dve, body, 2, NT, 2)
                dve.wait_ge(stats, 2 * NT)
                spread(k, nc, dve, rooted, to_root, link, 2)

                def body(i):
                    if i.back(2).live:
                        dve.wait_ge(stored[i.slot(2)], i.back(2).turns(2) * 16)
                    nc.vector.tensor_scalar(yo[:, i.slot(2)], tile_of(k["acc"], i.s, D), k["mv"][:, bass.ds(i.s, 1), 0],
                                            k["rstd"][:, bass.ds(i.s, 1)], ALU.subtract, ALU.mult).then_inc(made, 1)
                run_steps(dve, body, 2, FULL, 0)
                body(Step(FULL // 2, 0, 2, FULL + 2))


_WEIGHTS = {
    "W1": "L0_gnn_W1", "b1": "L0_gnn_b1", "W2": "L0_gnn_W2", "b2": "L0_gnn_b2", "Wg": "L0_gnn_Wg", "bg": "L0_gnn_bg",
    "gamma": "L0_gnn_gamma", "beta": "L0_gnn_beta", "Wl1": "L1_gnn_Wl1", "Wr1": "L1_gnn_Wr1", "We1": "L1_gnn_We1",
    "att1": "L1_gnn_att1", "cb1": "L1_gnn_b1", "g1": "L1_gnn_g1", "be1": "L1_gnn_be1", "Wl2": "L1_gnn_Wl2",
    "Wr2": "L1_gnn_Wr2", "We2": "L1_gnn_We2", "att2": "L1_gnn_att2", "cb2": "L1_gnn_b2", "g2": "L1_gnn_g2",
    "be2": "L1_gnn_be2",
}
BEYOND = 1 << 20


def laid_out(inputs):
    x = np.asarray(inputs["x"])
    edges = EP - E
    arrays = {
        "x": np.pad(x, ((0, NP - N), (0, 0))),
        "src": np.pad(np.asarray(inputs["src"]), (0, edges)).reshape(EP, 1),
        "dst": np.pad(np.asarray(inputs["dst"]), (0, edges), constant_values=BEYOND).reshape(EP, 1),
        "ea4": np.pad(np.asarray(inputs["edge_attr_4"]), ((0, edges), (0, 0))),
        "ea64t": np.ascontiguousarray(np.pad(np.asarray(inputs["edge_attr_64"]), ((0, edges), (0, 0))).T),
    }
    arrays["xt"] = np.ascontiguousarray(arrays["x"].T)
    for short, name in _WEIGHTS.items():
        w = np.ascontiguousarray(inputs[name])
        arrays[short] = w.reshape(1, -1) if w.ndim == 1 or short.startswith("att") else w
    return arrays


def kernel(**inputs):
    import concourse.bacc as bacc
    from concourse.bass_utils import run_bass_kernel_spmd

    nc = bacc.Bacc("TRN2", target_bir_lowering=False, num_devices=1)
    arrays = laid_out(inputs)
    a = {n: nc.dram_tensor(f"in_{n}", v.shape, mybir.dt.from_np(v.dtype), kind="ExternalInput").ap() for n, v in arrays.items()}
    out = nc.dram_tensor("out_x", (N, D), F32, kind="ExternalOutput").ap()
    gnn(nc, a, out)
    r = run_bass_kernel_spmd(nc, [{f"in_{n}": v for n, v in arrays.items()}], core_ids=[0])
    return r.results[0]["out_x"]
```

```python
from contextlib import ExitStack

import numpy as np

import concourse.bass as bass
from concourse import mybir
from concourse.alu_op_type import AluOpType as ALU

ACT = mybir.ActivationFunctionType
AX = mybir.AxisListType
F32 = mybir.dt.float32
BF16 = mybir.dt.bfloat16
I32 = mybir.dt.int32

P = 128
N, E, D = 3125, 50000, 256
DE, ED = 64, 4
HEADS, HID = 4, 128
NT = 26
NP = NT * P
U = 8
BASE = -(-E // P) + -(-N // P) - 1
STEPS = -(-BASE // U) * U
SW = -(-STEPS // P)
ST = SW * P
RMAX = -(-E // P) * P
DC = RMAX // P + 2
EP = DC * P
IRING = 4
BIG = 1e30
PARTS = 3
EROWS = PARTS * PARTS * ED
SLOPE = 0.2
EPS = 1e-5


class Step:

    def __init__(self, it, k, unroll, count):
        self.it, self.k, self.unroll, self.count = it, k, unroll, count

    def back(self, n):
        return Step(self.it, self.k - n, self.unroll, self.count)

    @property
    def live(self):
        return not isinstance(self.it, int) or 0 <= self.it * self.unroll + self.k < self.count

    @property
    def s(self):
        return self.it * self.unroll + self.k

    @property
    def done(self):
        return self.it * self.unroll + (self.k + 1)

    def slot(self, ring):
        return self.k % ring

    def turns(self, ring):
        return self.it * (self.unroll // ring) + (self.k // ring + 1)

    def turns_of(self, group, ring):
        return self.it * (self.unroll // (group * ring)) + (self.k // (group * ring) + 1)


def run_steps(eng, body, unroll, count, lag, head=None):
    turns = count // unroll
    if head:
        head(0)
    for k in range(unroll):
        body(Step(0, k, unroll, count))
    with eng.Fori(1, turns) as it:
        if head:
            head(it)
        for k in range(unroll):
            body(Step(it, k, unroll, count))
    if head and lag:
        head(turns)
    for k in range(lag):
        body(Step(turns, k, unroll, count))


def gnn(nc, a, out):
    with ExitStack() as whole:
        def sb(name, shape, dt=F32, scope=whole):
            return scope.enter_context(nc.sbuf_tensor(name, shape, dt))

        banks = whole.enter_context(nc.psum_tensor("banks", [P, 8, 512], F32))
        taken = []

        def ps(name, shape, scope):
            count = shape[1] if len(shape) == 3 else 1
            n = len(taken)
            assert n + count <= 8, name
            taken.extend([name] * count)
            scope.callback(taken.__delitem__, slice(n, n + count))
            return banks[:, n:n + count] if len(shape) == 3 else banks[:, n]

        def sem(name, scope):
            if scope not in held:
                held[scope] = []
                scope.callback(clear, scope)
            held[scope].append(nc.alloc_semaphore(name))
            return held[scope][-1]

        held = {}

        def clear(scope):
            nc.clear_and_free_semaphores(held.pop(scope))
            nc.all_engine_barrier()

        k = {"in": a}
        k["acc"] = sb("acc", [P, NT, 512])
        k["xn"] = sb("xn", [P, NT, D])
        k["low"] = sb("low", [P, NT, HEADS])
        k["den"] = sb("den", [P, NT, HEADS])
        k["ident"] = sb("ident", [P, P])
        k["bigi"] = sb("bigi", [P, P], BF16)
        k["node_row"] = sb("node_row", [P, P])
        k["part"] = sb("part", [P, 1])
        k["dl"] = sb("dl", [P, ST])
        k["idx"] = sb("idx", [P, ST, 2], I32)
        k["row_i"] = sb("row_i", [1, ST], I32)
        k["tile_i"] = sb("tile_i", [1, U + ST], I32)
        k["w1e"] = sb("w1e", [DE, D])
        k["wge"] = sb("wge", [DE, D])
        k["w2"] = sb("w2", [P, 2, D])
        k["b2s"] = sb("b2s", [PARTS, D], BF16)
        k["ones3"] = sb("ones3", [PARTS, P], BF16)
        k["emean"] = sb("emean", [ED, P])
        k["mv"] = sb("mv", [P, NT, 2])
        k["st"] = sb("st", [P, NT, 6])
        k["rstd"] = sb("rstd", [P, NT])
        k["rden"] = sb("rden", [P, NT * HEADS])
        k["sel"] = sb("sel", [P, 2 * PARTS])
        k["d_row"] = nc.dram_tensor("d_row", (ST, 1), I32, kind="Internal").ap()
        k["d_tile"] = nc.dram_tensor("d_tile", (ST, 1), I32, kind="Internal").ap()
        k["d_ea"] = nc.dram_tensor("d_ea", (ST, EROWS, P), BF16, kind="Internal").ap()
        k["d_xw"] = nc.dram_tensor("d_xw", (NP, 2 * D), F32, kind="Internal").ap()
        for c, w in ((1, HEADS * HID), (2, D)):
            for side in "lr":
                k[f"d_x{side}{c}"] = nc.dram_tensor(f"d_x{side}{c}", (NP, w), F32, kind="Internal").ap()

        setup(nc, a, k, sb, ps, sem)
        with ExitStack() as scope:
            gated_steps(nc, a, k, sb, ps, sem, scope)
        with ExitStack() as scope:
            w = attention_weights(nc, a, k, sb, ps, sem, scope, 1, D, HEADS, HID)
            gated_nodes(nc, a, k, sb, ps, sem)
            project(nc, k, w, sb, ps, sem, 1, D, HEADS, HID)
            attention_steps(nc, k, w, sb, ps, sem, 1, HEADS, HID)
        with ExitStack() as scope:
            w = attention_weights(nc, a, k, sb, ps, sem, scope, 2, HEADS * HID, 1, D)
            attended_nodes(nc, a, k, sb, ps, sem)
            project(nc, k, w, sb, ps, sem, 2, HEADS * HID, 1, D)
            attention_steps(nc, k, w, sb, ps, sem, 2, 1, D)
        with ExitStack() as scope:
            last_nodes(nc, a, k, sb, ps, sem, out)


class Chain:

    def __init__(self, eng, semaphore):
        self.eng, self.semaphore, self.n = eng, semaphore, 0

    def __call__(self, instruction):
        self.n += 1
        instruction.then_inc(self.semaphore, 1)
        self.eng.wait_ge(self.semaphore, self.n)


def split(link, nc, src, parts, rest):
    link(nc.vector.tensor_copy(parts[0], src))
    link(nc.vector.tensor_tensor(rest, src, parts[0], ALU.subtract))
    link(nc.vector.tensor_copy(parts[1], rest))
    link(nc.vector.tensor_tensor(rest, rest, parts[1], ALU.subtract))
    link(nc.vector.tensor_copy(parts[2], rest))


def pick(link, nc, dst, parts, masks, n):
    for i in range(PARTS):
        link(nc.vector.tensor_scalar(parts[i], parts[i], masks[0:n, i:i + 1], None, ALU.mult))
    link(nc.vector.tensor_tensor(parts[0], parts[0], parts[1], ALU.add))
    link(nc.vector.tensor_tensor(dst, parts[0], parts[2], ALU.add))


def setup(nc, a, k, sb, ps, sem):
    with ExitStack() as scope:
        def tmp(name, shape, dt=F32):
            return sb("s_" + name, shape, dt, scope)

        wa = tmp("wa", [P, 2, 2 * D])
        ba = tmp("ba", [P, 2 * D])
        beta = tmp("beta", [P, D])
        xt = tmp("xt", [P, 2, 2, P])
        xws = tmp("xws", [P, 2, 2 * D])
        dst_i = tmp("dst_i", [P, DC], I32)
        dst_f = tmp("dst_f", [P, DC])
        below = tmp("below", [P, DC])
        cnt = tmp("cnt", [P, NT])
        ea = tmp("ea", [P, DC, ED])
        easum = tmp("easum", [P, ED])
        ones = tmp("ones", [P, P])
        iot_i = tmp("iot_i", [P, P], I32)
        par_i = tmp("par_i", [P, 1], I32)
        stp_i = tmp("stp_i", [P, SW], I32)
        stp = tmp("stp", [P, SW])
        first = tmp("first", [P, NT + 1])
        need = tmp("need", [P, NT])
        need_i = tmp("need_i", [P, NT], I32)
        wins_i = tmp("wins_i", [P, NT], I32)
        sa = tmp("sa", [P, 16 + NT])
        sbb = tmp("sbb", [P, 16 + NT])
        uu = tmp("uu", [P, 1 + NT])
        dd = tmp("dd", [P, NT])
        ge = tmp("ge", [P, NT])
        gd = tmp("gd", [P, NT])
        tcol = tmp("tcol", [P, SW])
        rcol = tmp("rcol", [P, SW])
        toff = tmp("toff", [P, SW])
        rcol_i = tmp("rcol_i", [P, SW], I32)
        tcol_i = tmp("tcol_i", [P, SW], I32)
        dwin = tmp("dwin", [P, SW, P], I32)
        swin = tmp("swin", [P, SW, P], I32)
        ewin = tmp("ewin", [P, SW, P * ED])
        dwf = tmp("dwf", [P, SW, P])
        swf = tmp("swf", [P, SW, P])
        dcl = tmp("dcl", [P, SW, P])
        dlw = tmp("dlw", [P, SW, P])
        eparts = tmp("eparts", [P, SW, PARTS, ED * P], BF16)
        erest = tmp("erest", [P, ED * P])
        b2r = tmp("b2r", [PARTS, D])
        b2p = tmp("b2p", [PARTS, PARTS, D], BF16)
        b2q = tmp("b2q", [PARTS, D])

        xw_ps = ps("xw_ps", [P, 2, 512], scope)
        cnt_ps = ps("cnt_ps", [P, 512], scope)
        tr_ps = ps("tr_ps", [P, 3, 512], scope)

        loaded_dst = sem("loaded_dst", scope)
        loaded = sem("loaded", scope)
        loaded_w = sem("loaded_w", scope)
        xt_in = [sem(f"xt_in{i}", scope) for i in range(2)]
        xw_made = sem("xw_made", scope)
        xw_taken = sem("xw_taken", scope)
        xw_out = [sem(f"xw_out{i}", scope) for i in range(2)]
        consts = sem("consts", scope)
        pool_own = sem("pool_own", scope)
        counted = sem("counted", scope)
        summed = sem("summed", scope)
        rows_known = sem("rows_known", scope)
        table_out = sem("table_out", scope)
        row_out = sem("row_out", scope)
        row_in = sem("row_in", scope)
        win_in = sem("win_in", scope)
        win_f = sem("win_f", scope)
        turned = sem("turned", scope)
        esplit = sem("esplit", scope)
        zeroed = sem("zeroed", scope)
        dve_own = sem("dve_own", scope)
        xb = sem("xb", scope)

        with nc.Block() as block:
            @block.sync
            def _(sp):
                sp.dma_start(dst_i[:], a["dst"].rearrange("(p c) one -> p (c one)", p=P)).then_inc(loaded_dst, 16)
                for c in range(2):
                    sp.dma_start(wa[:, c, 0:D], a["W1"][c * P:(c + 1) * P, :]).then_inc(loaded_w, 16)
                    sp.dma_start(wa[:, c, D:], a["Wg"][c * P:(c + 1) * P, :]).then_inc(loaded_w, 16)
                sp.dma_start(ba[:, 0:D], a["b1"].to_broadcast((P, D))).then_inc(loaded_w, 16)
                sp.dma_start(ba[:, D:], a["bg"].to_broadcast((P, D))).then_inc(loaded_w, 16)

                def load_xt(i):
                    if i.back(2).live:
                        sp.wait_ge(xw_made, i.back(2).done)
                    sp.dma_start(xt[:, i.slot(2)], a["xt"].rearrange("(c p) n -> p c n", p=P)[
                        :, :, bass.ds(i.s * P, P)]).then_inc(xt_in[i.slot(2)], 16)

                def body(i):
                    if i.live:
                        load_xt(i)
                    j = i.back(2)
                    if j.live:
                        sp.wait_ge(xw_taken, j.done)
                        sp.dma_start(k["d_xw"][bass.ds(j.s * P, P), :], xws[:, j.slot(2)]).then_inc(xw_out[j.slot(2)], 16)
                run_steps(sp, body, 2, NT, 2)
                for i in range(2):
                    sp.wait_ge(xw_out[i], 16 * (NT // 2))

            @block.scalar
            def _(act):
                act.dma_start(ea[:], a["ea4"].rearrange("(p c) k -> p c k", p=P)).then_inc(loaded, 16)
                act.dma_start(beta[:], a["beta"].to_broadcast((P, D))).then_inc(loaded, 16)
                act.dma_start(k["xn"][:], a["x"].rearrange("(t p) f -> p t f", p=P)).then_inc(loaded, 16)
                act.dma_start(k["acc"][:, :, 0:D], a["x"].rearrange("(t p) f -> p t f", p=P)).then_inc(loaded, 16)
                act.dma_start(k["w1e"][:], a["W1"][D:D + DE, :]).then_inc(loaded, 16)
                act.dma_start(k["wge"][:], a["Wg"][D:D + DE, :]).then_inc(loaded, 16)
                act.dma_start(k["w2"][:], a["W2"].rearrange("(c p) f -> p c f", p=P)).then_inc(loaded, 16)
                act.dma_start(b2r[:], a["b2"].to_broadcast((PARTS, D))).then_inc(loaded, 16)
                act.wait_ge(rows_known, 2)
                with nc.allow_non_contiguous_dma(reason="a number a step"):
                    act.dma_start(k["d_row"].rearrange("(j p) one -> p (j one)", p=P), rcol_i[:]).then_inc(row_out, 16)
                    act.dma_start(k["d_tile"].rearrange("(j p) one -> p (j one)", p=P), tcol_i[:]).then_inc(row_out, 16)
                act.wait_ge(row_out, 32)
                act.dma_start(k["row_i"][:], k["d_row"].rearrange("s one -> one s")).then_inc(row_in, 16)
                act.wait_ge(zeroed, 1)
                act.dma_start(k["tile_i"][0:1, U:], k["d_tile"].rearrange("s one -> one s")).then_inc(row_in, 16)
                for j in range(SW):
                    act.wait_ge(esplit, j + 1)
                    for i in range(PARTS):
                        act.dma_start(
                            k["d_ea"][j * P:(j + 1) * P, i * PARTS * ED:(i + 1) * PARTS * ED, :].rearrange("s r e -> s (r e)"),
                            eparts[:, j].rearrange("p a b -> p (a b)")).then_inc(table_out, 16)
                act.wait_ge(row_in, 32)
                act.wait_ge(table_out, 16 * SW * PARTS)
                act.wait_ge(loaded, 16 * 8)

            @block.gpsimd
            def _(pool):
                nc.gpsimd.iota(iot_i[:], [[1, P]], base=0, channel_multiplier=0)
                nc.gpsimd.iota(par_i[:], [[0, 1]], base=0, channel_multiplier=1)
                nc.gpsimd.iota(stp_i[:], [[P, SW]], base=0, channel_multiplier=1)
                nc.gpsimd.memset(ones[:], 1.0)
                nc.gpsimd.memset(k["den"][:], 1.0)
                nc.gpsimd.memset(k["ident"][:], 0.0)
                nc.gpsimd.memset(k["bigi"][:], 0.0).then_inc(pool_own, 1)
                pool.wait_ge(pool_own, 1)
                nc.gpsimd.affine_select(out=k["ident"][:], in_=k["ident"][:], compare_op=ALU.not_equal, fill=1.0,
                                        base=0, pattern=[[-1, P]], channel_multiplier=1)
                nc.gpsimd.affine_select(out=k["bigi"][:], in_=k["bigi"][:], compare_op=ALU.not_equal, fill=BIG,
                                        base=0, pattern=[[-1, P]], channel_multiplier=1).then_inc(consts, 1)
                pool.wait_ge(rows_known, 1)
                for j in range(SW):
                    at = bass.IndirectOffsetOnAxis(ap=rcol_i[:, j:j + 1], axis=0)
                    nc.gpsimd.indirect_dma_start(out=dwin[:, j], out_offset=None, in_=a["dst"], in_offset=at).then_inc(win_in, 16)
                    nc.gpsimd.indirect_dma_start(out=swin[:, j], out_offset=None, in_=a["src"], in_offset=at).then_inc(win_in, 16)
                    nc.gpsimd.indirect_dma_start(out=ewin[:, j], out_offset=None, in_=a["ea4"], in_offset=at).then_inc(win_in, 16)
                pool.wait_ge(loaded, 16 * 8)
                for t in range(NT):
                    last = nc.gpsimd.tensor_tensor(k["xn"][:, t], k["xn"][:, t], beta[:], ALU.add)
                last.then_inc(xb, 1)

            @block.tensor
            def _(pe):
                pe.wait_ge(loaded_w, 16 * 6)

                def body(i):
                    pe.wait_ge(xt_in[i.slot(2)], i.turns(2) * 16)
                    if i.back(2).live:
                        pe.wait_ge(xw_taken, i.back(2).done)
                    for c in range(2):
                        last = nc.tensor.matmul(xw_ps[:, i.slot(2)], xt[:, i.slot(2), c], wa[:, c], start=(c == 0), stop=(c == 1))
                    last.then_inc(xw_made, 1)
                run_steps(pe, body, 2, NT, 0)
                pe.wait_ge(consts, 1)
                pe.wait_ge(counted, 1)
                nc.tensor.matmul(cnt_ps[:, 0:NT], ones[:], cnt[:], start=True, stop=True)
                nc.tensor.matmul(cnt_ps[0:ED, P:2 * P], easum[:], ones[:], start=True, stop=True).then_inc(summed, 1)
                pe.wait_ge(win_f, 1)
                for n, src in enumerate((dlw, swf, dcl)):
                    for j in range(SW):
                        last = nc.tensor.transpose(tr_ps[:, n, j * P:(j + 1) * P], src[:, j], k["ident"][:])
                last.then_inc(turned, 1)

            @block.vector
            def _(dve):
                link = Chain(dve, dve_own)
                nc.vector.memset(k["tile_i"][:], 0).then_inc(zeroed, 1)
                nc.vector.memset(k["ones3"][:], 1.0)
                nc.vector.memset(sa[:], 0.0)
                nc.vector.memset(uu[:], 0.0)
                link(nc.vector.memset(sbb[:], 0.0))
                dve.wait_ge(loaded_dst, 16)
                link(nc.vector.tensor_copy(dst_f[:], dst_i[:]))
                for t in range(NT):
                    last = nc.vector.tensor_scalar(below[:], dst_f[:], float(t * P), None, ALU.is_lt, ALU.add,
                                                   accum_out=cnt[:, t:t + 1])
                    link(last)
                dve.wait_ge(loaded, 16 * 8)
                nc.vector.tensor_reduce(easum[:], ea[:].rearrange("p c k -> p k c"), AX.X, ALU.add).then_inc(counted, 1)

                dve.wait_ge(consts, 1)
                link(nc.vector.tensor_copy(k["node_row"][:], iot_i[:]))
                link(nc.vector.tensor_copy(k["part"][:], par_i[:]))
                link(nc.vector.tensor_copy(stp[:], stp_i[:]))
                for g, size in ((0, 1), (PARTS, PARTS * ED)):
                    for i in range(PARTS):
                        m = k["sel"][:, g + i:g + i + 1]
                        link(nc.vector.tensor_scalar(m, k["part"][:], float(i * size), None, ALU.is_ge))
                        link(nc.vector.tensor_scalar(below[:, 0:1], k["part"][:], float((i + 1) * size), None, ALU.is_lt))
                        link(nc.vector.tensor_tensor(m, m, below[:, 0:1], ALU.mult))
                split(link, nc, b2r[:], [b2p[:, i] for i in range(PARTS)], b2q[:])
                pick(link, nc, k["b2s"][:], [b2p[:, i] for i in range(PARTS)], k["sel"], PARTS)

                def take(i):
                    dve.wait_ge(xw_made, i.done)
                    if i.back(2).live:
                        dve.wait_ge(xw_out[i.slot(2)], i.back(2).turns(2) * 16)
                    nc.vector.tensor_tensor(xws[:, i.slot(2)], xw_ps[:, i.slot(2)], ba[:], ALU.add).then_inc(xw_taken, 1)
                dve.wait_ge(loaded_w, 16 * 6)
                run_steps(dve, take, 2, NT, 0)

                dve.wait_ge(summed, 1)
                link(nc.vector.tensor_copy(first[:, 0:NT], cnt_ps[:, 0:NT]))
                link(nc.vector.memset(first[:, NT:], float(E)))
                link(nc.vector.tensor_scalar(k["emean"][:], cnt_ps[0:ED, P:2 * P], 1.0 / E, None, ALU.mult))
                link(nc.vector.tensor_tensor(need[:], first[:, 1:], first[:, 0:NT], ALU.subtract))
                link(nc.vector.tensor_scalar(need_i[:], need[:], float(P - 1), None, ALU.add))
                link(nc.vector.tensor_scalar(wins_i[:], need_i[:], P.bit_length() - 1, None, ALU.arith_shift_right))
                link(nc.vector.tensor_copy(sa[:, 17:], wins_i[:, 0:NT - 1]))
                cur, other = sa, sbb
                for d in (1, 2, 4, 8, 16):
                    link(nc.vector.tensor_tensor(other[:, 16:], cur[:, 16:], cur[:, 16 - d:16 + NT - d], ALU.add))
                    cur, other = other, cur
                starts = cur[:, 16:]
                link(nc.vector.tensor_scalar(uu[:, 1:], starts, -float(P), None, ALU.mult))
                link(nc.vector.tensor_tensor(uu[:, 1:], uu[:, 1:], first[:, 0:NT], ALU.add))
                link(nc.vector.tensor_tensor(dd[:], uu[:, 1:], uu[:, 0:NT], ALU.subtract))
                for j in range(SW):
                    link(nc.vector.tensor_scalar(ge[:], starts, stp[:, j:j + 1], None, ALU.is_le, ALU.add,
                                                 accum_out=tcol[:, j:j + 1]))
                    link(nc.vector.tensor_tensor_reduce(gd[:], ge[:], dd[:], 1.0, 0.0, ALU.mult, ALU.add,
                                                        rcol[:, j:j + 1]))
                link(nc.vector.scalar_tensor_tensor(rcol[:], stp[:], float(P), rcol[:], ALU.mult, ALU.add))
                nc.vector.tensor_scalar(rcol_i[:], rcol[:], float(RMAX), None, ALU.min).then_inc(rows_known, 1)
                link(nc.vector.tensor_scalar(toff[:], tcol[:], float(P), -float(P), ALU.mult, ALU.add))
                nc.vector.tensor_scalar(tcol_i[:], tcol[:], -1.0, None, ALU.add).then_inc(rows_known, 1)

                dve.wait_ge(win_in, 16 * 3 * SW)
                link(nc.vector.tensor_copy(dwf[:], dwin[:]))
                link(nc.vector.tensor_copy(swf[:], swin[:]))
                link(nc.vector.tensor_scalar(dcl[:], dwf[:], float(N - 1), None, ALU.min))
                for j in range(SW):
                    last = nc.vector.tensor_scalar(dlw[:, j], dwf[:, j], toff[:, j:j + 1], None, ALU.subtract)
                last.then_inc(win_f, 1)
                dve.wait_ge(turned, 1)
                link(nc.vector.tensor_copy(k["dl"][:], tr_ps[:, 0]))
                link(nc.vector.tensor_copy(k["idx"][:, :, 0], tr_ps[:, 1]))
                link(nc.vector.tensor_copy(k["idx"][:, :, 1], tr_ps[:, 2]))
                for j in range(SW):
                    parts = [eparts[:, j, i].rearrange("p (k e) -> p k e", e=P) for i in range(PARTS)]
                    src = ewin[:, j].rearrange("p (e k) -> p k e", k=ED)
                    split(link, nc, src, parts, erest[:].rearrange("p (k e) -> p k e", e=P))
                    nc.vector.tensor_copy(gd[:, 0:1], ge[:, 0:1]).then_inc(esplit, 1)
                dve.wait_ge(xb, 1)


def gated_steps(nc, a, k, sb, ps, sem, scope):
    RING = 4
    with ExitStack() as scope:
        ix = sb("g_ix", [P, 2, IRING, 2], I32, scope)
        xw = sb("g_xw", [P, RING, 2 * D], F32, scope)
        eat = sb("g_eat", [DE, RING, P], F32, scope)
        rt = sb("g_rt", [P, 2, 2 * P], F32, scope)
        gate = sb("g_gate", [P, 2, D], F32, scope)
        msg = sb("g_msg", [P, 2, D], F32, scope)
        hot = sb("g_hot", [P, 2, P], F32, scope)
        hid_ps = ps("hid_ps", [P, 2, 512], scope)
        gate_ps = ps("gate_ps", [P, 2, 512], scope)
        core_ps = ps("core_ps", [P, 2, 512], scope)
        sum_ps = ps("sum_ps", [P, 2, 512], scope)

        ix_ready = sem("g_ix_ready", scope)
        xw_in = [sem(f"g_xw_in{i}", scope) for i in range(RING)]
        ea_in = [sem(f"g_ea_in{i}", scope) for i in range(RING)]
        hid_made = sem("g_hid_made", scope)
        relu_made = sem("g_relu_made", scope)
        gate_in = sem("g_gate_in", scope)
        gate_made = sem("g_gate_made", scope)
        core_made = sem("g_core_made", scope)
        hot_made = sem("g_hot_made", scope)
        msg_made = sem("g_msg_made", scope)
        sum_made = sem("g_sum_made", scope)
        added = sem("g_added", scope)

        with nc.Block() as block:
            @block.sync
            def _(sp):
                regs = [sp.alloc_register(f"g_row{i}") for i in range(U)]
                rows = [None] * U

                def head(it):
                    sp.load(regs, k["row_i"][0:1, bass.ds(it * U, U)])
                    for i in range(U):
                        rows[i] = sp.snap(regs[i], min_val=0, max_val=RMAX)

                def body(i):
                    if i.back(RING).live:
                        sp.wait_ge(hid_made, i.back(RING).done)
                        nc.sync.nop(nofuse=True)
                    sp.dma_start(eat[:, i.slot(RING)], a["ea64t"][:, bass.ds(rows[i.k], P)]).then_inc(ea_in[i.slot(RING)], 16)
                run_steps(sp, body, U, STEPS, 0, head)

            @block.gpsimd
            def _(pool):
                def body(i):
                    if i.k % IRING == 0:
                        if i.back(2 * IRING).live:
                            j = i.back(IRING + 1)
                            pool.wait_ge(xw_in[j.slot(RING)], j.turns(RING) * 16)
                        nc.gpsimd.tensor_copy(ix[:, i.k // IRING % 2], k["idx"][:, bass.ds(i.s, IRING), :]).then_inc(ix_ready, 1)
                        pool.wait_ge(ix_ready, i.turns(IRING))
                        nc.gpsimd.nop(nofuse=True)
                    if i.back(RING).live:
                        pool.wait_ge(gate_in, i.back(RING).done)
                        pool.wait_ge(hid_made, i.back(RING).done)
                        nc.gpsimd.nop(nofuse=True)
                    at = bass.IndirectOffsetOnAxis(ap=ix[:, i.k // IRING % 2, i.k % IRING, 0:1], axis=0)
                    nc.gpsimd.indirect_dma_start(out=xw[:, i.slot(RING)], out_offset=None, in_=k["d_xw"],
                                                 in_offset=at).then_inc(xw_in[i.slot(RING)], 16)
                run_steps(pool, body, U, STEPS, 0)

            @block.tensor
            def _(pe):
                def body(i):
                    j = i.back(1)
                    if j.live:
                        pe.wait_ge(relu_made, j.done)
                        if j.back(2).live:
                            pe.wait_ge(msg_made, j.back(2).done)
                        o = core_ps[:, j.slot(2), 0:D]
                        for c in range(2):
                            nc.tensor.matmul(o, rt[:, j.slot(2), c * P:(c + 1) * P], k["w2"][:, c], start=(c == 0), stop=False)
                        nc.tensor.matmul(o, k["ones3"][:], k["b2s"][:], start=False, stop=True).then_inc(core_made, 1)
                    if i.live:
                        pe.wait_ge(ea_in[i.slot(RING)], i.turns(RING) * 16)
                        pe.wait_ge(xw_in[i.slot(RING)], i.turns(RING) * 16)
                        if i.back(2).live:
                            pe.wait_ge(relu_made, i.back(2).done)
                            pe.wait_ge(gate_in, i.back(2).done)
                        e = eat[:, i.slot(RING)]
                        for c in range(2):
                            cols = slice(c * P, (c + 1) * P)
                            nc.tensor.matmul(hid_ps[:, i.slot(2), cols], xw[:, i.slot(RING), cols], k["ident"][:],
                                             is_transpose=True, start=True, stop=False, skip_group_check=True)
                            nc.tensor.matmul(hid_ps[:, i.slot(2), cols], k["w1e"][:, cols], e,
                                             start=False, stop=True, skip_group_check=True)
                        nc.tensor.matmul(gate_ps[:, i.slot(2), 0:D], e, k["wge"][:], start=True, stop=True).then_inc(hid_made, 1)
                    j = i.back(2)
                    if j.live:
                        pe.wait_ge(msg_made, j.done)
                        pe.wait_ge(hot_made, j.done)
                        if j.back(2).live:
                            pe.wait_ge(added, j.back(2).done)
                        nc.tensor.matmul(sum_ps[:, j.slot(2), 0:D], hot[:, j.slot(2)], msg[:, j.slot(2)],
                                         start=True, stop=True).then_inc(sum_made, 1)
                run_steps(pe, body, U, STEPS, 2)

            @block.scalar
            def _(act):
                def body(i):
                    act.wait_ge(hid_made, i.done)
                    if i.back(2).live:
                        act.wait_ge(core_made, i.back(2).done)
                    nc.scalar.activation(rt[:, i.slot(2)], hid_ps[:, i.slot(2), 0:2 * P], ACT.Relu).then_inc(relu_made, 1)
                    act.wait_ge(gate_in, i.done)
                    nc.scalar.activation(gate[:, i.slot(2)], gate[:, i.slot(2)], ACT.Sigmoid).then_inc(gate_made, 1)
                run_steps(act, body, U, STEPS, 0)

            @block.vector
            def _(dve):
                LAG = 2
                regs = [dve.alloc_register(f"g_tile{i}") for i in range(U)]
                tiles = [None] * U

                def head(it):
                    dve.load(regs, k["tile_i"][0:1, bass.ds(it * U + (U - LAG), U)])
                    for i in range(U):
                        tiles[i] = dve.snap(regs[i], min_val=0, max_val=NT - 1)

                def body(i):
                    j = i.back(1)
                    if j.live:
                        if j.back(2).live:
                            dve.wait_ge(sum_made, j.back(2).done)
                        nc.vector.tensor_scalar(hot[:, j.slot(2)], k["node_row"][:], k["dl"][:, bass.ds(j.s, 1)], None,
                                                ALU.is_equal).then_inc(hot_made, 1)
                        dve.wait_ge(core_made, j.done)
                        dve.wait_ge(gate_made, j.done)
                        nc.vector.tensor_tensor(msg[:, j.slot(2)], core_ps[:, j.slot(2), 0:D], gate[:, j.slot(2)],
                                                ALU.mult).then_inc(msg_made, 1)
                    if i.live:
                        dve.wait_ge(hid_made, i.done)
                        dve.wait_ge(xw_in[i.slot(RING)], i.turns(RING) * 16)
                        if i.back(2).live:
                            dve.wait_ge(msg_made, i.back(2).done)
                        nc.vector.tensor_tensor(gate[:, i.slot(2)], gate_ps[:, i.slot(2), 0:D], xw[:, i.slot(RING), D:],
                                                ALU.add).then_inc(gate_in, 1)
                    j = i.back(LAG)
                    if j.live:
                        dve.wait_ge(sum_made, j.done)
                        if j.back(1).live:
                            dve.wait_ge(added, j.back(1).done)
                        row = k["acc"][:, bass.ds(tiles[i.k], 1), 0:D].rearrange("p t f -> p (t f)")
                        nc.vector.tensor_tensor(row, row, sum_ps[:, j.slot(2), 0:D], ALU.add).then_inc(added, 1)
                run_steps(dve, body, U, STEPS, LAG, head)


def attention_weights(nc, a, k, sb, ps, sem, scope, layer, din, heads, ch):
    W = heads * ch
    K = din // P
    w = {
        "wl": sb(f"wl{layer}", [P, K, W], F32, scope), "wr": sb(f"wr{layer}", [P, K, W], F32, scope),
        "we": sb(f"we{layer}", [EROWS, W], BF16, scope),
        "ebias": sb(f"ebias{layer}", [P, W], F32, scope),
        "att_row": sb(f"att_row{layer}", [P, W], F32, scope),
        "att_col": sb(f"att_col{layer}", [P, W // P], F32, scope),
    }
    with ExitStack() as own:
        wef = sb(f"wef{layer}", [EROWS, W], F32, own)
        weq = sb(f"weq{layer}", [EROWS, W], F32, own)
        wep = sb(f"wep{layer}", [EROWS, PARTS, W], BF16, own)
        ebias_ps = ps(f"ebias_ps{layer}", [P, 512], own)
        loaded = sem(f"w_loaded{layer}", own)
        loaded_we = sem(f"w_loaded_we{layer}", own)
        dve_own = sem(f"w_dve_own{layer}", own)
        eb_made = sem(f"w_eb_made{layer}", own)
        with nc.Block() as block:
            @block.sync
            def _(sp):
                for g in range(PARTS * PARTS):
                    sp.dma_start(wef[g * ED:(g + 1) * ED, :], a[f"We{layer}"]).then_inc(loaded_we, 16)

            @block.scalar
            def _(act):
                act.dma_start(w["wl"][:], a[f"Wl{layer}"].rearrange("(c p) f -> p c f", p=P)).then_inc(loaded, 16)
                act.dma_start(w["wr"][:], a[f"Wr{layer}"].rearrange("(c p) f -> p c f", p=P)).then_inc(loaded, 16)
                act.dma_start(w["att_row"][:], a[f"att{layer}"].to_broadcast((P, W))).then_inc(loaded, 16)
                with nc.allow_non_contiguous_dma(reason="a column of attention weights"):
                    act.dma_start(w["att_col"][:], a[f"att{layer}"].rearrange("one (c p) -> p (one c)", p=P)).then_inc(loaded, 16)
                act.wait_ge(loaded, 16 * 4)

            @block.vector
            def _(dve):
                link = Chain(dve, dve_own)
                dve.wait_ge(loaded_we, 16 * PARTS * PARTS)
                split(link, nc, wef[:], [wep[:, i] for i in range(PARTS)], weq[:])
                pick(link, nc, w["we"][:], [wep[:, i] for i in range(PARTS)], k["sel"][:, PARTS:], EROWS)
                dve.wait_ge(eb_made, 1)
                link(nc.vector.tensor_copy(w["ebias"][:], ebias_ps[:, 0:W]))

            @block.tensor
            def _(pe):
                pe.wait_ge(loaded_we, 16 * PARTS * PARTS)
                nc.tensor.matmul(ebias_ps[:, 0:W], k["emean"][:], wef[0:ED, :], start=True, stop=True).then_inc(eb_made, 1)
    return w


def spread(k, nc, dve, act_sem, dve_sem, link, count):
    for t in range(NT):
        last = nc.vector.bn_aggr(k["mv"][:, t], k["st"][:, t])
    link(last)
    nc.vector.tensor_scalar(k["rstd"][:], k["mv"][:, :, 1], EPS, None, ALU.add).then_inc(dve_sem, 1)
    dve.wait_ge(act_sem, count)
    link(nc.vector.reciprocal(k["rstd"][:], k["rstd"][:]))


def root(k, nc, act, act_sem, dve_sem, count):
    act.wait_ge(dve_sem, count)
    nc.scalar.activation(k["rstd"][:], k["rstd"][:], ACT.Sqrt).then_inc(act_sem, 1)


def tile_of(buf, t, width):
    return buf[:, bass.ds(t, 1), 0:width].rearrange("p t f -> p (t f)")


def gated_nodes(nc, a, k, sb, ps, sem):
    with ExitStack() as own:
        gamma = sb("gamma", [P, D], F32, own)
        y = sb("gn_y", [P, 2, D], F32, own)
        loaded = sem("gn_loaded", own)
        stats = sem("gn_stats", own)
        dve_own = sem("gn_own", own)
        to_root = sem("gn_to_root", own)
        rooted = sem("gn_rooted", own)
        normed = sem("gn_normed", own)
        scaled = sem("gn_scaled", own)
        shifted = sem("gn_shifted", own)
        with nc.Block() as block:
            @block.sync
            def _(sp):
                sp.dma_start(gamma[:], a["gamma"].to_broadcast((P, D))).then_inc(loaded, 16)

            @block.scalar
            def _(act):
                for n in range(2):
                    root(k, nc, act, rooted, to_root, n + 1)

            @block.vector
            def _(dve):
                link = Chain(dve, dve_own)

                def stat(i):
                    nc.vector.bn_stats(tile_of(k["st"], i.s, 6), tile_of(k["acc"], i.s, D)).then_inc(stats, 1)
                run_steps(dve, stat, 2, NT, 0)
                dve.wait_ge(stats, NT)
                spread(k, nc, dve, rooted, to_root, link, 1)
                dve.wait_ge(loaded, 16)

                def body(i):
                    if i.live:
                        if i.back(2).live:
                            dve.wait_ge(shifted, i.back(2).done)
                        nc.vector.tensor_scalar(y[:, i.slot(2)], tile_of(k["acc"], i.s, D), k["mv"][:, bass.ds(i.s, 1), 0],
                                                k["rstd"][:, bass.ds(i.s, 1)], ALU.subtract, ALU.mult).then_inc(normed, 1)
                    j = i.back(1)
                    if j.live:
                        dve.wait_ge(normed, j.done)
                        nc.vector.tensor_tensor(y[:, j.slot(2)], y[:, j.slot(2)], gamma[:], ALU.mult).then_inc(scaled, 1)
                        dve.wait_ge(scaled, j.done)
                        nc.vector.tensor_tensor(tile_of(k["acc"], j.s, D), y[:, j.slot(2)], tile_of(k["xn"], j.s, D),
                                                ALU.add).then_inc(shifted, 1)
                    j = i.back(2)
                    if j.live:
                        dve.wait_ge(shifted, j.done)
                        nc.vector.bn_stats(tile_of(k["st"], j.s, 6), tile_of(k["acc"], j.s, D)).then_inc(stats, 1)
                run_steps(dve, body, 2, NT, 2)
                dve.wait_ge(stats, 2 * NT)
                spread(k, nc, dve, rooted, to_root, link, 2)


def attended_nodes(nc, a, k, sb, ps, sem):
    W = HEADS * HID
    with ExitStack() as own:
        bias = sb("an_bias", [P, W], F32, own)
        loaded = sem("an_loaded", own)
        stats = sem("an_stats", own)
        dve_own = sem("an_own", own)
        to_root = sem("an_to_root", own)
        rooted = sem("an_rooted", own)
        divided = sem("an_divided", own)
        with nc.Block() as block:
            @block.sync
            def _(sp):
                sp.dma_start(bias[:], a["cb1"].to_broadcast((P, W))).then_inc(loaded, 16)

            @block.scalar
            def _(act):
                root(k, nc, act, rooted, to_root, 1)

            @block.vector
            def _(dve):
                link = Chain(dve, dve_own)
                den = k["den"][:].rearrange("p t h -> p (t h)")
                link(nc.vector.tensor_scalar(den, den, 1e-16, None, ALU.add))
                link(nc.vector.reciprocal(k["rden"][:], den))
                dve.wait_ge(loaded, 16)

                def body(i):
                    if i.live:
                        for h in range(HEADS):
                            row = k["acc"][:, bass.ds(i.s, 1), h * HID:(h + 1) * HID].rearrange("p t f -> p (t f)")
                            last = nc.vector.scalar_tensor_tensor(row, row, k["rden"][:, bass.ds(i.s * HEADS + h, 1)],
                                                                  bias[:, h * HID:(h + 1) * HID], ALU.mult, ALU.add)
                        last.then_inc(divided, 1)
                    j = i.back(1)
                    if j.live:
                        dve.wait_ge(divided, j.done)
                        nc.vector.bn_stats(tile_of(k["st"], j.s, 6), tile_of(k["acc"], j.s, W)).then_inc(stats, 1)
                run_steps(dve, body, 2, NT, 1)
                dve.wait_ge(stats, NT)
                spread(k, nc, dve, rooted, to_root, link, 1)
                link(nc.vector.memset(k["den"][:], 1.0))


def project(nc, k, w, sb, ps, sem, layer, din, heads, ch):
    W = heads * ch
    K = din // P
    n = f"p{layer}_"
    dl, dr = k[f"d_xl{layer}"], k[f"d_xr{layer}"]
    with ExitStack() as own:
        xs = sb(n + "xs", [P, 2, din], F32, own)
        xt = sb(n + "xt", [P, 2, din], F32, own)
        xl = sb(n + "xl", [P, 2, W], F32, own)
        xr = sb(n + "xr", [P, 2, W], F32, own)
        xre = sb(n + "xre", [P, 2, W], F32, own)
        own_m = sb(n + "own_m", [P, 2, W], F32, own)
        leaky = sb(n + "leaky", [P, 2, W], F32, own)
        prod = sb(n + "prod", [P, W], F32, own)
        q = sb(n + "q", [P, 2, heads], F32, own)
        if layer == 2:
            gain = sb(n + "gain", [P, din], F32, own)
            offset = sb(n + "offset", [P, din], F32, own)
            ya = sb(n + "ya", [P, 2, din], F32, own)
            yb = sb(n + "yb", [P, 2, din], F32, own)
        xt_ps = ps(n + "xt_ps", [P, 2, 512], own)
        xl_ps = ps(n + "xl_ps", [P, 2, 512], own)
        xr_ps = ps(n + "xr_ps", [P, 2, 512], own)
        loaded = sem(n + "loaded", own)
        normed = sem(n + "normed", own)
        gained = sem(n + "gained", own)
        offsetted = sem(n + "offsetted", own)
        lowed = sem(n + "lowed", own)
        exped = sem(n + "exped", own)
        x_made = sem(n + "x_made", own)
        x_kept = sem(n + "x_kept", own)
        turned = sem(n + "turned", own)
        xt_made = sem(n + "xt_made", own)
        rows_made = sem(n + "rows_made", own)
        l_taken = sem(n + "l_taken", own)
        r_taken = sem(n + "r_taken", own)
        summed = sem(n + "summed", own)
        xre_made = sem(n + "xre_made", own)
        acc_set = sem(n + "acc_set", own)
        highed = sem(n + "highed", own)
        leaked = sem(n + "leaked", own)
        scored = sem(n + "scored", own)
        m_set = sem(n + "m_set", own)
        l_out = [sem(n + f"l_out{i}", own) for i in range(2)]
        r_out = [sem(n + f"r_out{i}", own) for i in range(2)]

        with nc.Block() as block:
            @block.sync
            def _(sp):
                if layer == 2:
                    sp.dma_start(gain[:], k["in"]["g1"].to_broadcast((P, din))).then_inc(loaded, 16)
                    sp.dma_start(offset[:], k["in"]["be1"].to_broadcast((P, din))).then_inc(loaded, 16)

                def body(i):
                    sp.wait_ge(l_taken, i.done)
                    sp.dma_start(dl[bass.ds(i.s * P, P), 0:W], xl[:, i.slot(2)]).then_inc(l_out[i.slot(2)], 16)
                    sp.wait_ge(r_taken, i.done)
                    sp.dma_start(dr[bass.ds(i.s * P, P), 0:W], xr[:, i.slot(2)]).then_inc(r_out[i.slot(2)], 16)
                run_steps(sp, body, 2, NT, 0)
                for i in range(2):
                    sp.wait_ge(l_out[i], 16 * (NT // 2))
                    sp.wait_ge(r_out[i], 16 * (NT // 2))

            @block.tensor
            def _(pe):
                def body(i):
                    if i.live:
                        pe.wait_ge(x_made, i.done)
                        if i.back(2).live:
                            pe.wait_ge(xt_made, i.back(2).done)
                        for c in range(K):
                            last = nc.tensor.transpose(xt_ps[:, i.slot(2), c * P:(c + 1) * P], xs[:, i.slot(2), c * P:(c + 1) * P],
                                                       k["ident"][:])
                        last.then_inc(turned, 1)
                    j = i.back(1)
                    if j.live:
                        pe.wait_ge(xt_made, j.done)
                        if j.back(2).live:
                            pe.wait_ge(l_taken, j.back(2).done)
                            pe.wait_ge(r_taken, j.back(2).done)
                        for bank, m in ((xl_ps, w["wl"]), (xr_ps, w["wr"])):
                            for c in range(K):
                                last = nc.tensor.matmul(bank[:, j.slot(2), 0:W], xt[:, j.slot(2), c * P:(c + 1) * P], m[:, c],
                                                        start=(c == 0), stop=(c == K - 1))
                        last.then_inc(rows_made, 1)
                run_steps(pe, body, 2, NT, 1)

            @block.scalar
            def _(act):
                def body(i):
                    if i.live:
                        if layer == 2:
                            act.wait_ge(lowed, i.done)
                            nc.scalar.activation(yb[:, i.slot(2)], yb[:, i.slot(2)], ACT.Exp).then_inc(exped, 1)
                        act.wait_ge(turned, i.done)
                        if i.back(2).live:
                            act.wait_ge(rows_made, i.back(2).done)
                        nc.scalar.copy(xt[:, i.slot(2)], xt_ps[:, i.slot(2), 0:din]).then_inc(xt_made, 1)
                    j = i.back(1)
                    if j.live:
                        act.wait_ge(rows_made, j.done)
                        if j.back(2).live:
                            act.wait_ge(l_out[j.slot(2)], j.back(2).turns(2) * 16)
                            act.wait_ge(r_out[j.slot(2)], j.back(2).turns(2) * 16)
                            act.wait_ge(acc_set, j.back(2).done)
                            act.wait_ge(summed, j.back(2).done)
                        nc.scalar.copy(xl[:, j.slot(2), 0:W], xl_ps[:, j.slot(2), 0:W]).then_inc(l_taken, 1)
                        nc.scalar.copy(xr[:, j.slot(2), 0:W], xr_ps[:, j.slot(2), 0:W]).then_inc(r_taken, 1)
                run_steps(act, body, 2, NT, 1)

            @block.gpsimd
            def _(pool):
                def body(i):
                    if layer == 1 and i.live:
                        pool.wait_ge(x_made, i.done)
                        nc.gpsimd.tensor_copy(tile_of(k["xn"], i.s, D), xs[:, i.slot(2)]).then_inc(x_kept, 1)
                    j = i.back(1)
                    if j.live:
                        pool.wait_ge(l_taken, j.done)
                        pool.wait_ge(xre_made, j.done)
                        nc.gpsimd.tensor_copy(tile_of(k["acc"], j.s, W), xl[:, j.slot(2), 0:W]).then_inc(acc_set, 1)
                        nc.gpsimd.tensor_tensor(own_m[:, j.slot(2)], xl[:, j.slot(2)], xre[:, j.slot(2)],
                                                ALU.add).then_inc(summed, 1)
                run_steps(pool, body, 2, NT, 1)

            @block.vector
            def _(dve):
                if layer == 2:
                    dve.wait_ge(loaded, 32)

                def source(i):
                    if i.back(2).live:
                        dve.wait_ge(turned, i.back(2).done)
                    if layer == 1:
                        if i.back(2).live:
                            dve.wait_ge(x_kept, i.back(2).done)
                        nc.vector.tensor_scalar(xs[:, i.slot(2)], tile_of(k["acc"], i.s, din), k["mv"][:, bass.ds(i.s, 1), 0],
                                                k["rstd"][:, bass.ds(i.s, 1)], ALU.subtract, ALU.mult).then_inc(x_made, 1)
                        return
                    nc.vector.tensor_scalar(ya[:, i.slot(2)], tile_of(k["acc"], i.s, din), k["mv"][:, bass.ds(i.s, 1), 0],
                                            k["rstd"][:, bass.ds(i.s, 1)], ALU.subtract, ALU.mult).then_inc(normed, 1)
                    dve.wait_ge(normed, i.done)
                    nc.vector.tensor_tensor(ya[:, i.slot(2)], ya[:, i.slot(2)], gain[:], ALU.mult).then_inc(gained, 1)
                    dve.wait_ge(gained, i.done)
                    nc.vector.tensor_tensor(ya[:, i.slot(2)], ya[:, i.slot(2)], offset[:], ALU.add).then_inc(offsetted, 1)
                    dve.wait_ge(offsetted, i.done)
                    nc.vector.tensor_scalar(yb[:, i.slot(2)], ya[:, i.slot(2)], 0.0, None, ALU.min).then_inc(lowed, 1)
                    dve.wait_ge(lowed, i.done)
                    nc.vector.tensor_scalar(ya[:, i.slot(2)], ya[:, i.slot(2)], 0.0, -1.0, ALU.max, ALU.add).then_inc(highed, 1)
                    dve.wait_ge(highed, i.done)
                    dve.wait_ge(exped, i.done)
                    nc.vector.tensor_tensor(xs[:, i.slot(2)], ya[:, i.slot(2)], yb[:, i.slot(2)], ALU.add).then_inc(x_made, 1)

                def body(i):
                    if i.live:
                        source(i)
                    j = i.back(1)
                    if j.live:
                        if j.back(2).live:
                            dve.wait_ge(summed, j.back(2).done)
                        dve.wait_ge(r_taken, j.done)
                        nc.vector.tensor_tensor(xre[:, j.slot(2), 0:W], xr[:, j.slot(2), 0:W], w["ebias"][:, 0:W],
                                                ALU.add).then_inc(xre_made, 1)
                    j = i.back(2)
                    if j.live:
                        dve.wait_ge(summed, j.done)
                        m = own_m[:, j.slot(2)]
                        nc.vector.scalar_tensor_tensor(leaky[:, j.slot(2)], m, SLOPE, m, ALU.mult, ALU.max).then_inc(leaked, 1)
                        dve.wait_ge(leaked, j.done)
                        for h in range(heads):
                            cols = slice(h * ch, (h + 1) * ch)
                            last = nc.vector.scalar_tensor_tensor(prod[:, cols], leaky[:, j.slot(2), cols], -1.0,
                                                                  w["att_row"][:, cols], ALU.mult, ALU.mult,
                                                                  accum_out=q[:, j.slot(2), h:h + 1])
                        last.then_inc(scored, 1)
                        dve.wait_ge(scored, j.done)
                        nc.vector.tensor_scalar(tile_of(k["low"], j.s, heads), q[:, j.slot(2)], 0.0, None, ALU.add).then_inc(m_set, 1)
                run_steps(dve, body, 2, NT, 2)


def attention_steps(nc, k, w, sb, ps, sem, layer, heads, ch):
    W = heads * ch
    K = W // P
    HP = heads * P
    RING = 8
    n = f"t{layer}_"
    with ExitStack() as own:
        ix = sb(n + "ix", [P, 2, IRING, 2], I32, own)
        dl = sb(n + "dl", [P, 2, IRING], F32, own)
        xl = sb(n + "xl", [P, RING, W], F32, own)
        xr = sb(n + "xr", [P, RING, W], F32, own)
        ea = sb(n + "ea", [EROWS, 2, IRING, P], BF16, own)
        slope = sb(n + "slope", [P, 2, W], F32, own)
        leaky = sb(n + "leaky", [P, 2, W], F32, own)
        cold = sb(n + "cold", [P, 2, P], BF16, own)
        top = sb(n + "top", [P, 2, heads], F32, own)
        low = sb(n + "low", [P, 2, heads], F32, own)
        fade = sb(n + "fade", [P, 4, heads], F32, own)
        exps = sb(n + "exps", [P, 2, HP], F32, own)
        exps_t = sb(n + "exps_t", [P, 2, HP], F32, own)
        part = sb(n + "part", [P, 4, heads], F32, own)
        dnew = sb(n + "dnew", [P, 2, heads], F32, own)
        m_ps = ps(n + "m_ps", [P, 2, 512], own)
        wide_ps = ps(n + "wide_ps", [P, 2, 512], own)
        turn_ps = ps(n + "turn_ps", [P, 512], own)
        sum_ps = ps(n + "sum_ps", [P, 2, 512], own)

        ix_ready = sem(n + "ix_ready", own)
        xl_in = [sem(n + f"xl_in{i}", own) for i in range(RING)]
        xr_in = [sem(n + f"xr_in{i}", own) for i in range(RING)]
        ea_in = [sem(n + f"ea_in{i}", own) for i in range(2)]
        m_made = sem(n + "m_made", own)
        slope_made = sem(n + "slope_made", own)
        leaky_made = sem(n + "leaky_made", own)
        wide_made = sem(n + "wide_made", own)
        top_made = sem(n + "top_made", own)
        low_made = sem(n + "low_made", own)
        drop_made = sem(n + "drop_made", own)
        kept = sem(n + "kept", own)
        exps_made = sem(n + "exps_made", own)
        turned = sem(n + "turned", own)
        copied = sem(n + "copied", own)
        sum_made = sem(n + "sum_made", own)
        den_faded = sem(n + "den_faded", own)
        added = sem(n + "added", own)

        with nc.Block() as block:
            @block.sync
            def _(sp):
                def body(i):
                    if i.k % IRING:
                        return
                    half = i.k // IRING % 2
                    j = i.back(IRING + 1)
                    if j.live:
                        sp.wait_ge(m_made, j.done)
                        nc.sync.nop(nofuse=True)
                    sp.dma_start(ea[:, half], k["d_ea"][bass.ds(i.s, IRING)].rearrange("s r e -> r s e")).then_inc(ea_in[half], 16)
                run_steps(sp, body, U, STEPS, 0)

            @block.gpsimd
            def _(pool):
                def body(i):
                    half = i.k // IRING % 2
                    if i.k % IRING == 0:
                        if i.back(2 * IRING).live:
                            pool.wait_ge(leaky_made, i.back(IRING + 1).done)
                        nc.gpsimd.tensor_copy(dl[:, half], k["dl"][:, bass.ds(i.s, IRING)])
                        nc.gpsimd.tensor_copy(ix[:, half], k["idx"][:, bass.ds(i.s, IRING), :]).then_inc(ix_ready, 1)
                        pool.wait_ge(ix_ready, i.turns(IRING))
                        nc.gpsimd.nop(nofuse=True)
                    if i.back(RING).live:
                        pool.wait_ge(sum_made, i.back(RING).done)
                        nc.gpsimd.nop(nofuse=True)
                    for c, (rows, table, landed) in enumerate(((xl, k[f"d_xl{layer}"], xl_in), (xr, k[f"d_xr{layer}"], xr_in))):
                        at = bass.IndirectOffsetOnAxis(ap=ix[:, half, i.k % IRING, c:c + 1], axis=0)
                        nc.gpsimd.indirect_dma_start(out=rows[:, i.slot(RING)], out_offset=None, in_=table,
                                                     in_offset=at).then_inc(landed[i.slot(RING)], 16)
                run_steps(pool, body, U, STEPS, 0)

            @block.tensor
            def _(pe):
                def body(i):
                    j = i.back(1)
                    if j.live:
                        pe.wait_ge(leaky_made, j.done)
                        for h in range(heads):
                            o = wide_ps[:, j.slot(2), h * P:(h + 1) * P]
                            for c in range(h * ch // P, (h + 1) * ch // P):
                                nc.tensor.matmul(o, w["att_col"][:, c:c + 1].to_broadcast((P, P)), leaky[:, j.slot(2), c * P:(c + 1) * P],
                                                 start=(c == h * ch // P), stop=False, skip_group_check=True)
                            last = nc.tensor.matmul(o, cold[:, j.slot(2)], k["bigi"][:], start=False, stop=True,
                                                    skip_group_check=True)
                        last.then_inc(wide_made, 1)
                    if i.live:
                        pe.wait_ge(xl_in[i.slot(RING)], i.turns(RING) * 16)
                        pe.wait_ge(xr_in[i.slot(RING)], i.turns(RING) * 16)
                        if i.k % IRING == 0:
                            pe.wait_ge(ea_in[i.k // IRING % 2], i.turns_of(IRING, 2) * 16)
                        for c in range(K):
                            cols = slice(c * P, (c + 1) * P)
                            o = m_ps[:, i.slot(2), cols]
                            for r, rows in enumerate((xl, xr)):
                                nc.tensor.matmul(o, rows[:, i.slot(RING), cols], k["ident"][:], is_transpose=True,
                                                 start=(r == 0), stop=False, skip_group_check=True)
                            last = nc.tensor.matmul(o, w["we"][:, cols], ea[:, i.k // IRING % 2, i.k % IRING],
                                                    start=False, stop=True, skip_group_check=True)
                        last.then_inc(m_made, 1)
                    j = i.back(3)
                    if j.live:
                        pe.wait_ge(copied, j.done)
                        if not i.back(1).live:
                            pe.wait_ge(added, j.back(2).done)
                        for h in range(heads):
                            cols = slice(h * ch, (h + 1) * ch)
                            last = nc.tensor.matmul(sum_ps[:, j.slot(2), cols], exps_t[:, j.slot(2), h * P:(h + 1) * P],
                                                    xl[:, j.slot(RING), cols], start=True, stop=True)
                        last.then_inc(sum_made, 1)
                    j = i.back(2)
                    if j.live:
                        pe.wait_ge(exps_made, j.done)
                        for h in range(heads):
                            cols = slice(h * P, (h + 1) * P)
                            last = nc.tensor.transpose(turn_ps[:, cols], exps[:, j.slot(2), cols], k["ident"][:])
                        last.then_inc(turned, 1)
                run_steps(pe, body, U, STEPS, 3)

            @block.scalar
            def _(act):
                regs = [act.alloc_register(f"{n}kept{i}") for i in range(U)]
                tiles = [None] * U

                def head(it):
                    act.load(regs, k["tile_i"][0:1, bass.ds(it * U + (U - 1), U)])
                    for i in range(U):
                        tiles[i] = act.snap(regs[i], min_val=0, max_val=NT - 1)

                def body(i):
                    if i.live:
                        act.wait_ge(m_made, i.done)
                        nc.scalar.activation(slope[:, i.slot(2)], m_ps[:, i.slot(2), 0:W], ACT.Copy, scale=SLOPE).then_inc(slope_made, 1)
                    j = i.back(1)
                    if j.live:
                        act.wait_ge(drop_made, j.done)
                        nc.scalar.copy(tile_of(k["low"], tiles[i.k], heads), low[:, j.slot(2)]).then_inc(kept, 1)
                        nc.scalar.activation(fade[:, j.slot(4)], fade[:, j.slot(4)], ACT.Exp)
                        for h in range(heads):
                            cols = slice(h * P, (h + 1) * P)
                            last = nc.scalar.activation(exps[:, j.slot(2), cols], wide_ps[:, j.slot(2), cols], ACT.Exp,
                                                        bias=low[:, j.slot(2), h:h + 1], accum_out=part[:, j.slot(4), h:h + 1])
                        last.then_inc(exps_made, 1)
                    j = i.back(2)
                    if j.live:
                        act.wait_ge(turned, j.done)
                        nc.scalar.copy(exps_t[:, j.slot(2)], turn_ps[:, 0:HP]).then_inc(copied, 1)
                run_steps(act, body, U, STEPS, 2, head)

            @block.vector
            def _(dve):
                r1 = [dve.alloc_register(f"{n}top{i}") for i in range(U)]
                r4 = [dve.alloc_register(f"{n}sum{i}") for i in range(U)]
                t1, t4 = [None] * U, [None] * U

                def head(it):
                    dve.load(r1, k["tile_i"][0:1, bass.ds(it * U + (U - 1), U)])
                    dve.load(r4, k["tile_i"][0:1, bass.ds(it * U + (U - 4), U)])
                    for i in range(U):
                        t1[i] = dve.snap(r1[i], min_val=0, max_val=NT - 1)
                        t4[i] = dve.snap(r4[i], min_val=0, max_val=NT - 1)

                def body(i):
                    j = i.back(4)
                    if j.live:
                        dve.wait_ge(sum_made, j.done)
                        if j.back(1).live:
                            dve.wait_ge(added, j.back(1).done)
                        den = tile_of(k["den"], t4[i.k], heads)
                        if heads == 1:
                            nc.vector.scalar_tensor_tensor(den, den, fade[:, j.slot(4)], part[:, j.slot(4)], ALU.mult, ALU.add)
                        else:
                            nc.vector.tensor_tensor(dnew[:, j.slot(2)], den, fade[:, j.slot(4)], ALU.mult).then_inc(den_faded, 1)
                        for h in range(heads):
                            cols = slice(h * ch, (h + 1) * ch)
                            row = k["acc"][:, bass.ds(t4[i.k], 1), cols].rearrange("p t f -> p (t f)")
                            last = nc.vector.scalar_tensor_tensor(row, row, fade[:, j.slot(4), h:h + 1],
                                                                  sum_ps[:, j.slot(2), cols], ALU.mult, ALU.add)
                        if heads > 1:
                            dve.wait_ge(den_faded, j.done)
                            last = nc.vector.tensor_tensor(den, dnew[:, j.slot(2)], part[:, j.slot(4)], ALU.add)
                        last.then_inc(added, 1)
                    j = i.back(1)
                    if j.live:
                        dve.wait_ge(wide_made, j.done)
                        nc.vector.tensor_reduce(top[:, j.slot(2)], wide_ps[:, j.slot(2), 0:HP].rearrange("p (h e) -> p h e", e=P),
                                                AX.X, ALU.max).then_inc(top_made, 1)
                    if i.live:
                        if i.k % IRING == 0:
                            dve.wait_ge(ix_ready, i.turns(IRING))
                        nc.vector.tensor_scalar(cold[:, i.slot(2)], k["node_row"][:], dl[:, i.k // IRING % 2, i.k % IRING:i.k % IRING + 1],
                                                -1.0, ALU.is_equal, ALU.add)
                    if j.live:
                        dve.wait_ge(top_made, j.done)
                        if j.back(1).live:
                            dve.wait_ge(kept, j.back(1).done)
                        old = tile_of(k["low"], t1[i.k], heads)
                        nc.vector.scalar_tensor_tensor(low[:, j.slot(2)], top[:, j.slot(2)], -1.0, old,
                                                       ALU.mult, ALU.min).then_inc(low_made, 1)
                        dve.wait_ge(low_made, j.done)
                        nc.vector.tensor_tensor(fade[:, j.slot(4)], low[:, j.slot(2)], old, ALU.subtract).then_inc(drop_made, 1)
                    if i.live:
                        dve.wait_ge(slope_made, i.done)
                        nc.vector.tensor_tensor(leaky[:, i.slot(2)], m_ps[:, i.slot(2), 0:W], slope[:, i.slot(2)],
                                                ALU.max).then_inc(leaky_made, 1)
                run_steps(dve, body, U, STEPS, 4, head)


def last_nodes(nc, a, k, sb, ps, sem, out):
    with ExitStack() as own:
        bias = sb("ln_bias", [P, D], F32, own)
        gain = sb("ln_gain", [P, D], F32, own)
        offset = sb("ln_offset", [P, D], F32, own)
        y = sb("ln_y", [P, 2, D], F32, own)
        yo = sb("ln_yo", [P, 2, D], F32, own)
        loaded = sem("ln_loaded", own)
        divided = sem("ln_divided", own)
        normed = sem("ln_normed", own)
        scaled = sem("ln_scaled", own)
        offsetted = sem("ln_offsetted", own)
        doubled = sem("ln_doubled", own)
        stats = sem("ln_stats", own)
        dve_own = sem("ln_own", own)
        to_root = sem("ln_to_root", own)
        rooted = sem("ln_rooted", own)
        made = sem("ln_made", own)
        stored = [sem(f"ln_stored{i}", own) for i in range(2)]
        FULL = N // P
        with nc.Block() as block:
            @block.sync
            def _(sp):
                sp.dma_start(bias[:], a["cb2"].to_broadcast((P, D))).then_inc(loaded, 16)
                sp.dma_start(gain[:], a["g2"].to_broadcast((P, D))).then_inc(loaded, 16)
                sp.dma_start(offset[:], a["be2"].to_broadcast((P, D))).then_inc(loaded, 16)

                def body(i):
                    sp.wait_ge(made, i.done)
                    sp.dma_start(out[bass.ds(i.s * P, P), :], yo[:, i.slot(2)]).then_inc(stored[i.slot(2)], 16)
                run_steps(sp, body, 2, FULL, 0)
                sp.wait_ge(made, FULL + 1)
                sp.dma_start(out[FULL * P:N, :], yo[0:N - FULL * P, 0]).then_inc(stored[0], 16)
                sp.wait_ge(stored[0], 16 * (FULL // 2 + 1))
                sp.wait_ge(stored[1], 16 * (FULL // 2))

            @block.scalar
            def _(act):
                for c in range(2):
                    root(k, nc, act, rooted, to_root, c + 1)

            @block.vector
            def _(dve):
                link = Chain(dve, dve_own)
                den = k["den"][:, :, 0]
                rden = k["rden"][:, 0:NT]
                link(nc.vector.tensor_scalar(den, den, 1e-16, None, ALU.add))
                link(nc.vector.reciprocal(rden, den))
                dve.wait_ge(loaded, 48)

                def body(i):
                    if i.live:
                        row = tile_of(k["acc"], i.s, D)
                        nc.vector.scalar_tensor_tensor(row, row, k["rden"][:, bass.ds(i.s, 1)], bias[:],
                                                       ALU.mult, ALU.add).then_inc(divided, 1)
                    j = i.back(1)
                    if j.live:
                        dve.wait_ge(divided, j.done)
                        nc.vector.bn_stats(tile_of(k["st"], j.s, 6), tile_of(k["acc"], j.s, D)).then_inc(stats, 1)
                run_steps(dve, body, 2, NT, 1)
                dve.wait_ge(stats, NT)
                spread(k, nc, dve, rooted, to_root, link, 1)

                def body(i):
                    if i.live:
                        if i.back(2).live:
                            dve.wait_ge(doubled, i.back(2).done)
                        nc.vector.tensor_scalar(y[:, i.slot(2)], tile_of(k["acc"], i.s, D), k["mv"][:, bass.ds(i.s, 1), 0],
                                                k["rstd"][:, bass.ds(i.s, 1)], ALU.subtract, ALU.mult).then_inc(normed, 1)
                    j = i.back(1)
                    if j.live:
                        dve.wait_ge(normed, j.done)
                        nc.vector.tensor_tensor(y[:, j.slot(2)], y[:, j.slot(2)], gain[:], ALU.mult).then_inc(scaled, 1)
                        dve.wait_ge(scaled, j.done)
                        nc.vector.tensor_tensor(y[:, j.slot(2)], y[:, j.slot(2)], offset[:], ALU.add).then_inc(offsetted, 1)
                        dve.wait_ge(offsetted, j.done)
                        nc.vector.scalar_tensor_tensor(tile_of(k["acc"], j.s, D), tile_of(k["xn"], j.s, D), 2.0,
                                                       y[:, j.slot(2)], ALU.mult, ALU.add).then_inc(doubled, 1)
                    j = i.back(2)
                    if j.live:
                        dve.wait_ge(doubled, j.done)
                        nc.vector.bn_stats(tile_of(k["st"], j.s, 6), tile_of(k["acc"], j.s, D)).then_inc(stats, 1)
                run_steps(dve, body, 2, NT, 2)
                dve.wait_ge(stats, 2 * NT)
                spread(k, nc, dve, rooted, to_root, link, 2)

                def body(i):
                    if i.back(2).live:
                        dve.wait_ge(stored[i.slot(2)], i.back(2).turns(2) * 16)
                    nc.vector.tensor_scalar(yo[:, i.slot(2)], tile_of(k["acc"], i.s, D), k["mv"][:, bass.ds(i.s, 1), 0],
                                            k["rstd"][:, bass.ds(i.s, 1)], ALU.subtract, ALU.mult).then_inc(made, 1)
                run_steps(dve, body, 2, FULL, 0)
                body(Step(FULL // 2, 0, 2, FULL + 2))


_WEIGHTS = {
    "W1": "L0_gnn_W1", "b1": "L0_gnn_b1", "W2": "L0_gnn_W2", "b2": "L0_gnn_b2", "Wg": "L0_gnn_Wg", "bg": "L0_gnn_bg",
    "gamma": "L0_gnn_gamma", "beta": "L0_gnn_beta", "Wl1": "L1_gnn_Wl1", "Wr1": "L1_gnn_Wr1", "We1": "L1_gnn_We1",
    "att1": "L1_gnn_att1", "cb1": "L1_gnn_b1", "g1": "L1_gnn_g1", "be1": "L1_gnn_be1", "Wl2": "L1_gnn_Wl2",
    "Wr2": "L1_gnn_Wr2", "We2": "L1_gnn_We2", "att2": "L1_gnn_att2", "cb2": "L1_gnn_b2", "g2": "L1_gnn_g2",
    "be2": "L1_gnn_be2",
}
BEYOND = 1 << 20


def laid_out(inputs):
    x = np.asarray(inputs["x"])
    edges = EP - E
    arrays = {
        "x": np.pad(x, ((0, NP - N), (0, 0))),
        "src": np.pad(np.asarray(inputs["src"]), (0, edges)).reshape(EP, 1),
        "dst": np.pad(np.asarray(inputs["dst"]), (0, edges), constant_values=BEYOND).reshape(EP, 1),
        "ea4": np.pad(np.asarray(inputs["edge_attr_4"]), ((0, edges), (0, 0))),
        "ea64t": np.ascontiguousarray(np.pad(np.asarray(inputs["edge_attr_64"]), ((0, edges), (0, 0))).T),
    }
    arrays["xt"] = np.ascontiguousarray(arrays["x"].T)
    for short, name in _WEIGHTS.items():
        w = np.ascontiguousarray(inputs[name])
        arrays[short] = w.reshape(1, -1) if w.ndim == 1 or short.startswith("att") else w
    return arrays


def kernel(**inputs):
    import concourse.bacc as bacc
    from concourse.bass_utils import run_bass_kernel_spmd

    nc = bacc.Bacc("TRN2", target_bir_lowering=False, num_devices=1)
    arrays = laid_out(inputs)
    a = {n: nc.dram_tensor(f"in_{n}", v.shape, mybir.dt.from_np(v.dtype), kind="ExternalInput").ap() for n, v in arrays.items()}
    out = nc.dram_tensor("out_x", (N, D), F32, kind="ExternalOutput").ap()
    gnn(nc, a, out)
    r = run_bass_kernel_spmd(nc, [{f"in_{n}": v for n, v in arrays.items()}], core_ids=[0])
    return r.results[0]["out_x"]
```

```python
from contextlib import ExitStack

import numpy as np

import concourse.bass as bass
from concourse import mybir
from concourse.alu_op_type import AluOpType as ALU

ACT = mybir.ActivationFunctionType
AX = mybir.AxisListType
F32 = mybir.dt.float32
BF16 = mybir.dt.bfloat16
I32 = mybir.dt.int32

P = 128
N, E, D = 3125, 50000, 256
DE, ED = 64, 4
HEADS, HID = 4, 128
NT = 26
NP = NT * P
U = 16
BASE = -(-E // P) + -(-N // P) - 1
STEPS = -(-BASE // U) * U
SW = -(-STEPS // P)
ST = SW * P
RMAX = -(-E // P) * P
DC = RMAX // P + 2
EP = DC * P
IRING = 4
BIG = 1e30
PARTS = 3
EROWS = PARTS * PARTS * ED
SLOPE = 0.2
EPS = 1e-5


class Step:

    def __init__(self, it, k, unroll, count):
        self.it, self.k, self.unroll, self.count = it, k, unroll, count

    def back(self, n):
        return Step(self.it, self.k - n, self.unroll, self.count)

    @property
    def live(self):
        return not isinstance(self.it, int) or 0 <= self.it * self.unroll + self.k < self.count

    @property
    def s(self):
        return self.it * self.unroll + self.k

    @property
    def done(self):
        return self.it * self.unroll + (self.k + 1)

    def slot(self, ring):
        return self.k % ring

    def turns(self, ring):
        return self.it * (self.unroll // ring) + (self.k // ring + 1)

    def turns_of(self, group, ring):
        return self.it * (self.unroll // (group * ring)) + (self.k // (group * ring) + 1)


def run_steps(eng, body, unroll, count, lag, head=None, peel=1):
    turns = count // unroll
    for turn in range(peel):
        if head:
            head(turn)
        for k in range(unroll):
            body(Step(turn, k, unroll, count))
    with eng.Fori(peel, turns) as it:
        if head:
            head(it)
        for k in range(unroll):
            body(Step(it, k, unroll, count))
    if head and lag:
        head(turns)
    for k in range(lag):
        body(Step(turns, k, unroll, count))


def gnn(nc, a, out):
    with ExitStack() as whole:
        def sb(name, shape, dt=F32, scope=whole):
            return scope.enter_context(nc.sbuf_tensor(name, shape, dt))

        banks = whole.enter_context(nc.psum_tensor("banks", [P, 8, 512], F32))
        taken = []

        def ps(name, shape, scope):
            count = shape[1] if len(shape) == 3 else 1
            n = len(taken)
            assert n + count <= 8, name
            taken.extend([name] * count)
            scope.callback(taken.__delitem__, slice(n, n + count))
            return banks[:, n:n + count] if len(shape) == 3 else banks[:, n]

        def sem(name, scope):
            if scope not in held:
                held[scope] = []
                scope.callback(clear, scope)
            held[scope].append(nc.alloc_semaphore(name))
            return held[scope][-1]

        held = {}

        def clear(scope):
            nc.clear_and_free_semaphores(held.pop(scope))
            nc.all_engine_barrier()

        k = {"in": a}
        k["acc"] = sb("acc", [P, NT, 512])
        k["xn"] = sb("xn", [P, NT, D])
        k["low"] = sb("low", [P, NT, HEADS])
        k["den"] = sb("den", [P, NT, HEADS])
        k["ident"] = sb("ident", [P, P])
        k["bigi"] = sb("bigi", [P, P], BF16)
        k["node_row"] = sb("node_row", [P, P])
        k["part"] = sb("part", [P, 1])
        k["dl"] = sb("dl", [P, ST])
        k["idx"] = sb("idx", [P, ST, 2], I32)
        k["row_i"] = sb("row_i", [1, ST], I32)
        k["tile_i"] = sb("tile_i", [1, U + ST], I32)
        k["w1e"] = sb("w1e", [DE, D])
        k["wge"] = sb("wge", [DE, D])
        k["w2"] = sb("w2", [P, 2, D])
        k["b2s"] = sb("b2s", [PARTS, D], BF16)
        k["ones3"] = sb("ones3", [PARTS, P], BF16)
        k["emean"] = sb("emean", [ED, P])
        k["mv"] = sb("mv", [P, NT, 2])
        k["st"] = sb("st", [P, NT, 6])
        k["rstd"] = sb("rstd", [P, NT])
        k["rden"] = sb("rden", [P, NT * HEADS])
        k["sel"] = sb("sel", [P, 2 * PARTS])
        k["d_row"] = nc.dram_tensor("d_row", (ST, 1), I32, kind="Internal").ap()
        k["d_tile"] = nc.dram_tensor("d_tile", (ST, 1), I32, kind="Internal").ap()
        k["d_dl"] = nc.dram_tensor("d_dl", (ST, P), F32, kind="Internal").ap()
        k["d_ea"] = nc.dram_tensor("d_ea", (ST, EROWS, P), BF16, kind="Internal").ap()
        k["d_xw"] = nc.dram_tensor("d_xw", (NP, 2 * D), F32, kind="Internal").ap()
        for name, w in (("d_xl1", HEADS * HID), ("d_xr1", HEADS * HID), ("d_xl2", D)):
            k[name] = nc.dram_tensor(name, (NP, w), F32, kind="Internal").ap()

        w = {1: attention_weights(a, sb, 1, D, HEADS, HID), 2: attention_weights(a, sb, 2, HEADS * HID, 1, D)}
        setup(nc, a, k, w, sb, ps, sem)
        gated_steps(nc, a, k, sb, ps, sem)
        gated_nodes(nc, a, k, sb, ps, sem)
        project(nc, k, w[1], sb, ps, sem, 1, D, HEADS, HID)
        attention_steps(nc, k, w[1], sb, ps, sem, 1, HEADS, HID)
        attended_nodes(nc, a, k, sb, ps, sem)
        k["xr_parts"] = sb("xr_parts", [P, NT, PARTS, D], BF16)
        project(nc, k, w[2], sb, ps, sem, 2, HEADS * HID, 1, D)
        attention_steps(nc, k, w[2], sb, ps, sem, 2, 1, D)
        last_nodes(nc, a, k, sb, ps, sem, out)


class Chain:

    def __init__(self, eng, semaphore):
        self.eng, self.semaphore, self.n = eng, semaphore, 0

    def __call__(self, instruction):
        self.n += 1
        instruction.then_inc(self.semaphore, 1)
        self.eng.wait_ge(self.semaphore, self.n)


def split(link, nc, src, parts, rest):
    link(nc.vector.tensor_copy(parts[0], src))
    link(nc.vector.tensor_tensor(rest, src, parts[0], ALU.subtract))
    link(nc.vector.tensor_copy(parts[1], rest))
    link(nc.vector.tensor_tensor(rest, rest, parts[1], ALU.subtract))
    link(nc.vector.tensor_copy(parts[2], rest))


def pick(link, nc, dst, parts, masks, n):
    for i in range(PARTS):
        link(nc.vector.tensor_scalar(parts[i], parts[i], masks[0:n, i:i + 1], None, ALU.mult))
    link(nc.vector.tensor_tensor(parts[0], parts[0], parts[1], ALU.add))
    link(nc.vector.tensor_tensor(dst, parts[0], parts[2], ALU.add))


def attention_weights(a, sb, layer, din, heads, ch):
    W = heads * ch
    K = din // P
    return {
        "wl": sb(f"wl{layer}", [P, K, W]), "wr": sb(f"wr{layer}", [P, K, W]),
        "we": sb(f"we{layer}", [EROWS, W], BF16),
        "ebias": sb(f"ebias{layer}", [P, W]),
        "att_row": sb(f"att_row{layer}", [P, W]),
        "att_col": sb(f"att_col{layer}", [P, W // P]),
        "width": W,
    }


def setup(nc, a, k, w, sb, ps, sem):
    with ExitStack() as scope:
        def tmp(name, shape, dt=F32):
            return sb("s_" + name, shape, dt, scope)

        wa = tmp("wa", [P, 2, 2 * D])
        ba = tmp("ba", [P, 2 * D])
        beta = tmp("beta", [P, D])
        xt = tmp("xt", [P, 2, 2, P])
        xws = tmp("xws", [P, 2, 2 * D])
        dst_i = tmp("dst_i", [P, DC], I32)
        dst_f = tmp("dst_f", [P, DC])
        below = tmp("below", [P, DC])
        cnt = tmp("cnt", [P, NT])
        ea = tmp("ea", [P, DC, ED])
        easum = tmp("easum", [P, ED])
        ones = tmp("ones", [P, P])
        iot_i = tmp("iot_i", [P, P], I32)
        par_i = tmp("par_i", [P, 1], I32)
        stp_i = tmp("stp_i", [P, SW], I32)
        stp = tmp("stp", [P, SW])
        first = tmp("first", [P, NT + 1])
        need = tmp("need", [P, NT])
        need_i = tmp("need_i", [P, NT], I32)
        wins_i = tmp("wins_i", [P, NT], I32)
        sa = tmp("sa", [P, 16 + NT])
        sbb = tmp("sbb", [P, 16 + NT])
        uu = tmp("uu", [P, 1 + NT])
        dd = tmp("dd", [P, NT])
        ge = tmp("ge", [P, NT])
        gd = tmp("gd", [P, NT])
        tcol = tmp("tcol", [P, SW])
        rcol = tmp("rcol", [P, SW])
        toff = tmp("toff", [P, SW])
        rcol_i = tmp("rcol_i", [P, SW], I32)
        tcol_i = tmp("tcol_i", [P, SW], I32)
        dwin = tmp("dwin", [P, SW, P], I32)
        swin = tmp("swin", [P, SW, P], I32)
        ewin = tmp("ewin", [P, SW, P * ED])
        dwf = tmp("dwf", [P, SW, P])
        swf = tmp("swf", [P, SW, P])
        dcl = tmp("dcl", [P, SW, P])
        dlw = tmp("dlw", [P, SW, P])
        eparts = tmp("eparts", [P, SW, PARTS, ED * P], BF16)
        erest = tmp("erest", [P, ED * P])
        b2r = tmp("b2r", [PARTS, D])
        b2p = tmp("b2p", [PARTS, PARTS, D], BF16)
        b2q = tmp("b2q", [PARTS, D])
        wef = {c: tmp(f"wef{c}", [EROWS, w[c]["width"]]) for c in w}
        weq = tmp("weq", [EROWS, 512])
        wep = tmp("wep", [EROWS, PARTS, 512], BF16)

        xw_ps = ps("xw_ps", [P, 2, 512], scope)
        cnt_ps = ps("cnt_ps", [P, 512], scope)
        tr_ps = ps("tr_ps", [P, 3, 512], scope)
        eb_ps = ps("eb_ps", [P, 2, 512], scope)

        loaded_dst = sem("loaded_dst", scope)
        loaded = sem("loaded", scope)
        loaded_w = sem("loaded_w", scope)
        xt_in = [sem(f"xt_in{i}", scope) for i in range(2)]
        xw_made = sem("xw_made", scope)
        xw_taken = sem("xw_taken", scope)
        xw_out = [sem(f"xw_out{i}", scope) for i in range(2)]
        consts = sem("consts", scope)
        pool_own = sem("pool_own", scope)
        counted = sem("counted", scope)
        summed = sem("summed", scope)
        rows_known = sem("rows_known", scope)
        table_out = sem("table_out", scope)
        row_out = sem("row_out", scope)
        row_in = sem("row_in", scope)
        win_in = sem("win_in", scope)
        win_f = sem("win_f", scope)
        turned = sem("turned", scope)
        esplit = sem("esplit", scope)
        zeroed = sem("zeroed", scope)
        dve_own = sem("dve_own", scope)
        xb = sem("xb", scope)
        we_in = sem("we_in", scope)
        att_in = sem("att_in", scope)
        emean_made = sem("emean_made", scope)
        eb_made = sem("eb_made", scope)

        with nc.Block() as block:
            @block.sync
            def _(sp):
                sp.dma_start(dst_i[:], a["dst"].rearrange("(p c) one -> p (c one)", p=P)).then_inc(loaded_dst, 16)
                for c in range(2):
                    sp.dma_start(wa[:, c, 0:D], a["W1"][c * P:(c + 1) * P, :]).then_inc(loaded_w, 16)
                    sp.dma_start(wa[:, c, D:], a["Wg"][c * P:(c + 1) * P, :]).then_inc(loaded_w, 16)
                sp.dma_start(ba[:, 0:D], a["b1"].to_broadcast((P, D))).then_inc(loaded_w, 16)
                sp.dma_start(ba[:, D:], a["bg"].to_broadcast((P, D))).then_inc(loaded_w, 16)

                def load_xt(i):
                    if i.back(2).live:
                        sp.wait_ge(xw_made, i.back(2).done)
                    sp.dma_start(xt[:, i.slot(2)], a["xt"].rearrange("(c p) n -> p c n", p=P)[
                        :, :, bass.ds(i.s * P, P)]).then_inc(xt_in[i.slot(2)], 16)

                def body(i):
                    if i.live:
                        load_xt(i)
                    j = i.back(2)
                    if j.live:
                        sp.wait_ge(xw_taken, j.done)
                        sp.dma_start(k["d_xw"][bass.ds(j.s * P, P), :], xws[:, j.slot(2)]).then_inc(xw_out[j.slot(2)], 16)
                for c in w:
                    for g in range(PARTS * PARTS):
                        sp.dma_start(wef[c][g * ED:(g + 1) * ED, :], a[f"We{c}"]).then_inc(we_in, 16)
                run_steps(sp, body, 2, NT, 2)
                for c in w:
                    sp.dma_start(w[c]["wl"][:], a[f"Wl{c}"].rearrange("(c p) f -> p c f", p=P)).then_inc(att_in, 16)
                    sp.dma_start(w[c]["wr"][:], a[f"Wr{c}"].rearrange("(c p) f -> p c f", p=P)).then_inc(att_in, 16)
                    sp.dma_start(w[c]["att_row"][:], a[f"att{c}"].to_broadcast((P, w[c]["width"]))).then_inc(att_in, 16)
                    with nc.allow_non_contiguous_dma(reason="a column of attention weights"):
                        sp.dma_start(w[c]["att_col"][:], a[f"att{c}"].rearrange("one (c p) -> p (one c)", p=P)).then_inc(att_in, 16)
                sp.wait_ge(att_in, 16 * 4 * len(w))
                for i in range(2):
                    sp.wait_ge(xw_out[i], 16 * (NT // 2))

            @block.scalar
            def _(act):
                act.dma_start(ea[:], a["ea4"].rearrange("(p c) k -> p c k", p=P)).then_inc(loaded, 16)
                act.dma_start(beta[:], a["beta"].to_broadcast((P, D))).then_inc(loaded, 16)
                act.dma_start(k["xn"][:], a["x"].rearrange("(t p) f -> p t f", p=P)).then_inc(loaded, 16)
                act.dma_start(k["acc"][:, :, 0:D], a["x"].rearrange("(t p) f -> p t f", p=P)).then_inc(loaded, 16)
                act.dma_start(k["w1e"][:], a["W1"][D:D + DE, :]).then_inc(loaded, 16)
                act.dma_start(k["wge"][:], a["Wg"][D:D + DE, :]).then_inc(loaded, 16)
                act.dma_start(k["w2"][:], a["W2"].rearrange("(c p) f -> p c f", p=P)).then_inc(loaded, 16)
                act.dma_start(b2r[:], a["b2"].to_broadcast((PARTS, D))).then_inc(loaded, 16)
                act.wait_ge(rows_known, 2)
                with nc.allow_non_contiguous_dma(reason="a number a step"):
                    act.dma_start(k["d_row"].rearrange("(j p) one -> p (j one)", p=P), rcol_i[:]).then_inc(row_out, 16)
                    act.dma_start(k["d_tile"].rearrange("(j p) one -> p (j one)", p=P), tcol_i[:]).then_inc(row_out, 16)
                act.wait_ge(row_out, 32)
                act.dma_start(k["row_i"][:], k["d_row"].rearrange("s one -> one s")).then_inc(row_in, 16)
                act.wait_ge(zeroed, 1)
                act.dma_start(k["tile_i"][0:1, U:], k["d_tile"].rearrange("s one -> one s")).then_inc(row_in, 16)
                act.wait_ge(win_f, 1)
                act.dma_start(k["d_dl"].rearrange("(j p) e -> p j e", p=P), dlw[:]).then_inc(table_out, 16)
                for j in range(SW):
                    act.wait_ge(esplit, j + 1)
                    for i in range(PARTS):
                        act.dma_start(
                            k["d_ea"][j * P:(j + 1) * P, i * PARTS * ED:(i + 1) * PARTS * ED, :].rearrange("s r e -> s (r e)"),
                            eparts[:, j].rearrange("p a b -> p (a b)")).then_inc(table_out, 16)
                act.wait_ge(row_in, 32)
                act.wait_ge(table_out, 16 * (1 + SW * PARTS))
                act.wait_ge(loaded, 16 * 8)

            @block.gpsimd
            def _(pool):
                nc.gpsimd.iota(iot_i[:], [[1, P]], base=0, channel_multiplier=0)
                nc.gpsimd.iota(par_i[:], [[0, 1]], base=0, channel_multiplier=1)
                nc.gpsimd.iota(stp_i[:], [[P, SW]], base=0, channel_multiplier=1)
                nc.gpsimd.memset(ones[:], 1.0)
                nc.gpsimd.memset(k["den"][:], 1.0)
                nc.gpsimd.memset(k["ident"][:], 0.0)
                nc.gpsimd.memset(k["bigi"][:], 0.0).then_inc(pool_own, 1)
                pool.wait_ge(pool_own, 1)
                nc.gpsimd.affine_select(out=k["ident"][:], in_=k["ident"][:], compare_op=ALU.not_equal, fill=1.0,
                                        base=0, pattern=[[-1, P]], channel_multiplier=1)
                nc.gpsimd.affine_select(out=k["bigi"][:], in_=k["bigi"][:], compare_op=ALU.not_equal, fill=BIG,
                                        base=0, pattern=[[-1, P]], channel_multiplier=1).then_inc(consts, 1)
                pool.wait_ge(rows_known, 1)
                for j in range(SW):
                    at = bass.IndirectOffsetOnAxis(ap=rcol_i[:, j:j + 1], axis=0)
                    nc.gpsimd.indirect_dma_start(out=dwin[:, j], out_offset=None, in_=a["dst"], in_offset=at).then_inc(win_in, 16)
                    nc.gpsimd.indirect_dma_start(out=swin[:, j], out_offset=None, in_=a["src"], in_offset=at).then_inc(win_in, 16)
                    nc.gpsimd.indirect_dma_start(out=ewin[:, j], out_offset=None, in_=a["ea4"], in_offset=at).then_inc(win_in, 16)
                pool.wait_ge(loaded, 16 * 8)
                for t in range(NT):
                    last = nc.gpsimd.tensor_tensor(k["xn"][:, t], k["xn"][:, t], beta[:], ALU.add)
                last.then_inc(xb, 1)

            @block.tensor
            def _(pe):
                pe.wait_ge(loaded_w, 16 * 6)

                def body(i):
                    pe.wait_ge(xt_in[i.slot(2)], i.turns(2) * 16)
                    if i.back(2).live:
                        pe.wait_ge(xw_taken, i.back(2).done)
                    for c in range(2):
                        last = nc.tensor.matmul(xw_ps[:, i.slot(2)], xt[:, i.slot(2), c], wa[:, c], start=(c == 0), stop=(c == 1))
                    last.then_inc(xw_made, 1)
                run_steps(pe, body, 2, NT, 0)
                pe.wait_ge(consts, 1)
                pe.wait_ge(counted, 1)
                nc.tensor.matmul(cnt_ps[:, 0:NT], ones[:], cnt[:], start=True, stop=True)
                nc.tensor.matmul(cnt_ps[0:ED, P:2 * P], easum[:], ones[:], start=True, stop=True).then_inc(summed, 1)
                pe.wait_ge(we_in, 16 * PARTS * PARTS * len(w))
                pe.wait_ge(emean_made, 1)
                for c in w:
                    last = nc.tensor.matmul(eb_ps[:, c - 1, 0:w[c]["width"]], k["emean"][:], wef[c][0:ED, :], start=True, stop=True)
                last.then_inc(eb_made, 1)
                pe.wait_ge(win_f, 1)
                for n, src in enumerate((dlw, swf, dcl)):
                    for j in range(SW):
                        last = nc.tensor.transpose(tr_ps[:, n, j * P:(j + 1) * P], src[:, j], k["ident"][:])
                last.then_inc(turned, 1)

            @block.vector
            def _(dve):
                link = Chain(dve, dve_own)
                nc.vector.memset(k["tile_i"][:], 0).then_inc(zeroed, 1)
                nc.vector.memset(k["ones3"][:], 1.0)
                nc.vector.memset(sa[:], 0.0)
                nc.vector.memset(uu[:], 0.0)
                link(nc.vector.memset(sbb[:], 0.0))
                dve.wait_ge(loaded_dst, 16)
                link(nc.vector.tensor_copy(dst_f[:], dst_i[:]))
                for t in range(NT):
                    last = nc.vector.tensor_scalar(below[:], dst_f[:], float(t * P), None, ALU.is_lt, ALU.add,
                                                   accum_out=cnt[:, t:t + 1])
                    link(last)
                dve.wait_ge(loaded, 16 * 8)
                nc.vector.tensor_reduce(easum[:], ea[:].rearrange("p c k -> p k c"), AX.X, ALU.add).then_inc(counted, 1)

                dve.wait_ge(consts, 1)
                link(nc.vector.tensor_copy(k["node_row"][:], iot_i[:]))
                link(nc.vector.tensor_copy(k["part"][:], par_i[:]))
                link(nc.vector.tensor_copy(stp[:], stp_i[:]))
                for g, size in ((0, 1), (PARTS, PARTS * ED)):
                    for i in range(PARTS):
                        m = k["sel"][:, g + i:g + i + 1]
                        link(nc.vector.tensor_scalar(m, k["part"][:], float(i * size), None, ALU.is_ge))
                        link(nc.vector.tensor_scalar(below[:, 0:1], k["part"][:], float((i + 1) * size), None, ALU.is_lt))
                        link(nc.vector.tensor_tensor(m, m, below[:, 0:1], ALU.mult))
                split(link, nc, b2r[:], [b2p[:, i] for i in range(PARTS)], b2q[:])
                pick(link, nc, k["b2s"][:], [b2p[:, i] for i in range(PARTS)], k["sel"], PARTS)

                def take(i):
                    dve.wait_ge(xw_made, i.done)
                    if i.back(2).live:
                        dve.wait_ge(xw_out[i.slot(2)], i.back(2).turns(2) * 16)
                    nc.vector.tensor_tensor(xws[:, i.slot(2)], xw_ps[:, i.slot(2)], ba[:], ALU.add).then_inc(xw_taken, 1)
                dve.wait_ge(loaded_w, 16 * 6)
                run_steps(dve, take, 2, NT, 0)

                dve.wait_ge(summed, 1)
                link(nc.vector.tensor_copy(first[:, 0:NT], cnt_ps[:, 0:NT]))
                link(nc.vector.memset(first[:, NT:], float(E)))
                link(nc.vector.tensor_scalar(k["emean"][:], cnt_ps[0:ED, P:2 * P], 1.0 / E, None, ALU.mult))
                link(nc.vector.tensor_tensor(need[:], first[:, 1:], first[:, 0:NT], ALU.subtract))
                link(nc.vector.tensor_scalar(need_i[:], need[:], float(P - 1), None, ALU.add))
                link(nc.vector.tensor_scalar(wins_i[:], need_i[:], P.bit_length() - 1, None, ALU.arith_shift_right))
                link(nc.vector.tensor_copy(sa[:, 17:], wins_i[:, 0:NT - 1]))
                cur, other = sa, sbb
                for d in (1, 2, 4, 8, 16):
                    link(nc.vector.tensor_tensor(other[:, 16:], cur[:, 16:], cur[:, 16 - d:16 + NT - d], ALU.add))
                    cur, other = other, cur
                starts = cur[:, 16:]
                link(nc.vector.tensor_scalar(uu[:, 1:], starts, -float(P), None, ALU.mult))
                link(nc.vector.tensor_tensor(uu[:, 1:], uu[:, 1:], first[:, 0:NT], ALU.add))
                link(nc.vector.tensor_tensor(dd[:], uu[:, 1:], uu[:, 0:NT], ALU.subtract))
                for j in range(SW):
                    link(nc.vector.tensor_scalar(ge[:], starts, stp[:, j:j + 1], None, ALU.is_le, ALU.add,
                                                 accum_out=tcol[:, j:j + 1]))
                    link(nc.vector.tensor_tensor_reduce(gd[:], ge[:], dd[:], 1.0, 0.0, ALU.mult, ALU.add,
                                                        rcol[:, j:j + 1]))
                link(nc.vector.scalar_tensor_tensor(rcol[:], stp[:], float(P), rcol[:], ALU.mult, ALU.add))
                nc.vector.tensor_scalar(rcol_i[:], rcol[:], float(RMAX), None, ALU.min).then_inc(rows_known, 1)
                link(nc.vector.tensor_scalar(toff[:], tcol[:], float(P), -float(P), ALU.mult, ALU.add))
                nc.vector.tensor_scalar(tcol_i[:], tcol[:], -1.0, None, ALU.add).then_inc(rows_known, 1)
                nc.vector.tensor_copy(gd[:, 0:1], k["sel"][:, 0:1]).then_inc(emean_made, 1)

                dve.wait_ge(we_in, 16 * PARTS * PARTS * len(w))
                for c in w:
                    width = w[c]["width"]
                    parts = [wep[:, i, 0:width] for i in range(PARTS)]
                    split(link, nc, wef[c][:], parts, weq[:, 0:width])
                    pick(link, nc, w[c]["we"][:], parts, k["sel"][:, PARTS:], EROWS)

                dve.wait_ge(win_in, 16 * 3 * SW)
                link(nc.vector.tensor_copy(dwf[:], dwin[:]))
                link(nc.vector.tensor_copy(swf[:], swin[:]))
                link(nc.vector.tensor_scalar(dcl[:], dwf[:], float(N - 1), None, ALU.min))
                for j in range(SW):
                    last = nc.vector.tensor_scalar(dlw[:, j], dwf[:, j], toff[:, j:j + 1], None, ALU.subtract)
                last.then_inc(win_f, 1)
                dve.wait_ge(turned, 1)
                link(nc.vector.tensor_copy(k["dl"][:], tr_ps[:, 0]))
                link(nc.vector.tensor_copy(k["idx"][:, :, 0], tr_ps[:, 1]))
                link(nc.vector.tensor_copy(k["idx"][:, :, 1], tr_ps[:, 2]))
                for j in range(SW):
                    parts = [eparts[:, j, i].rearrange("p (k e) -> p k e", e=P) for i in range(PARTS)]
                    src = ewin[:, j].rearrange("p (e k) -> p k e", k=ED)
                    split(link, nc, src, parts, erest[:].rearrange("p (k e) -> p k e", e=P))
                    nc.vector.tensor_copy(gd[:, 0:1], ge[:, 0:1]).then_inc(esplit, 1)
                dve.wait_ge(eb_made, 1)
                for c in w:
                    link(nc.vector.tensor_copy(w[c]["ebias"][:], eb_ps[:, c - 1, 0:w[c]["width"]]))
                dve.wait_ge(xb, 1)


def gated_steps(nc, a, k, sb, ps, sem):
    RING = 4
    with ExitStack() as scope:
        ix = sb("g_ix", [P, 2, IRING, 2], I32, scope)
        dl = sb("g_dl", [P, 2, IRING], F32, scope)
        xw = sb("g_xw", [P, RING, 2 * D], F32, scope)
        eat = sb("g_eat", [DE, RING, P], F32, scope)
        rt = sb("g_rt", [P, 2, 2 * P], F32, scope)
        gate = sb("g_gate", [P, 4, D], F32, scope)
        msg = sb("g_msg", [P, 2, D], F32, scope)
        hot = sb("g_hot", [P, 2, P], F32, scope)
        hid_ps = ps("hid_ps", [P, 2, 512], scope)
        gate_ps = ps("gate_ps", [P, 2, 512], scope)
        core_ps = ps("core_ps", [P, 2, 512], scope)
        sum_ps = ps("sum_ps", [P, 2, 512], scope)

        ix_ready = sem("g_ix_ready", scope)
        xw_in = [sem(f"g_xw_in{i}", scope) for i in range(RING)]
        ea_in = [sem(f"g_ea_in{i}", scope) for i in range(RING)]
        hid_made = sem("g_hid_made", scope)
        relu_made = sem("g_relu_made", scope)
        gate_in = sem("g_gate_in", scope)
        gate_made = sem("g_gate_made", scope)
        core_made = sem("g_core_made", scope)
        msg_made = sem("g_msg_made", scope)
        sum_made = sem("g_sum_made", scope)
        added = sem("g_added", scope)

        with nc.Block() as block:
            @block.sync
            def _(sp):
                regs = [sp.alloc_register(f"g_row{i}") for i in range(U)]
                rows = [None] * U

                def head(it):
                    sp.load(regs, k["row_i"][0:1, bass.ds(it * U, U)])
                    for i in range(U):
                        rows[i] = sp.snap(regs[i], min_val=0, max_val=RMAX)

                def body(i):
                    if i.back(RING).live:
                        sp.wait_ge(hid_made, i.back(RING).done)
                        nc.sync.nop(nofuse=True)
                    sp.dma_start(eat[:, i.slot(RING)], a["ea64t"][:, bass.ds(rows[i.k], P)]).then_inc(ea_in[i.slot(RING)], 16)
                run_steps(sp, body, U, STEPS, 0, head)

            @block.gpsimd
            def _(pool):
                def body(i):
                    half = i.k // IRING % 2
                    if i.k % IRING == 0:
                        if i.back(2 * IRING).live:
                            pool.wait_ge(msg_made, i.back(IRING + 1).done)
                        nc.gpsimd.tensor_copy(dl[:, half], k["dl"][:, bass.ds(i.s, IRING)])
                        nc.gpsimd.tensor_copy(ix[:, half], k["idx"][:, bass.ds(i.s, IRING), :]).then_inc(ix_ready, 1)
                        pool.wait_ge(ix_ready, i.turns(IRING))
                        nc.gpsimd.nop(nofuse=True)
                    if i.back(RING).live:
                        pool.wait_ge(gate_in, i.back(RING).done)
                        nc.gpsimd.nop(nofuse=True)
                    at = bass.IndirectOffsetOnAxis(ap=ix[:, half, i.k % IRING, 0:1], axis=0)
                    nc.gpsimd.indirect_dma_start(out=xw[:, i.slot(RING)], out_offset=None, in_=k["d_xw"],
                                                 in_offset=at).then_inc(xw_in[i.slot(RING)], 16)
                run_steps(pool, body, U, STEPS, 0)

            @block.tensor
            def _(pe):
                def body(i):
                    if i.live:
                        pe.wait_ge(ea_in[i.slot(RING)], i.turns(RING) * 16)
                        pe.wait_ge(xw_in[i.slot(RING)], i.turns(RING) * 16)
                        if i.back(2).live:
                            pe.wait_ge(gate_in, i.back(2).done)
                        e = eat[:, i.slot(RING)]
                        for c in range(2):
                            cols = slice(c * P, (c + 1) * P)
                            nc.tensor.matmul(hid_ps[:, i.slot(2), cols], xw[:, i.slot(RING), cols], k["ident"][:],
                                             is_transpose=True, start=True, stop=False, skip_group_check=True)
                            nc.tensor.matmul(hid_ps[:, i.slot(2), cols], k["w1e"][:, cols], e,
                                             start=False, stop=True, skip_group_check=True)
                        nc.tensor.matmul(gate_ps[:, i.slot(2), 0:D], e, k["wge"][:], start=True, stop=True).then_inc(hid_made, 1)
                    j = i.back(1)
                    if j.live:
                        pe.wait_ge(relu_made, j.done)
                        o = core_ps[:, j.slot(2), 0:D]
                        for c in range(2):
                            nc.tensor.matmul(o, rt[:, j.slot(2), c * P:(c + 1) * P], k["w2"][:, c], start=(c == 0), stop=False)
                        nc.tensor.matmul(o, k["ones3"][:], k["b2s"][:], start=False, stop=True).then_inc(core_made, 1)
                    j = i.back(2)
                    if j.live:
                        pe.wait_ge(msg_made, j.done)
                        if j.back(2).live:
                            pe.wait_ge(added, j.back(2).done)
                        nc.tensor.matmul(sum_ps[:, j.slot(2), 0:D], hot[:, j.slot(2)], msg[:, j.slot(2)],
                                         start=True, stop=True).then_inc(sum_made, 1)
                run_steps(pe, body, U, STEPS, 2)

            @block.scalar
            def _(act):
                def body(i):
                    act.wait_ge(hid_made, i.done)
                    nc.scalar.activation(rt[:, i.slot(2)], hid_ps[:, i.slot(2), 0:2 * P], ACT.Relu).then_inc(relu_made, 1)
                    act.wait_ge(gate_in, i.done)
                    nc.scalar.activation(gate[:, i.slot(4)], gate[:, i.slot(4)], ACT.Sigmoid).then_inc(gate_made, 1)
                run_steps(act, body, U, STEPS, 0)

            @block.vector
            def _(dve):
                LAG = 3
                regs = [dve.alloc_register(f"g_tile{i}") for i in range(U)]
                tiles = [None] * U

                def head(it):
                    dve.load(regs, k["tile_i"][0:1, bass.ds(it * U + (U - LAG), U)])
                    for i in range(U):
                        tiles[i] = dve.snap(regs[i], min_val=0, max_val=NT - 1)

                def body(i):
                    if i.live:
                        dve.wait_ge(hid_made, i.done)
                        nc.vector.tensor_tensor(gate[:, i.slot(4)], gate_ps[:, i.slot(2), 0:D], xw[:, i.slot(RING), D:],
                                                ALU.add).then_inc(gate_in, 1)
                    j = i.back(LAG)
                    if j.live:
                        dve.wait_ge(sum_made, j.done)
                        if j.back(1).live:
                            dve.wait_ge(added, j.back(1).done)
                        row = tile_of(k["acc"], tiles[i.k], D)
                        nc.vector.tensor_tensor(row, row, sum_ps[:, j.slot(2), 0:D], ALU.add).then_inc(added, 1)
                    j = i.back(1)
                    if j.live:
                        if j.k % IRING == 0:
                            dve.wait_ge(ix_ready, j.turns(IRING))
                        nc.vector.tensor_scalar(hot[:, j.slot(2)], k["node_row"][:], dl[:, j.k // IRING % 2, j.k % IRING:j.k % IRING + 1],
                                                None, ALU.is_equal)
                        dve.wait_ge(core_made, j.done)
                        dve.wait_ge(gate_made, j.done)
                        nc.vector.tensor_tensor(msg[:, j.slot(2)], core_ps[:, j.slot(2), 0:D], gate[:, j.slot(4)],
                                                ALU.mult).then_inc(msg_made, 1)
                run_steps(dve, body, U, STEPS, LAG, head)


def spread(k, nc, dve, act_sem, dve_sem, link, count):
    for t in range(NT):
        last = nc.vector.bn_aggr(k["mv"][:, t], k["st"][:, t])
    link(last)
    nc.vector.tensor_scalar(k["rstd"][:], k["mv"][:, :, 1], EPS, None, ALU.add).then_inc(dve_sem, 1)
    dve.wait_ge(act_sem, count)
    link(nc.vector.reciprocal(k["rstd"][:], k["rstd"][:]))


def root(k, nc, act, act_sem, dve_sem, count):
    act.wait_ge(dve_sem, count)
    nc.scalar.activation(k["rstd"][:], k["rstd"][:], ACT.Sqrt).then_inc(act_sem, 1)


def tile_of(buf, t, width):
    return buf[:, bass.ds(t, 1), 0:width].rearrange("p t f -> p (t f)")


class Normed:

    def __init__(self, nc, k, n, sb, sem, own, gain):
        self.nc, self.k, self.gain = nc, k, gain
        self.y = sb(n + "y", [P, 4, D], F32, own)
        self.normed = sem(n + "normed", own)
        self.scaled = sem(n + "scaled", own)
        self.shifted = sem(n + "shifted", own)
        self.stats = sem(n + "stats", own)

    def vector(self, dve):
        nc, k, y = self.nc, self.k, self.y

        def body(i):
            if i.live:
                if i.back(4).live:
                    dve.wait_ge(self.shifted, i.back(4).done)
                nc.vector.tensor_scalar(y[:, i.slot(4)], tile_of(k["acc"], i.s, D), k["mv"][:, bass.ds(i.s, 1), 0],
                                        k["rstd"][:, bass.ds(i.s, 1)], ALU.subtract, ALU.mult).then_inc(self.normed, 1)
            j = i.back(2)
            if j.live:
                dve.wait_ge(self.scaled, j.done)
                nc.vector.tensor_tensor(tile_of(k["acc"], j.s, D), y[:, j.slot(4)], tile_of(k["xn"], j.s, D),
                                        ALU.add).then_inc(self.shifted, 1)
            j = i.back(3)
            if j.live:
                dve.wait_ge(self.shifted, j.done)
                nc.vector.bn_stats(tile_of(k["st"], j.s, 6), tile_of(k["acc"], j.s, D)).then_inc(self.stats, 1)
        run_steps(dve, body, 4, NT - NT % 4, 0, peel=2)
        for extra in range(NT % 4 + 3):
            body(Step(NT // 4, extra, 4, NT))
        dve.wait_ge(self.stats, NT)

    def pool(self, pool):
        nc, y = self.nc, self.y

        def body(i):
            pool.wait_ge(self.normed, i.done)
            nc.gpsimd.tensor_tensor(y[:, i.slot(4)], y[:, i.slot(4)], self.gain[:], ALU.mult).then_inc(self.scaled, 1)
        run_steps(pool, body, 4, NT - NT % 4, 0)
        for extra in range(NT % 4):
            body(Step(NT // 4, extra, 4, NT))


def gated_nodes(nc, a, k, sb, ps, sem):
    with ExitStack() as own:
        gamma = sb("gamma", [P, D], F32, own)
        loaded = sem("gn_loaded", own)
        stats = sem("gn_stats", own)
        dve_own = sem("gn_own", own)
        to_root = sem("gn_to_root", own)
        rooted = sem("gn_rooted", own)
        normed = Normed(nc, k, "gn_n_", sb, sem, own, gamma)
        with nc.Block() as block:
            @block.sync
            def _(sp):
                sp.dma_start(gamma[:], a["gamma"].to_broadcast((P, D))).then_inc(loaded, 16)

            @block.scalar
            def _(act):
                for n in range(2):
                    root(k, nc, act, rooted, to_root, n + 1)

            @block.gpsimd
            def _(pool):
                pool.wait_ge(loaded, 16)
                normed.pool(pool)

            @block.vector
            def _(dve):
                link = Chain(dve, dve_own)

                def stat(i):
                    nc.vector.bn_stats(tile_of(k["st"], i.s, 6), tile_of(k["acc"], i.s, D)).then_inc(stats, 1)
                run_steps(dve, stat, 2, NT, 0)
                dve.wait_ge(stats, NT)
                spread(k, nc, dve, rooted, to_root, link, 1)
                normed.vector(dve)
                spread(k, nc, dve, rooted, to_root, link, 2)


def attended_nodes(nc, a, k, sb, ps, sem):
    W = HEADS * HID
    with ExitStack() as own:
        bias = sb("an_bias", [P, W], F32, own)
        loaded = sem("an_loaded", own)
        stats = sem("an_stats", own)
        dve_own = sem("an_own", own)
        to_root = sem("an_to_root", own)
        rooted = sem("an_rooted", own)
        divided = sem("an_divided", own)
        with nc.Block() as block:
            @block.sync
            def _(sp):
                sp.dma_start(bias[:], a["cb1"].to_broadcast((P, W))).then_inc(loaded, 16)

            @block.scalar
            def _(act):
                root(k, nc, act, rooted, to_root, 1)

            @block.vector
            def _(dve):
                link = Chain(dve, dve_own)
                den = k["den"][:].rearrange("p t h -> p (t h)")
                link(nc.vector.tensor_scalar(den, den, 1e-16, None, ALU.add))
                link(nc.vector.reciprocal(k["rden"][:], den))
                dve.wait_ge(loaded, 16)

                def body(i):
                    if i.live:
                        for h in range(HEADS):
                            row = k["acc"][:, bass.ds(i.s, 1), h * HID:(h + 1) * HID].rearrange("p t f -> p (t f)")
                            last = nc.vector.scalar_tensor_tensor(row, row, k["rden"][:, bass.ds(i.s * HEADS + h, 1)],
                                                                  bias[:, h * HID:(h + 1) * HID], ALU.mult, ALU.add)
                        last.then_inc(divided, 1)
                    j = i.back(1)
                    if j.live:
                        dve.wait_ge(divided, j.done)
                        nc.vector.bn_stats(tile_of(k["st"], j.s, 6), tile_of(k["acc"], j.s, W)).then_inc(stats, 1)
                run_steps(dve, body, 2, NT, 1)
                dve.wait_ge(stats, NT)
                spread(k, nc, dve, rooted, to_root, link, 1)
                link(nc.vector.memset(k["den"][:], 1.0))


def project(nc, k, w, sb, ps, sem, layer, din, heads, ch):
    W = heads * ch
    K = din // P
    n = f"p{layer}_"
    ahead = layer - 1
    with ExitStack() as own:
        xs = sb(n + "xs", [P, 2, din], F32, own)
        xt = sb(n + "xt", [P, 2, din], F32, own)
        xr = sb(n + "xr", [P, 2, W], F32, own)
        xre = sb(n + "xre", [P, 2, W], F32, own)
        own_m = sb(n + "own_m", [P, 2, W], F32, own)
        leaky = sb(n + "leaky", [P, 2, W], F32, own)
        prod = sb(n + "prod", [P, W], F32, own)
        q = sb(n + "q", [P, 2, heads], F32, own)
        if layer == 2:
            left = sb(n + "left", [P, 2, W], F32, own)
            part_made = [sem(n + f"part_made{i}", own) for i in range(4)]
            gain = sb(n + "gain", [P, din], F32, own)
            offset = sb(n + "offset", [P, din], F32, own)
            ya = sb(n + "ya", [P, 2, din], F32, own)
            yb = sb(n + "yb", [P, 2, din], F32, own)
        xt_ps = ps(n + "xt_ps", [P, 2, 512], own)
        xl_ps = ps(n + "xl_ps", [P, 2, 512], own)
        xr_ps = ps(n + "xr_ps", [P, 2, 512], own)
        loaded = sem(n + "loaded", own)
        normed = sem(n + "normed", own)
        gained = sem(n + "gained", own)
        offsetted = sem(n + "offsetted", own)
        lowed = sem(n + "lowed", own)
        exped = sem(n + "exped", own)
        x_made = sem(n + "x_made", own)
        x_kept = sem(n + "x_kept", own)
        turned = sem(n + "turned", own)
        xt_made = sem(n + "xt_made", own)
        rows_made = sem(n + "rows_made", own)
        l_taken = sem(n + "l_taken", own)
        r_taken = sem(n + "r_taken", own)
        summed = sem(n + "summed", own)
        xre_made = sem(n + "xre_made", own)
        leaked = sem(n + "leaked", own)
        scored = sem(n + "scored", own)
        m_set = sem(n + "m_set", own)
        l_out = sem(n + "l_out", own)
        r_out = [sem(n + f"r_out{i}", own) for i in range(2)]

        def part_of(i, part):
            return k["xr_parts"][:, bass.ds(i.s, 1), part].rearrange("p t f -> p (t f)")

        with nc.Block() as block:
            @block.sync
            def _(sp):
                if layer == 2:
                    sp.dma_start(gain[:], k["in"]["g1"].to_broadcast((P, din))).then_inc(loaded, 16)
                    sp.dma_start(offset[:], k["in"]["be1"].to_broadcast((P, din))).then_inc(loaded, 16)

                def body(i):
                    sp.wait_ge(l_taken, i.done)
                    nc.sync.nop(nofuse=True)
                    sp.dma_start(k[f"d_xl{layer}"][bass.ds(i.s * P, P), :], tile_of(k["acc"], i.s, W)).then_inc(l_out, 16)
                    if layer == 1:
                        sp.wait_ge(r_taken, i.done)
                        nc.sync.nop(nofuse=True)
                        sp.dma_start(k["d_xr1"][bass.ds(i.s * P, P), :], xr[:, i.slot(2)]).then_inc(r_out[i.slot(2)], 16)
                run_steps(sp, body, 2, NT, 0)
                sp.wait_ge(l_out, 16 * NT)
                if layer == 1:
                    for i in range(2):
                        sp.wait_ge(r_out[i], 16 * (NT // 2))

            @block.tensor
            def _(pe):
                def body(i):
                    if i.live:
                        pe.wait_ge(x_made, i.done)
                        for c in range(K):
                            last = nc.tensor.transpose(xt_ps[:, i.slot(2), c * P:(c + 1) * P], xs[:, i.slot(2), c * P:(c + 1) * P],
                                                       k["ident"][:])
                        last.then_inc(turned, 1)
                    j = i.back(1)
                    if j.live:
                        pe.wait_ge(xt_made, j.done)
                        if j.back(2).live:
                            pe.wait_ge(r_taken, j.back(2).done)
                        for bank, m in ((xl_ps, w["wl"]), (xr_ps, w["wr"])):
                            for c in range(K):
                                last = nc.tensor.matmul(bank[:, j.slot(2), 0:W], xt[:, j.slot(2), c * P:(c + 1) * P], m[:, c],
                                                        start=(c == 0), stop=(c == K - 1))
                        last.then_inc(rows_made, 1)
                run_steps(pe, body, 2, NT, 1)

            @block.scalar
            def _(act):
                def body(i):
                    if layer == 2 and i.live:
                        act.wait_ge(lowed, i.done)
                        nc.scalar.activation(yb[:, i.slot(2)], yb[:, i.slot(2)], ACT.Exp).then_inc(exped, 1)
                    i = i.back(ahead)
                    if i.live:
                        act.wait_ge(turned, i.done)
                        if i.back(2).live:
                            act.wait_ge(rows_made, i.back(2).done)
                        nc.scalar.copy(xt[:, i.slot(2)], xt_ps[:, i.slot(2), 0:din]).then_inc(xt_made, 1)
                        if layer == 1:
                            nc.scalar.copy(tile_of(k["xn"], i.s, D), xs[:, i.slot(2)]).then_inc(x_kept, 1)
                    j = i.back(1)
                    if j.live:
                        act.wait_ge(rows_made, j.done)
                        nc.scalar.copy(tile_of(k["acc"], j.s, W), xl_ps[:, j.slot(2), 0:W]).then_inc(l_taken, 1)
                        if j.back(2).live:
                            act.wait_ge(xre_made, j.back(2).done)
                            if layer == 1:
                                act.wait_ge(r_out[j.slot(2)], j.back(2).turns(2) * 16)
                            else:
                                act.wait_ge(part_made[1], j.back(2).done)
                        nc.scalar.copy(xr[:, j.slot(2)], xr_ps[:, j.slot(2), 0:W]).then_inc(r_taken, 1)
                        if layer == 2:
                            act.wait_ge(r_taken, j.done)
                            nc.scalar.copy(part_of(j, 0), xr[:, j.slot(2)]).then_inc(part_made[0], 1)
                    j = j.back(1)
                    if layer == 2 and j.live:
                        act.wait_ge(part_made[1], j.done)
                        nc.scalar.copy(part_of(j, 1), left[:, j.slot(2)]).then_inc(part_made[2], 1)
                run_steps(act, body, 2, NT, 1 + 2 * ahead, peel=3)

            @block.gpsimd
            def _(pool):
                def body(i):
                    if layer == 2 and i.live:
                        pool.wait_ge(offsetted, i.done)
                        if i.back(2).live:
                            pool.wait_ge(x_made, i.back(2).done)
                        nc.gpsimd.nop(nofuse=True)
                        nc.gpsimd.tensor_scalar(yb[:, i.slot(2)], ya[:, i.slot(2)], 0.0, None, ALU.min).then_inc(lowed, 1)
                    j = i.back(1 + ahead)
                    if j.live:
                        pool.wait_ge(xre_made, j.done)
                        pool.wait_ge(l_taken, j.done)
                        if j.back(2).live:
                            pool.wait_ge(leaked, j.back(2).done)
                        nc.gpsimd.tensor_tensor(own_m[:, j.slot(2)], tile_of(k["acc"], j.s, W), xre[:, j.slot(2)],
                                                ALU.add).then_inc(summed, 1)
                    if layer == 2 and j.live:
                        pool.wait_ge(part_made[0], j.done)
                        if j.back(2).live:
                            pool.wait_ge(part_made[3], j.back(2).done)
                        nc.gpsimd.tensor_tensor(left[:, j.slot(2)], xr[:, j.slot(2)], part_of(j, 0), ALU.subtract).then_inc(part_made[1], 1)
                    j = j.back(1)
                    if layer == 2 and j.live:
                        pool.wait_ge(part_made[2], j.done)
                        nc.gpsimd.tensor_tensor(part_of(j, 2), left[:, j.slot(2)], part_of(j, 1), ALU.subtract).then_inc(part_made[3], 1)
                run_steps(pool, body, 2, NT, 1 + 2 * ahead, peel=3)

            @block.vector
            def _(dve):
                if layer == 2:
                    dve.wait_ge(loaded, 32)

                def scaled(i):
                    out = xs if layer == 1 else ya
                    if i.back(2).live:
                        if layer == 1:
                            dve.wait_ge(turned, i.back(2).done)
                            dve.wait_ge(x_kept, i.back(2).done)
                        else:
                            dve.wait_ge(x_made, i.back(2).done)
                    nc.vector.tensor_scalar(out[:, i.slot(2)], tile_of(k["acc"], i.s, din), k["mv"][:, bass.ds(i.s, 1), 0],
                                            k["rstd"][:, bass.ds(i.s, 1)], ALU.subtract, ALU.mult
                                            ).then_inc(x_made if layer == 1 else normed, 1)

                def shifted(i):
                    dve.wait_ge(normed, i.done)
                    nc.vector.tensor_tensor(ya[:, i.slot(2)], ya[:, i.slot(2)], gain[:], ALU.mult).then_inc(gained, 1)
                    dve.wait_ge(gained, i.done)
                    nc.vector.tensor_tensor(ya[:, i.slot(2)], ya[:, i.slot(2)], offset[:], ALU.add).then_inc(offsetted, 1)

                def elu(i):
                    dve.wait_ge(exped, i.done)
                    if i.back(2).live:
                        dve.wait_ge(turned, i.back(2).done)
                    nc.vector.scalar_tensor_tensor(xs[:, i.slot(2)], yb[:, i.slot(2)], -1.0, ya[:, i.slot(2)],
                                                   ALU.add, ALU.max).then_inc(x_made, 1)

                def body(i):
                    if i.live:
                        scaled(i)
                        if layer == 2:
                            shifted(i)
                    i = i.back(ahead)
                    if i.live and layer == 2:
                        elu(i)
                    j = i.back(2)
                    if j.live:
                        dve.wait_ge(r_taken, j.done)
                        if j.back(2).live:
                            dve.wait_ge(summed, j.back(2).done)
                        nc.vector.tensor_tensor(xre[:, j.slot(2)], xr[:, j.slot(2)], w["ebias"][:], ALU.add).then_inc(xre_made, 1)
                    j = i.back(3)
                    if j.live:
                        dve.wait_ge(summed, j.done)
                        m = own_m[:, j.slot(2)]
                        nc.vector.scalar_tensor_tensor(leaky[:, j.slot(2)], m, SLOPE, m, ALU.mult, ALU.max).then_inc(leaked, 1)
                        dve.wait_ge(leaked, j.done)
                        for h in range(heads):
                            cols = slice(h * ch, (h + 1) * ch)
                            last = nc.vector.scalar_tensor_tensor(prod[:, cols], leaky[:, j.slot(2), cols], -1.0,
                                                                  w["att_row"][:, cols], ALU.mult, ALU.mult,
                                                                  accum_out=q[:, j.slot(2), h:h + 1])
                        last.then_inc(scored, 1)
                        dve.wait_ge(scored, j.done)
                        nc.vector.tensor_scalar(tile_of(k["low"], j.s, heads), q[:, j.slot(2)], 0.0, None, ALU.add).then_inc(m_set, 1)
                run_steps(dve, body, 2, NT, 3 + ahead, peel=3)


def attention_steps(nc, k, w, sb, ps, sem, layer, heads, ch):
    W = heads * ch
    K = W // P
    HP = heads * P
    RING = 8
    ahead = layer - 1
    both = 3 * P if layer == 1 else 0
    n = f"t{layer}_"
    with ExitStack() as own:
        ix = sb(n + "ix", [P, 2, IRING, 2], I32, own)
        dl = sb(n + "dl", [P, 2, IRING], F32, own)
        xl = sb(n + "xl", [P, RING, W], F32, own)
        if layer == 1:
            xr = sb(n + "xr", [P, RING, W], F32, own)
        else:
            dlb = sb(n + "dlb", [P, 2, IRING, P], F32, own)
            hot_t = sb(n + "hot_t", [P, 4, P], BF16, own)
        ea = sb(n + "ea", [EROWS, 2, IRING, P], BF16, own)
        slope = sb(n + "slope", [P, 2, W], F32, own)
        leaky = sb(n + "leaky", [P, 4, W], F32, own)
        cold = sb(n + "cold", [P, 4, P], BF16, own)
        top = sb(n + "top", [P, 2, heads], F32, own)
        low = sb(n + "low", [P, 2, heads], F32, own)
        fade = sb(n + "fade", [P, 4, heads], F32, own)
        exps = sb(n + "exps", [P, 2, HP], F32, own)
        exps_t = sb(n + "exps_t", [P, 2, HP], F32, own)
        share = sb(n + "share", [P, 4, heads], F32, own)
        dnew = sb(n + "dnew", [P, 2, heads], F32, own)
        m_ps = ps(n + "m_ps", [P, 2, 512], own)
        wide_ps = ps(n + "wide_ps", [P, 2, 512], own)
        turn_ps = ps(n + "turn_ps", [P, 512], own)
        sum_ps = ps(n + "sum_ps", [P, 2, 512], own)

        ix_ready = sem(n + "ix_ready", own)
        xl_in = [sem(n + f"xl_in{i}", own) for i in range(RING)]
        xr_in = [sem(n + f"xr_in{i}", own) for i in range(RING)]
        ea_in = [sem(n + f"ea_in{i}", own) for i in range(2)]
        dlb_in = [sem(n + f"dlb_in{i}", own) for i in range(2)]
        rows_summed = sem(n + "rows_summed", own)
        hot_t_made = sem(n + "hot_t_made", own)
        m_made = sem(n + "m_made", own)
        slope_made = sem(n + "slope_made", own)
        leaky_made = sem(n + "leaky_made", own)
        wide_made = sem(n + "wide_made", own)
        top_made = sem(n + "top_made", own)
        low_made = sem(n + "low_made", own)
        drop_made = sem(n + "drop_made", own)
        kept = sem(n + "kept", own)
        exps_made = sem(n + "exps_made", own)
        turned = sem(n + "turned", own)
        copied = sem(n + "copied", own)
        sum_made = sem(n + "sum_made", own)
        den_faded = sem(n + "den_faded", own)
        added = sem(n + "added", own)

        with nc.Block() as block:
            @block.sync
            def _(sp):
                def body(i):
                    if i.k % IRING:
                        return
                    half = i.k // IRING % 2
                    j = i.back(IRING + 1)
                    if j.live:
                        sp.wait_ge(m_made, j.done)
                        nc.sync.nop(nofuse=True)
                    sp.dma_start(ea[:, half], k["d_ea"][bass.ds(i.s, IRING)].rearrange("s r e -> r s e")).then_inc(ea_in[half], 16)
                    if layer == 2:
                        sp.dma_start(dlb[:, half].rearrange("p s e -> p (s e)"),
                                     k["d_dl"].rearrange("(one s) e -> one (s e)", one=1)[:, bass.ds(i.s * P, IRING * P)]
                                     .to_broadcast((P, IRING * P))).then_inc(dlb_in[half], 16)
                run_steps(sp, body, U, STEPS, 0)

            @block.gpsimd
            def _(pool):
                def body(i):
                    if i.live:
                        half = i.k // IRING % 2
                        if i.k % IRING == 0:
                            if i.back(2 * IRING).live:
                                pool.wait_ge(leaky_made, i.back(IRING + 1).done)
                            nc.gpsimd.tensor_copy(dl[:, half], k["dl"][:, bass.ds(i.s, IRING)])
                            nc.gpsimd.tensor_copy(ix[:, half], k["idx"][:, bass.ds(i.s, IRING), :]).then_inc(ix_ready, 1)
                            pool.wait_ge(ix_ready, i.turns(IRING))
                            nc.gpsimd.nop(nofuse=True)
                        if i.back(RING).live:
                            pool.wait_ge(sum_made, i.back(RING).done)
                            nc.gpsimd.nop(nofuse=True)
                        for c, side in enumerate("lr"[:3 - layer]):
                            at = bass.IndirectOffsetOnAxis(ap=ix[:, half, i.k % IRING, c:c + 1], axis=0)
                            rows, landed = (xl, xl_in) if side == "l" else (xr, xr_in)
                            nc.gpsimd.indirect_dma_start(out=rows[:, i.slot(RING)], out_offset=None, in_=k[f"d_x{side}{layer}"],
                                                         in_offset=at).then_inc(landed[i.slot(RING)], 16)
                    j = i.back(2)
                    if j.live and both:
                        pool.wait_ge(xl_in[j.slot(RING)], j.turns(RING) * 16)
                        pool.wait_ge(xr_in[j.slot(RING)], j.turns(RING) * 16)
                        nc.gpsimd.tensor_tensor(xr[:, j.slot(RING), 0:both], xl[:, j.slot(RING), 0:both], xr[:, j.slot(RING), 0:both],
                                                ALU.add).then_inc(rows_summed, 1)
                run_steps(pool, body, U, STEPS, 2 if both else 0)

            @block.tensor
            def _(pe):
                regs = [pe.alloc_register(f"{n}row{i}") for i in range(U)]
                tiles = [None] * U

                def head(it):
                    pe.load(regs, k["tile_i"][0:1, bass.ds(it * U + U, U)])
                    for i in range(U):
                        tiles[i] = pe.snap(regs[i], min_val=0, max_val=NT - 1)

                def body(i):
                    j = i.back(2)
                    if j.live:
                        pe.wait_ge(leaky_made, j.done)
                        for h in range(heads):
                            o = wide_ps[:, j.slot(2), h * P:(h + 1) * P]
                            for c in range(h * ch // P, (h + 1) * ch // P):
                                nc.tensor.matmul(o, w["att_col"][:, c:c + 1].to_broadcast((P, P)), leaky[:, j.slot(4), c * P:(c + 1) * P],
                                                 start=(c == h * ch // P), stop=False, skip_group_check=True)
                            last = nc.tensor.matmul(o, cold[:, j.slot(4)], k["bigi"][:], start=False, stop=True,
                                                    skip_group_check=True)
                        last.then_inc(wide_made, 1)
                    if i.live:
                        if layer == 1:
                            pe.wait_ge(rows_summed, i.done)
                        else:
                            pe.wait_ge(xl_in[i.slot(RING)], i.turns(RING) * 16)
                            pe.wait_ge(hot_t_made, i.done)
                        if i.k % IRING == 0:
                            pe.wait_ge(ea_in[i.k // IRING % 2], i.turns_of(IRING, 2) * 16)
                        for c in range(K):
                            cols = slice(c * P, (c + 1) * P)
                            o = m_ps[:, i.slot(2), cols]
                            gathered = (xl,) if layer == 2 else (xr,) if (c + 1) * P <= both else (xl, xr)
                            for r, rows in enumerate(gathered):
                                nc.tensor.matmul(o, rows[:, i.slot(RING), cols], k["ident"][:], is_transpose=True,
                                                 start=(r == 0), stop=False, skip_group_check=True)
                            if layer == 2:
                                for part in range(PARTS):
                                    rows = k["xr_parts"][:, bass.ds(tiles[i.k], 1), part, cols].rearrange("p t f -> p (t f)")
                                    nc.tensor.matmul(o, rows, hot_t[:, i.slot(4)], start=False, stop=False, skip_group_check=True)
                            last = nc.tensor.matmul(o, w["we"][:, cols], ea[:, i.k // IRING % 2, i.k % IRING],
                                                    start=False, stop=True, skip_group_check=True)
                        last.then_inc(m_made, 1)
                    j = i.back(4)
                    if j.live:
                        pe.wait_ge(copied, j.done)
                        if j.back(2).live:
                            pe.wait_ge(added, j.back(2).done)
                        for h in range(heads):
                            cols = slice(h * ch, (h + 1) * ch)
                            last = nc.tensor.matmul(sum_ps[:, j.slot(2), cols], exps_t[:, j.slot(2), h * P:(h + 1) * P],
                                                    xl[:, j.slot(RING), cols], start=True, stop=True)
                        last.then_inc(sum_made, 1)
                    j = i.back(3)
                    if j.live:
                        pe.wait_ge(exps_made, j.done)
                        for h in range(heads):
                            cols = slice(h * P, (h + 1) * P)
                            last = nc.tensor.transpose(turn_ps[:, cols], exps[:, j.slot(2), cols], k["ident"][:])
                        last.then_inc(turned, 1)
                run_steps(pe, body, U, STEPS, 4, head if layer == 2 else None)

            @block.scalar
            def _(act):
                regs = [act.alloc_register(f"{n}kept{i}") for i in range(U)]
                tiles = [None] * U

                def head(it):
                    act.load(regs, k["tile_i"][0:1, bass.ds(it * U + (U - 2), U)])
                    for i in range(U):
                        tiles[i] = act.snap(regs[i], min_val=0, max_val=NT - 1)

                def body(i):
                    if i.live:
                        act.wait_ge(m_made, i.done)
                        nc.scalar.activation(slope[:, i.slot(2)], m_ps[:, i.slot(2), 0:W], ACT.Copy, scale=SLOPE).then_inc(slope_made, 1)
                    j = i.back(2)
                    if j.live:
                        act.wait_ge(drop_made, j.done)
                        nc.scalar.copy(tile_of(k["low"], tiles[i.k], heads), low[:, j.slot(2)]).then_inc(kept, 1)
                        nc.scalar.activation(fade[:, j.slot(4)], fade[:, j.slot(4)], ACT.Exp)
                        for h in range(heads):
                            cols = slice(h * P, (h + 1) * P)
                            last = nc.scalar.activation(exps[:, j.slot(2), cols], wide_ps[:, j.slot(2), cols], ACT.Exp,
                                                        bias=low[:, j.slot(2), h:h + 1], accum_out=share[:, j.slot(4), h:h + 1])
                        last.then_inc(exps_made, 1)
                    j = i.back(3)
                    if j.live:
                        act.wait_ge(turned, j.done)
                        nc.scalar.copy(exps_t[:, j.slot(2)], turn_ps[:, 0:HP]).then_inc(copied, 1)
                run_steps(act, body, U, STEPS, 3, head)

            @block.vector
            def _(dve):
                regs = [dve.alloc_register(f"{n}tile{i}") for i in range(U + 3)]
                tiles = [None] * (U + 3)

                def head(it):
                    dve.load(regs, k["tile_i"][0:1, bass.ds(it * U + (U - 5 - ahead), U + 3)])
                    for i in range(U + 3):
                        tiles[i] = dve.snap(regs[i], min_val=0, max_val=NT - 1)

                def body(i):
                    at = i.k
                    if layer == 2 and i.live:
                        half, col = i.k // IRING % 2, i.k % IRING
                        if col == 0:
                            dve.wait_ge(dlb_in[half], i.turns_of(IRING, 2) * 16)
                        nc.vector.tensor_scalar(hot_t[:, i.slot(4)], dlb[:, half, col], k["part"][:, 0:1], None,
                                                ALU.is_equal).then_inc(hot_t_made, 1)
                    i = i.back(ahead)
                    j = i.back(5)
                    if j.live:
                        dve.wait_ge(sum_made, j.done)
                        if j.back(1).live:
                            dve.wait_ge(added, j.back(1).done)
                        den = tile_of(k["den"], tiles[at], heads)
                        if heads == 1:
                            nc.vector.scalar_tensor_tensor(den, den, fade[:, j.slot(4)], share[:, j.slot(4)], ALU.mult, ALU.add)
                        else:
                            nc.vector.tensor_tensor(dnew[:, j.slot(2)], den, fade[:, j.slot(4)], ALU.mult).then_inc(den_faded, 1)
                        for h in range(heads):
                            cols = slice(h * ch, (h + 1) * ch)
                            row = k["acc"][:, bass.ds(tiles[at], 1), cols].rearrange("p t f -> p (t f)")
                            last = nc.vector.scalar_tensor_tensor(row, row, fade[:, j.slot(4), h:h + 1],
                                                                  sum_ps[:, j.slot(2), cols], ALU.mult, ALU.add)
                        if heads > 1:
                            dve.wait_ge(den_faded, j.done)
                            last = nc.vector.tensor_tensor(den, dnew[:, j.slot(2)], share[:, j.slot(4)], ALU.add)
                        last.then_inc(added, 1)
                    j = i.back(2)
                    if j.live:
                        dve.wait_ge(wide_made, j.done)
                        nc.vector.tensor_reduce(top[:, j.slot(2)], wide_ps[:, j.slot(2), 0:HP].rearrange("p (h e) -> p h e", e=P),
                                                AX.X, ALU.max).then_inc(top_made, 1)
                    if i.live:
                        if i.k % IRING == 0:
                            dve.wait_ge(ix_ready, i.turns(IRING))
                        nc.vector.tensor_scalar(cold[:, i.slot(4)], k["node_row"][:], dl[:, i.k // IRING % 2, i.k % IRING:i.k % IRING + 1],
                                                -1.0, ALU.is_equal, ALU.add)
                    if j.live:
                        dve.wait_ge(top_made, j.done)
                        if j.back(1).live:
                            dve.wait_ge(kept, j.back(1).done)
                        old = tile_of(k["low"], tiles[at + 3], heads)
                        nc.vector.scalar_tensor_tensor(low[:, j.slot(2)], top[:, j.slot(2)], -1.0, old,
                                                       ALU.mult, ALU.min).then_inc(low_made, 1)
                        dve.wait_ge(low_made, j.done)
                        nc.vector.tensor_tensor(fade[:, j.slot(4)], low[:, j.slot(2)], old, ALU.subtract).then_inc(drop_made, 1)
                    if i.live:
                        dve.wait_ge(slope_made, i.done)
                        nc.vector.tensor_tensor(leaky[:, i.slot(4)], m_ps[:, i.slot(2), 0:W], slope[:, i.slot(2)],
                                                ALU.max).then_inc(leaky_made, 1)
                run_steps(dve, body, U, STEPS, 5 + ahead, head)


def last_nodes(nc, a, k, sb, ps, sem, out):
    with ExitStack() as own:
        bias = sb("ln_bias", [P, D], F32, own)
        gain = sb("ln_gain", [P, D], F32, own)
        offset = sb("ln_offset", [P, D], F32, own)
        loaded = sem("ln_loaded", own)
        divided = sem("ln_divided", own)
        stats = sem("ln_stats", own)
        dve_own = sem("ln_own", own)
        to_root = sem("ln_to_root", own)
        rooted = sem("ln_rooted", own)
        made = sem("ln_made", own)
        doubled = sem("ln_doubled", own)
        normed = Normed(nc, k, "ln_n_", sb, sem, own, gain)
        stored = sem("ln_stored", own)
        FULL = N // P
        with nc.Block() as block:
            @block.sync
            def _(sp):
                sp.dma_start(bias[:], a["cb2"].to_broadcast((P, D))).then_inc(loaded, 16)
                sp.dma_start(gain[:], a["g2"].to_broadcast((P, D))).then_inc(loaded, 16)
                sp.dma_start(offset[:], a["be2"].to_broadcast((P, D))).then_inc(loaded, 16)

                def body(i):
                    sp.wait_ge(made, i.done)
                    nc.sync.nop(nofuse=True)
                    sp.dma_start(out[bass.ds(i.s * P, P), :], tile_of(k["acc"], i.s, D)).then_inc(stored, 16)
                run_steps(sp, body, 2, FULL, 0)
                sp.wait_ge(made, FULL + 1)
                sp.dma_start(out[FULL * P:N, :], k["acc"][0:N - FULL * P, FULL, 0:D]).then_inc(stored, 16)
                sp.wait_ge(stored, 16 * (FULL + 1))

            @block.scalar
            def _(act):
                nc.scalar.activation(k["xn"][:], k["xn"][:], ACT.Copy, scale=2.0).then_inc(doubled, 1)
                for c in range(2):
                    root(k, nc, act, rooted, to_root, c + 1)

            @block.gpsimd
            def _(pool):
                pool.wait_ge(loaded, 48)

                pool.wait_ge(doubled, 1)
                nc.gpsimd.tensor_tensor(k["xn"][:], k["xn"][:],
                                        offset[:].rearrange("p (one f) -> p one f", one=1).to_broadcast((P, NT, D)),
                                        ALU.add).then_inc(doubled, 1)
                normed.pool(pool)

            @block.vector
            def _(dve):
                link = Chain(dve, dve_own)
                den = k["den"][:, :, 0]
                rden = k["rden"][:, 0:NT]
                link(nc.vector.tensor_scalar(den, den, 1e-16, None, ALU.add))
                link(nc.vector.reciprocal(rden, den))
                dve.wait_ge(loaded, 48)

                def body(i):
                    if i.live:
                        row = tile_of(k["acc"], i.s, D)
                        nc.vector.scalar_tensor_tensor(row, row, k["rden"][:, bass.ds(i.s, 1)], bias[:],
                                                       ALU.mult, ALU.add).then_inc(divided, 1)
                    j = i.back(1)
                    if j.live:
                        dve.wait_ge(divided, j.done)
                        nc.vector.bn_stats(tile_of(k["st"], j.s, 6), tile_of(k["acc"], j.s, D)).then_inc(stats, 1)
                run_steps(dve, body, 2, NT, 1)
                dve.wait_ge(stats, NT)
                spread(k, nc, dve, rooted, to_root, link, 1)

                dve.wait_ge(doubled, 2)
                normed.vector(dve)
                spread(k, nc, dve, rooted, to_root, link, 2)

                def body(i):
                    row = tile_of(k["acc"], i.s, D)
                    nc.vector.tensor_scalar(row, row, k["mv"][:, bass.ds(i.s, 1), 0],
                                            k["rstd"][:, bass.ds(i.s, 1)], ALU.subtract, ALU.mult).then_inc(made, 1)
                run_steps(dve, body, 2, FULL, 0)
                body(Step(FULL // 2, 0, 2, FULL + 2))


_WEIGHTS = {
    "W1": "L0_gnn_W1", "b1": "L0_gnn_b1", "W2": "L0_gnn_W2", "b2": "L0_gnn_b2", "Wg": "L0_gnn_Wg", "bg": "L0_gnn_bg",
    "gamma": "L0_gnn_gamma", "beta": "L0_gnn_beta", "Wl1": "L1_gnn_Wl1", "Wr1": "L1_gnn_Wr1", "We1": "L1_gnn_We1",
    "att1": "L1_gnn_att1", "cb1": "L1_gnn_b1", "g1": "L1_gnn_g1", "be1": "L1_gnn_be1", "Wl2": "L1_gnn_Wl2",
    "Wr2": "L1_gnn_Wr2", "We2": "L1_gnn_We2", "att2": "L1_gnn_att2", "cb2": "L1_gnn_b2", "g2": "L1_gnn_g2",
    "be2": "L1_gnn_be2",
}
BEYOND = 1 << 20


def laid_out(inputs):
    x = np.asarray(inputs["x"])
    edges = EP - E
    arrays = {
        "x": np.pad(x, ((0, NP - N), (0, 0))),
        "src": np.pad(np.asarray(inputs["src"]), (0, edges)).reshape(EP, 1),
        "dst": np.pad(np.asarray(inputs["dst"]), (0, edges), constant_values=BEYOND).reshape(EP, 1),
        "ea4": np.pad(np.asarray(inputs["edge_attr_4"]), ((0, edges), (0, 0))),
        "ea64t": np.ascontiguousarray(np.pad(np.asarray(inputs["edge_attr_64"]), ((0, edges), (0, 0))).T),
    }
    arrays["xt"] = np.ascontiguousarray(arrays["x"].T)
    for short, name in _WEIGHTS.items():
        w = np.ascontiguousarray(inputs[name])
        arrays[short] = w.reshape(1, -1) if w.ndim == 1 or short.startswith("att") else w
    return arrays


def kernel(**inputs):
    import concourse.bacc as bacc
    from concourse.bass_utils import run_bass_kernel_spmd

    nc = bacc.Bacc("TRN2", target_bir_lowering=False, num_devices=1)
    arrays = laid_out(inputs)
    a = {n: nc.dram_tensor(f"in_{n}", v.shape, mybir.dt.from_np(v.dtype), kind="ExternalInput").ap() for n, v in arrays.items()}
    out = nc.dram_tensor("out_x", (N, D), F32, kind="ExternalOutput").ap()
    gnn(nc, a, out)
    r = run_bass_kernel_spmd(nc, [{f"in_{n}": v for n, v in arrays.items()}], core_ids=[0])
    return r.results[0]["out_x"]
```
